# Optimizing a Trainium2 kernel written in Bass

```python
import numpy as np
import jax
import jax.numpy as jnp

def _softmax(x, axis=-1):
    return jax.nn.softmax(x, axis=axis)

def _gelu(x):
    return jax.nn.gelu(x, approximate=True)

def _silu(x):
    return jax.nn.silu(x)

def _sigmoid(x):
    return jax.nn.sigmoid(x)

def _layernorm(x, axis=-1, eps=1e-05):
    m = jnp.mean(x, axis=axis, keepdims=True)
    v = jnp.var(x, axis=axis, keepdims=True)
    return (x - m) / jnp.sqrt(v + eps)

def _scatter_add(tgt, idx, src, axis=0):
    return tgt.at[idx].add(src)

def _segment_sum(src, seg, n):
    return jax.ops.segment_sum(src, seg, n)
kernel_name = 'mk_cond_seq_d4_seqx_r2_5f41d9'

def setup_inputs(seed: int=0):
    np.random.seed(seed)
    _w = jnp.asarray

    def _rec_inputs():
        import jax
        import jax.numpy as jnp
        _rk = jax.random.key(seed)
        x = -0.0002928 + 1 * jax.random.normal(jax.random.fold_in(_rk, 1), (2, 2048, 512), jnp.float32)
        _lenS = 2048 - jax.random.randint(jax.random.fold_in(_rk, 7), (2,), 0, max(1, 2048 // 4) + 1, jnp.int32)
        _lenS2 = 2048 - jax.random.randint(jax.random.fold_in(_rk, 8), (2,), 0, max(1, 2048 // 4) + 1, jnp.int32)
        cond_2048 = 0.0061147 + 1.02565 * jax.random.normal(jax.random.fold_in(_rk, 11), (2, 1024), jnp.float32)
        _validS = jnp.arange(2048)[None, :] < _lenS[:, None]
        _validS2 = jnp.arange(2048)[None, :] < _lenS2[:, None]
        _causal = jnp.tril(jnp.ones((2048, 2048), dtype=bool))
        mask_BxS_ff1 = jnp.where(jnp.ones((2, 2048), dtype=bool), 1.0, 0.0).astype(jnp.float32)
        mask_BxS_ik0 = jnp.where(jnp.broadcast_to(_validS[:, :], (2, 2048)), 0, 1).astype(jnp.int32)
        mask_BxSx1_fk1 = jnp.where(jnp.ones((2, 2048, 1), dtype=bool), 1.0, 0.0).astype(jnp.float32)
        return (x, cond_2048, mask_BxS_ff1, mask_BxS_ik0, mask_BxSx1_fk1)
    x, cond_2048, mask_BxS_ff1, mask_BxS_ik0, mask_BxSx1_fk1 = _rec_inputs()

    def _L0_cond_setup():
        import jax, jax.numpy as jnp
        import numpy as np
        D = 512
        DI = 1024
        N = 16
        DT_RANK = 64
        D_CONV = 4
        EPS = 1e-05

        def _layernorm(x, g, b):
            mu = jnp.mean(x, axis=-1, keepdims=True)
            var = jnp.mean((x - mu) ** 2, axis=-1, keepdims=True)
            return (x - mu) * jax.lax.rsqrt(var + EPS) * g + b

        def _mamba(xn, in_proj_w, conv_w, conv_b, x_proj_w, dt_proj_w, dt_proj_b, A_log, D_param, out_proj_w):
            b, sl, _ = xn.shape
            xz = jnp.einsum('bsd,ed->bse', xn, in_proj_w)
            x_in, z = jnp.split(xz, 2, axis=-1)
            xt = jnp.transpose(x_in, (0, 2, 1))
            u = jax.lax.conv_general_dilated(xt, conv_w[:, None, :], (1,), [(D_CONV - 1, 0)], feature_group_count=DI, dimension_numbers=('NCH', 'OIH', 'NCH')) + conv_b[None, :, None]
            u = jax.nn.silu(jnp.transpose(u, (0, 2, 1)))
            x_dbl = jnp.einsum('bsd,ed->bse', u, x_proj_w)
            dt_r, B, C = jnp.split(x_dbl, [DT_RANK, DT_RANK + N], axis=-1)
            dt = jax.nn.softplus(jnp.einsum('bsr,dr->bsd', dt_r, dt_proj_w) + dt_proj_b)
            A = -jnp.exp(A_log)

            def step(h, inp):
                dt_t, B_t, C_t, u_t = inp
                dA = jnp.exp(dt_t[:, :, None] * A)
                h = h * dA + (dt_t * u_t)[:, :, None] * B_t[:, None, :]
                y = jnp.einsum('bdn,bn->bd', h, C_t)
                return (h, y)
            seq = (jnp.transpose(dt, (1, 0, 2)), jnp.transpose(B, (1, 0, 2)), jnp.transpose(C, (1, 0, 2)), jnp.transpose(u, (1, 0, 2)))
            h0 = jnp.zeros((b, DI, N), xn.dtype)
            _, ys = jax.lax.scan(step, h0, seq)
            y = jnp.transpose(ys, (1, 0, 2)) + u * D_param
            y = y * jax.nn.silu(z)
            return jnp.einsum('bsd,ed->bse', y, out_proj_w)
        key = jax.random.key(seed)
        ks = jax.random.split(key, 16)
        s = lambda fan: 1.0 / np.sqrt(fan)
        inp = {'x': jax.random.normal(ks[0], (2, 1024, D), jnp.float32), 'c': jax.random.normal(ks[1], (2, 2 * D), jnp.float32), 'ln_g': jnp.ones((D,), jnp.float32), 'ln_b': jnp.zeros((D,), jnp.float32), 'ada_w': jax.random.normal(ks[2], (3 * D, 2 * D), jnp.float32) * s(2 * D), 'ada_b': jnp.zeros((3 * D,), jnp.float32), 'in_proj_w': jax.random.normal(ks[3], (2 * DI, D), jnp.float32) * s(D), 'conv_w': jax.random.normal(ks[4], (DI, D_CONV), jnp.float32) * s(D_CONV), 'conv_b': jnp.zeros((DI,), jnp.float32), 'x_proj_w': jax.random.normal(ks[5], (DT_RANK + 2 * N, DI), jnp.float32) * s(DI), 'dt_proj_w': jax.random.normal(ks[6], (DI, DT_RANK), jnp.float32) * s(DT_RANK), 'dt_proj_b': jax.random.uniform(ks[7], (DI,), jnp.float32, -4.0, -2.0), 'A_log': jnp.tile(jnp.log(jnp.arange(1, N + 1, dtype=jnp.float32)), (DI, 1)), 'D_param': jnp.ones((DI,), jnp.float32), 'out_proj_w': jax.random.normal(ks[8], (D, DI), jnp.float32) * s(DI)}
        return inp
    _L0_cond_all = _L0_cond_setup()
    _L0_cond_in = {k: v for k, v in _L0_cond_all.items() if k in ('ln_g', 'ln_b', 'ada_w', 'ada_b', 'in_proj_w', 'conv_w', 'conv_b', 'x_proj_w', 'dt_proj_w', 'dt_proj_b', 'A_log', 'D_param', 'out_proj_w')}
    del _L0_cond_all

    def _L1_cond_setup():
        import jax, jax.numpy as jnp
        import numpy as np
        B, T, D, H, TE = (8, 512, 512, 16, 1024)
        LN_EPS = 1e-05

        def layer_norm(x, w, b):
            m = jnp.mean(x, axis=-1, keepdims=True)
            v = jnp.var(x, axis=-1, keepdims=True)
            return (x - m) / jnp.sqrt(v + LN_EPS) * w + b
        key = jax.random.key(seed)
        ks = jax.random.split(key, 8)
        s = lambda k, sh: jax.random.normal(k, sh, jnp.float32) * 0.02
        return dict(x=jax.random.normal(ks[0], (B, T, D), jnp.float32), emb=jax.random.normal(ks[1], (B, TE), jnp.float32), src_mask=jnp.ones((B, T), jnp.float32), norm_w=jnp.ones((D,), jnp.float32), norm_b=jnp.zeros((D,), jnp.float32), q_w=s(ks[2], (D, D)), q_b=jnp.zeros((D,), jnp.float32), k_w=s(ks[3], (D, D)), k_b=jnp.zeros((D,), jnp.float32), v_w=s(ks[4], (D, D)), v_b=jnp.zeros((D,), jnp.float32), emb_w=s(ks[5], (TE, 2 * D)), emb_b=jnp.zeros((2 * D,), jnp.float32), sb_norm_w=jnp.ones((D,), jnp.float32), sb_norm_b=jnp.zeros((D,), jnp.float32), out_w=s(ks[6], (D, D)), out_b=jnp.zeros((D,), jnp.float32))
    _L1_cond_all = _L1_cond_setup()
    _L1_cond_in = {k: v for k, v in _L1_cond_all.items() if k in ('norm_w', 'norm_b', 'q_w', 'q_b', 'k_w', 'k_b', 'v_w', 'v_b', 'emb_w', 'emb_b', 'sb_norm_w', 'sb_norm_b', 'out_w', 'out_b')}
    del _L1_cond_all

    def _L2_cond_setup():
        import jax, jax.numpy as jnp
        import numpy as np
        H = 16
        LN_EPS = 1e-05

        def _layernorm(x, scale, bias):
            mu = jnp.mean(x, axis=-1, keepdims=True)
            var = jnp.var(x, axis=-1, keepdims=True)
            return (x - mu) * jax.lax.rsqrt(var + LN_EPS) * scale + bias
        key = jax.random.key(seed)
        ks = jax.random.split(key, 8)
        B, T, D, E = (4, 2048, 512, 1024)
        s = 0.02
        return {'x': jax.random.normal(ks[0], (B, T, D), jnp.float32), 'emb': jax.random.normal(ks[1], (B, E), jnp.float32), 'src_mask': jax.random.randint(ks[2], (B, T), 0, 2).astype(jnp.int32), 'norm_scale': jnp.ones((D,), jnp.float32), 'norm_bias': jnp.zeros((D,), jnp.float32), 'Wq': jax.random.normal(ks[3], (D, D), jnp.float32) * s, 'bq': jnp.zeros((D,), jnp.float32), 'Wk': jax.random.normal(ks[4], (D, D), jnp.float32) * s, 'bk': jnp.zeros((D,), jnp.float32), 'Wv': jax.random.normal(ks[5], (D, D), jnp.float32) * s, 'bv': jnp.zeros((D,), jnp.float32), 'film_emb_W': jax.random.normal(ks[6], (E, 2 * D), jnp.float32) * s, 'film_emb_b': jnp.zeros((2 * D,), jnp.float32), 'film_norm_scale': jnp.ones((D,), jnp.float32), 'film_norm_bias': jnp.zeros((D,), jnp.float32), 'film_out_W': jax.random.normal(ks[7], (D, D), jnp.float32) * s, 'film_out_b': jnp.zeros((D,), jnp.float32)}
    _L2_cond_all = _L2_cond_setup()
    _L2_cond_in = {k: v for k, v in _L2_cond_all.items() if k in ('norm_scale', 'norm_bias', 'Wq', 'bq', 'Wk', 'bk', 'Wv', 'bv', 'film_emb_W', 'film_emb_b', 'film_norm_scale', 'film_norm_bias', 'film_out_W', 'film_out_b')}
    del _L2_cond_all

    def _L3_cond_setup():
        import jax, jax.numpy as jnp
        import numpy as np
        B, T, D, H, TE = (4, 1024, 512, 8, 1024)
        EPS = 1e-05

        def _ln(x, w, b):
            m = jnp.mean(x, axis=-1, keepdims=True)
            v = jnp.mean((x - m) ** 2, axis=-1, keepdims=True)
            return (x - m) * jax.lax.rsqrt(v + EPS) * w + b
        key = jax.random.key(seed)
        ks = jax.random.split(key, 16)
        s = 0.02
        inp = {'x': jax.random.normal(ks[0], (B, T, D), jnp.float32), 'emb': jax.random.normal(ks[1], (B, TE), jnp.float32), 'src_mask': (jax.random.uniform(ks[2], (B, T, 1)) > 0.2).astype(jnp.float32), 'num_head': H, 'ln_w': jnp.ones((D,), jnp.float32), 'ln_b': jnp.zeros((D,), jnp.float32), 'Wq': jax.random.normal(ks[3], (D, D), jnp.float32) * s, 'bq': jnp.zeros((D,), jnp.float32), 'Wk': jax.random.normal(ks[4], (D, D), jnp.float32) * s, 'bk': jnp.zeros((D,), jnp.float32), 'Wv': jax.random.normal(ks[5], (D, D), jnp.float32) * s, 'bv': jnp.zeros((D,), jnp.float32), 'W_emb': jax.random.normal(ks[6], (TE, 2 * D), jnp.float32) * s, 'b_emb': jnp.zeros((2 * D,), jnp.float32), 'ln2_w': jnp.ones((D,), jnp.float32), 'ln2_b': jnp.zeros((D,), jnp.float32), 'W_out': jax.random.normal(ks[7], (D, D), jnp.float32) * s, 'b_out': jnp.zeros((D,), jnp.float32)}
        return inp
    _L3_cond_all = _L3_cond_setup()
    _L3_cond_in = {k: v for k, v in _L3_cond_all.items() if k in ('ln_w', 'ln_b', 'Wq', 'bq', 'Wk', 'bk', 'Wv', 'bv', 'W_emb', 'b_emb', 'ln2_w', 'ln2_b', 'W_out', 'b_out')}
    del _L3_cond_all
    return {'x': x, 'cond_2048': cond_2048, 'mask_BxS_ff1': mask_BxS_ff1, 'mask_BxS_ik0': mask_BxS_ik0, 'mask_BxSx1_fk1': mask_BxSx1_fk1, 'L0_cond_ln_g': _L0_cond_in['ln_g'], 'L0_cond_ln_b': _L0_cond_in['ln_b'], 'L0_cond_ada_w': _L0_cond_in['ada_w'], 'L0_cond_ada_b': _L0_cond_in['ada_b'], 'L0_cond_in_proj_w': _L0_cond_in['in_proj_w'], 'L0_cond_conv_w': _L0_cond_in['conv_w'], 'L0_cond_conv_b': _L0_cond_in['conv_b'], 'L0_cond_x_proj_w': _L0_cond_in['x_proj_w'], 'L0_cond_dt_proj_w': _L0_cond_in['dt_proj_w'], 'L0_cond_dt_proj_b': _L0_cond_in['dt_proj_b'], 'L0_cond_A_log': _L0_cond_in['A_log'], 'L0_cond_D_param': _L0_cond_in['D_param'], 'L0_cond_out_proj_w': _L0_cond_in['out_proj_w'], 'L1_cond_norm_w': _L1_cond_in['norm_w'], 'L1_cond_norm_b': _L1_cond_in['norm_b'], 'L1_cond_q_w': _L1_cond_in['q_w'], 'L1_cond_q_b': _L1_cond_in['q_b'], 'L1_cond_k_w': _L1_cond_in['k_w'], 'L1_cond_k_b': _L1_cond_in['k_b'], 'L1_cond_v_w': _L1_cond_in['v_w'], 'L1_cond_v_b': _L1_cond_in['v_b'], 'L1_cond_emb_w': _L1_cond_in['emb_w'], 'L1_cond_emb_b': _L1_cond_in['emb_b'], 'L1_cond_sb_norm_w': _L1_cond_in['sb_norm_w'], 'L1_cond_sb_norm_b': _L1_cond_in['sb_norm_b'], 'L1_cond_out_w': _L1_cond_in['out_w'], 'L1_cond_out_b': _L1_cond_in['out_b'], 'L2_cond_norm_scale': _L2_cond_in['norm_scale'], 'L2_cond_norm_bias': _L2_cond_in['norm_bias'], 'L2_cond_Wq': _L2_cond_in['Wq'], 'L2_cond_bq': _L2_cond_in['bq'], 'L2_cond_Wk': _L2_cond_in['Wk'], 'L2_cond_bk': _L2_cond_in['bk'], 'L2_cond_Wv': _L2_cond_in['Wv'], 'L2_cond_bv': _L2_cond_in['bv'], 'L2_cond_film_emb_W': _L2_cond_in['film_emb_W'], 'L2_cond_film_emb_b': _L2_cond_in['film_emb_b'], 'L2_cond_film_norm_scale': _L2_cond_in['film_norm_scale'], 'L2_cond_film_norm_bias': _L2_cond_in['film_norm_bias'], 'L2_cond_film_out_W': _L2_cond_in['film_out_W'], 'L2_cond_film_out_b': _L2_cond_in['film_out_b'], 'L3_cond_ln_w': _L3_cond_in['ln_w'], 'L3_cond_ln_b': _L3_cond_in['ln_b'], 'L3_cond_Wq': _L3_cond_in['Wq'], 'L3_cond_bq': _L3_cond_in['bq'], 'L3_cond_Wk': _L3_cond_in['Wk'], 'L3_cond_bk': _L3_cond_in['bk'], 'L3_cond_Wv': _L3_cond_in['Wv'], 'L3_cond_bv': _L3_cond_in['bv'], 'L3_cond_W_emb': _L3_cond_in['W_emb'], 'L3_cond_b_emb': _L3_cond_in['b_emb'], 'L3_cond_ln2_w': _L3_cond_in['ln2_w'], 'L3_cond_ln2_b': _L3_cond_in['ln2_b'], 'L3_cond_W_out': _L3_cond_in['W_out'], 'L3_cond_b_out': _L3_cond_in['b_out']}

def reference(x, cond_2048, mask_BxS_ff1, mask_BxS_ik0, mask_BxSx1_fk1, L0_cond_ln_g, L0_cond_ln_b, L0_cond_ada_w, L0_cond_ada_b, L0_cond_in_proj_w, L0_cond_conv_w, L0_cond_conv_b, L0_cond_x_proj_w, L0_cond_dt_proj_w, L0_cond_dt_proj_b, L0_cond_A_log, L0_cond_D_param, L0_cond_out_proj_w, L1_cond_norm_w, L1_cond_norm_b, L1_cond_q_w, L1_cond_q_b, L1_cond_k_w, L1_cond_k_b, L1_cond_v_w, L1_cond_v_b, L1_cond_emb_w, L1_cond_emb_b, L1_cond_sb_norm_w, L1_cond_sb_norm_b, L1_cond_out_w, L1_cond_out_b, L2_cond_norm_scale, L2_cond_norm_bias, L2_cond_Wq, L2_cond_bq, L2_cond_Wk, L2_cond_bk, L2_cond_Wv, L2_cond_bv, L2_cond_film_emb_W, L2_cond_film_emb_b, L2_cond_film_norm_scale, L2_cond_film_norm_bias, L2_cond_film_out_W, L2_cond_film_out_b, L3_cond_ln_w, L3_cond_ln_b, L3_cond_Wq, L3_cond_bq, L3_cond_Wk, L3_cond_bk, L3_cond_Wv, L3_cond_bv, L3_cond_W_emb, L3_cond_b_emb, L3_cond_ln2_w, L3_cond_ln2_b, L3_cond_W_out, L3_cond_b_out):
    import jax
    import jax.numpy as jnp

    def _L0_cond_ref(x, c, ln_g, ln_b, ada_w, ada_b, in_proj_w, conv_w, conv_b, x_proj_w, dt_proj_w, dt_proj_b, A_log, D_param, out_proj_w):
        import jax, jax.numpy as jnp
        import numpy as np
        D = 512
        DI = 1024
        N = 16
        DT_RANK = 64
        D_CONV = 4
        EPS = 1e-05

        def _layernorm(x, g, b):
            mu = jnp.mean(x, axis=-1, keepdims=True)
            var = jnp.mean((x - mu) ** 2, axis=-1, keepdims=True)
            return (x - mu) * jax.lax.rsqrt(var + EPS) * g + b

        def _mamba(xn, in_proj_w, conv_w, conv_b, x_proj_w, dt_proj_w, dt_proj_b, A_log, D_param, out_proj_w):
            b, sl, _ = xn.shape
            xz = jnp.einsum('bsd,ed->bse', xn, in_proj_w)
            x_in, z = jnp.split(xz, 2, axis=-1)
            xt = jnp.transpose(x_in, (0, 2, 1))
            u = jax.lax.conv_general_dilated(xt, conv_w[:, None, :], (1,), [(D_CONV - 1, 0)], feature_group_count=DI, dimension_numbers=('NCH', 'OIH', 'NCH')) + conv_b[None, :, None]
            u = jax.nn.silu(jnp.transpose(u, (0, 2, 1)))
            x_dbl = jnp.einsum('bsd,ed->bse', u, x_proj_w)
            dt_r, B, C = jnp.split(x_dbl, [DT_RANK, DT_RANK + N], axis=-1)
            dt = jax.nn.softplus(jnp.einsum('bsr,dr->bsd', dt_r, dt_proj_w) + dt_proj_b)
            A = -jnp.exp(A_log)

            def step(h, inp):
                dt_t, B_t, C_t, u_t = inp
                dA = jnp.exp(dt_t[:, :, None] * A)
                h = h * dA + (dt_t * u_t)[:, :, None] * B_t[:, None, :]
                y = jnp.einsum('bdn,bn->bd', h, C_t)
                return (h, y)
            seq = (jnp.transpose(dt, (1, 0, 2)), jnp.transpose(B, (1, 0, 2)), jnp.transpose(C, (1, 0, 2)), jnp.transpose(u, (1, 0, 2)))
            h0 = jnp.zeros((b, DI, N), xn.dtype)
            _, ys = jax.lax.scan(step, h0, seq)
            y = jnp.transpose(ys, (1, 0, 2)) + u * D_param
            y = y * jax.nn.silu(z)
            return jnp.einsum('bsd,ed->bse', y, out_proj_w)
        ada = jnp.einsum('bc,ec->be', jax.nn.silu(c), ada_w) + ada_b
        shift, scale, gate = jnp.split(ada, 3, axis=1)
        xn = _layernorm(x, ln_g, ln_b)
        xn = xn * (1.0 + scale[:, None, :]) + shift[:, None, :]
        x_ssm = _mamba(xn, in_proj_w, conv_w, conv_b, x_proj_w, dt_proj_w, dt_proj_b, A_log, D_param, out_proj_w)
        return x + gate[:, None, :] * x_ssm

    def _L1_cond_ref(x, emb, src_mask, norm_w, norm_b, q_w, q_b, k_w, k_b, v_w, v_b, emb_w, emb_b, sb_norm_w, sb_norm_b, out_w, out_b):
        import jax, jax.numpy as jnp
        import numpy as np
        B, T, D, H, TE = (8, 512, 512, 16, 1024)
        LN_EPS = 1e-05

        def layer_norm(x, w, b):
            m = jnp.mean(x, axis=-1, keepdims=True)
            v = jnp.var(x, axis=-1, keepdims=True)
            return (x - m) / jnp.sqrt(v + LN_EPS) * w + b
        Bx, Tx, Dx = x.shape
        xn = layer_norm(x, norm_w, norm_b)
        q = (xn @ q_w + q_b).reshape(Bx, Tx, H, -1)
        k = (xn @ k_w + k_b).reshape(Bx, Tx, H, -1)
        att = jnp.einsum('bnhl,bmhl->bnmh', q, k)
        mask = src_mask.reshape(Bx, 1, Tx, 1)
        att = att + (1.0 - mask) * -1000000.0
        att = jax.nn.softmax(att, axis=2)
        v = ((xn @ v_w + v_b) * src_mask[:, :, None]).reshape(Bx, Tx, H, -1)
        y = jnp.einsum('bnmh,bmhl->bnhl', att, v).reshape(Bx, Tx, Dx)
        e = jax.nn.silu(emb) @ emb_w + emb_b
        scale, shift = jnp.split(e[:, None, :], 2, axis=2)
        h = layer_norm(y, sb_norm_w, sb_norm_b) * (1.0 + scale) + shift
        h = jax.nn.silu(h) @ out_w + out_b
        return x + h

    def _L2_cond_ref(x, emb, src_mask, norm_scale, norm_bias, Wq, bq, Wk, bk, Wv, bv, film_emb_W, film_emb_b, film_norm_scale, film_norm_bias, film_out_W, film_out_b):
        import jax, jax.numpy as jnp
        import numpy as np
        H = 16
        LN_EPS = 1e-05

        def _layernorm(x, scale, bias):
            mu = jnp.mean(x, axis=-1, keepdims=True)
            var = jnp.var(x, axis=-1, keepdims=True)
            return (x - mu) * jax.lax.rsqrt(var + LN_EPS) * scale + bias
        B, T, D = x.shape
        dh = D // H
        xn = _layernorm(x, norm_scale, norm_bias)
        q = xn @ Wq + bq
        k = xn @ Wk + bk
        v = xn @ Wv + bv
        mask = (src_mask == 1)[:, :, None]
        k = jnp.where(mask, -jnp.inf, k)
        v = jnp.where(mask, 0.0, v)
        q = q.reshape(B, T, H, dh).transpose(0, 2, 1, 3)
        k = k.reshape(B, T, H, dh).transpose(0, 2, 1, 3)
        v = v.reshape(B, T, H, dh).transpose(0, 2, 1, 3)
        q = jax.nn.softmax(q, axis=-1)
        k = jax.nn.softmax(k, axis=2)
        attn = jnp.einsum('bhse,bhsd->bhed', k, v)
        y = jnp.einsum('bhtd,bhed->bhte', q, attn)
        y = y.transpose(0, 2, 1, 3).reshape(B, T, D)
        emb_out = jax.nn.silu(emb) @ film_emb_W + film_emb_b
        scale, shift = jnp.split(emb_out, 2, axis=-1)
        h = _layernorm(y, film_norm_scale, film_norm_bias) * (1.0 + scale[:, None, :]) + shift[:, None, :]
        h = jax.nn.silu(h) @ film_out_W + film_out_b
        return x + h

    def _L3_cond_ref(x, emb, src_mask, num_head, ln_w, ln_b, Wq, bq, Wk, bk, Wv, bv, W_emb, b_emb, ln2_w, ln2_b, W_out, b_out):
        import jax, jax.numpy as jnp
        import numpy as np
        B, T, D, H, TE = (4, 1024, 512, 8, 1024)
        EPS = 1e-05

        def _ln(x, w, b):
            m = jnp.mean(x, axis=-1, keepdims=True)
            v = jnp.mean((x - m) ** 2, axis=-1, keepdims=True)
            return (x - m) * jax.lax.rsqrt(v + EPS) * w + b
        b, t, d = x.shape
        h = num_head
        dh = d // h
        xn = _ln(x, ln_w, ln_b)
        q = xn @ Wq + bq
        k = xn @ Wk + bk + (1.0 - src_mask) * -1000000.0
        q = jax.nn.softmax(q.reshape(b, t, h, dh), axis=-1)
        k = jax.nn.softmax(k.reshape(b, t, h, dh), axis=1)
        v = ((xn @ Wv + bv) * src_mask).reshape(b, t, h, dh)
        att = jnp.einsum('bnhd,bnhl->bhdl', k, v)
        y = jnp.einsum('bnhd,bhdl->bnhl', q, att).reshape(b, t, d)
        emb_out = (jax.nn.silu(emb) @ W_emb + b_emb)[:, None, :]
        scale, shift = jnp.split(emb_out, 2, axis=2)
        hh = _ln(y, ln2_w, ln2_b) * (1.0 + scale) + shift
        hh = jax.nn.silu(hh) @ W_out + b_out
        return x + hh
    x = _L0_cond_ref(x, cond_2048, L0_cond_ln_g, L0_cond_ln_b, L0_cond_ada_w, L0_cond_ada_b, L0_cond_in_proj_w, L0_cond_conv_w, L0_cond_conv_b, L0_cond_x_proj_w, L0_cond_dt_proj_w, L0_cond_dt_proj_b, L0_cond_A_log, L0_cond_D_param, L0_cond_out_proj_w)
    x = _L1_cond_ref(x, cond_2048, mask_BxS_ff1, L1_cond_norm_w, L1_cond_norm_b, L1_cond_q_w, L1_cond_q_b, L1_cond_k_w, L1_cond_k_b, L1_cond_v_w, L1_cond_v_b, L1_cond_emb_w, L1_cond_emb_b, L1_cond_sb_norm_w, L1_cond_sb_norm_b, L1_cond_out_w, L1_cond_out_b)
    x = _L2_cond_ref(x, cond_2048, mask_BxS_ik0, L2_cond_norm_scale, L2_cond_norm_bias, L2_cond_Wq, L2_cond_bq, L2_cond_Wk, L2_cond_bk, L2_cond_Wv, L2_cond_bv, L2_cond_film_emb_W, L2_cond_film_emb_b, L2_cond_film_norm_scale, L2_cond_film_norm_bias, L2_cond_film_out_W, L2_cond_film_out_b)
    x = _L3_cond_ref(x, cond_2048, mask_BxSx1_fk1, 8, L3_cond_ln_w, L3_cond_ln_b, L3_cond_Wq, L3_cond_bq, L3_cond_Wk, L3_cond_bk, L3_cond_Wv, L3_cond_bv, L3_cond_W_emb, L3_cond_b_emb, L3_cond_ln2_w, L3_cond_ln2_b, L3_cond_W_out, L3_cond_b_out)
    return x

_drawn_inputs = setup_inputs


def setup_inputs(seed=0):
    import zlib

    import numpy as np

    out = dict(_drawn_inputs(seed))
    spreads = {'L0_cond_ln_g': (1.0, 0.2),
     'L0_cond_ln_b': (0.0, 0.1),
     'L0_cond_ada_b': (0.0, 0.1),
     'L0_cond_conv_b': (0.0, 0.1),
     'L0_cond_D_param': (1.0, 0.2),
     'L1_cond_norm_w': (1.0, 0.2),
     'L1_cond_norm_b': (0.0, 0.1),
     'L1_cond_q_b': (0.0, 0.368),
     'L1_cond_k_b': (0.0, 0.8),
     'L1_cond_v_b': (0.0, 0.1),
     'L1_cond_emb_b': (0.0, 0.1),
     'L1_cond_sb_norm_w': (1.0, 0.2),
     'L1_cond_sb_norm_b': (0.0, 0.1),
     'L1_cond_out_b': (0.0, 0.1),
     'L2_cond_norm_scale': (1.0, 0.2),
     'L2_cond_norm_bias': (0.0, 0.1),
     'L2_cond_bq': (0.0, 0.294),
     'L2_cond_bk': (0.0, 0.8),
     'L2_cond_bv': (0.0, 0.1),
     'L2_cond_film_emb_b': (0.0, 0.1),
     'L2_cond_film_norm_scale': (1.0, 0.2),
     'L2_cond_film_norm_bias': (0.0, 0.1),
     'L2_cond_film_out_b': (0.0, 0.1),
     'L3_cond_ln_w': (1.0, 0.2),
     'L3_cond_ln_b': (0.0, 0.1),
     'L3_cond_bq': (0.0, 0.8),
     'L3_cond_bk': (0.0, 0.8),
     'L3_cond_bv': (0.0, 0.1),
     'L3_cond_b_emb': (0.0, 0.1),
     'L3_cond_ln2_w': (1.0, 0.2),
     'L3_cond_ln2_b': (0.0, 0.324),
     'L3_cond_b_out': (0.0, 0.1)}
    factors = {'L3_cond_Wq': 8.0, 'L3_cond_Wk': 8.0}
    for name, (base, spread) in spreads.items():
        noise = np.random.default_rng([zlib.crc32(name.encode()), seed]).standard_normal(out[name].shape)
        drawn = base * np.exp(spread * noise) if base else spread * noise
        out[name] = jnp.asarray(drawn.astype(out[name].dtype))
    for name, factor in factors.items():
        out[name] = (out[name] * factor).astype(out[name].dtype)
    return out
```

```python
from contextlib import ExitStack

import concourse.bass as bass
from concourse import mybir

F32 = mybir.dt.float32
F32R = mybir.dt.float32r
I32 = mybir.dt.int32
ACT = mybir.ActivationFunctionType
ALU = mybir.AluOpType
AX = mybir.AxisListType

P = 128
NB = 2
S = 2048
D = 512
KD = D // P
CH = 512
NC_B = S // CH
NCH = NB * NC_B
TT = CH // P
DI = 1024
CT = DI // P
N = 16
RANK = 64
CONV = 4
CW = 1024
KC = CW // P
EPS = 1e-5


class Chain:

    def __init__(self, engine, sem, base, per):
        self.engine, self.sem, self.base, self.per, self.n = engine, sem, base, per, 0

    def inc(self, ins):
        ins.then_inc(self.sem, 1)
        self.n += 1

    def wait(self):
        self.engine.wait_ge(self.sem, self.base * self.per + self.n)

    def end(self):
        assert self.n == self.per, (self.sem, self.n, self.per)


class Room:

    def __init__(self, nc, ctx, stage):
        self.nc, self.ctx, self.stage, self.sems = nc, ctx, stage, []
        ctx.callback(self.close)

    def sb(self, name, shape, dt=F32):
        return self.ctx.enter_context(self.nc.sbuf_tensor(f"{self.stage}_{name}", shape, dt))

    def ps(self, name, shape, dt=F32):
        return self.ctx.enter_context(self.nc.psum_tensor(f"{self.stage}_{name}", shape, dt))

    def sem(self, name):
        self.sems.append(self.nc.alloc_semaphore(f"{self.stage}_{name}"))
        return self.sems[-1]

    def close(self):
        self.nc.clear_and_free_semaphores(self.sems)
        self.nc.all_engine_barrier()


COLUMNS = [("L0_cond_ln_g", KD), ("L0_cond_ln_b", KD), ("L0_cond_ada_b", 3 * KD), ("L0_cond_conv_b", CT),
           ("L0_cond_dt_proj_b", CT), ("L0_cond_D_param", CT), ("L0_cond_conv_w", CT * CONV), ("L0_cond_A_log", CT * N),
           ("L1_cond_norm_w", KD), ("L1_cond_norm_b", KD), ("L1_cond_q_b", KD), ("L1_cond_k_b", KD),
           ("L1_cond_emb_b", 2 * KD), ("L1_cond_sb_norm_w", KD), ("L1_cond_sb_norm_b", KD),
           ("L2_cond_norm_scale", KD), ("L2_cond_norm_bias", KD), ("L2_cond_bk", KD),
           ("L2_cond_film_emb_b", 2 * KD), ("L2_cond_film_norm_scale", KD), ("L2_cond_film_norm_bias", KD),
           ("L3_cond_ln_w", KD), ("L3_cond_ln_b", KD), ("L3_cond_bk", KD),
           ("L3_cond_b_emb", 2 * KD), ("L3_cond_ln2_w", KD), ("L3_cond_ln2_b", KD)]
NCOLS = sum(w for _, w in COLUMNS)


def column(cols, name, first=0, count=None):
    at = 0
    for other, width in COLUMNS:
        if other == name:
            return cols[:, at + first:at + (width if count is None else first + count)]
        at += width
    raise KeyError(name)


def row_on_all(vec, parts=P):
    return bass.AP(tensor=vec.tensor, offset=vec.offset, ap=[[0, parts], [1, vec.shape[0]]])


def make_identity(pool, ident, done):
    pool.memset(ident[:, :], 0.0).then_inc(done, 1)
    pool.wait_ge(done, 1)
    pool.affine_select(out=ident[:, :], in_=ident[:, :], compare_op=ALU.not_equal, fill=1.0, base=0,
                       pattern=[[-1, P]], channel_multiplier=1).then_inc(done, 1)


def stage_condition(nc, a, keep):
    with ExitStack() as ctx:
        r = Room(nc, ctx, "cond")
        films = [("L1", a["L1_cond_emb_w"], "L1_cond_emb_b", "L1_cond_sb_norm_w", "L1_cond_sb_norm_b"),
                 ("L2", a["L2_cond_film_emb_W"], "L2_cond_film_emb_b", "L2_cond_film_norm_scale", "L2_cond_film_norm_bias"),
                 ("L3", a["L3_cond_W_emb"], "L3_cond_b_emb", "L3_cond_ln2_w", "L3_cond_ln2_b")]
        cond = r.sb("cond", [P, KC, NB])
        silu = r.sb("silu", [P, KC, NB])
        ada_w = r.sb("ada_w", [P, KC, 3 * D])
        film_w = r.sb("film_w", [P, KC, 2 * D])
        gate_b = r.sb("gate_b", [P, D])
        cols = keep["cols"]
        proj = r.sb("proj", [P, 4, 2, KD, NB])
        ps_col = [r.ps(f"ps_col{i}", [P, 2 * KD, NB]) for i in range(2)]
        ps_gate = [r.ps(f"ps_gate{i}", [P, D]) for i in range(NB)]
        cond_in, ada_in, film_in, small_in = (r.sem(x) for x in ("cond_in", "ada_in", "film_in", "small_in"))
        silu_done, cols_done, gate_done = (r.sem(x) for x in ("silu_done", "cols_done", "gate_done"))
        bias_done, fold_done = (r.sem(x) for x in ("bias_done", "fold_done"))
        block = ctx.enter_context(nc.Block())

        @block.sync
        def _(sp):
            sp.dma_start(cond[:, :, :], a["cond_T"].rearrange("(k p) b -> p k b", p=P)).then_inc(cond_in, 16)
            sp.dma_start(ada_w[:, :, :], a["ada_w_T"].rearrange("(k p) n -> p k n", p=P)).then_inc(ada_in, 16)
            for i, film in enumerate(films):
                if i:
                    sp.wait_ge(cols_done, i + 1)
                sp.dma_start(film_w[:, :, :], film[1].rearrange("(k p) n -> p k n", p=P)).then_inc(film_in, 16)

        @block.scalar
        def _(act):
            act.dma_start(cols[:, :], a["columns"]).then_inc(small_in, 16)
            act.dma_start(gate_b[:, :], row_on_all(a["L0_cond_ada_b"][2 * D:3 * D])).then_inc(small_in, 16)
            act.wait_ge(cond_in, 16)
            nc.scalar.activation(silu[:, :, :], cond[:, :, :], ACT.Silu).then_inc(silu_done, 1)

        @block.tensor
        def _(pe):
            pe.wait_ge(silu_done, 1)
            for i in range(4):
                if i == 0:
                    pe.wait_ge(ada_in, 16)
                else:
                    pe.wait_ge(film_in, 16 * i)
                if i >= 2:
                    pe.wait_ge(bias_done, 2 * (i - 1))
                w = ada_w if i == 0 else film_w
                for t in range(2 * KD):
                    for k in range(KC):
                        mm = nc.tensor.matmul(ps_col[i % 2][:, t, :], w[:, k, t * P:(t + 1) * P], silu[:, k, :],
                                              start=(k == 0), stop=(k == KC - 1))
                mm.then_inc(cols_done, 1)
                if i == 0:
                    for b in range(NB):
                        for k in range(KC):
                            mm = nc.tensor.matmul(ps_gate[b][:, :], silu[:, k, b:b + 1].to_broadcast([P, P]),
                                                  ada_w[:, k, 2 * D:3 * D], start=(k == 0), stop=(k == KC - 1))
                    mm.then_inc(gate_done, 1)

        @block.vector
        def _(dve):
            dve.wait_ge(small_in, 16 * 2)
            for i in range(4):
                dve.wait_ge(cols_done, i + 1)
                bias = column(cols, "L0_cond_ada_b" if i == 0 else films[i - 1][2], 0, 2 * KD)
                for part in range(2):
                    slot = (1 - part) if i == 0 else part
                    nc.vector.tensor_tensor(
                        proj[:, i, slot, :, :], ps_col[i % 2][:, part * KD:(part + 1) * KD, :],
                        bias[:, part * KD:(part + 1) * KD].unsqueeze(2).to_broadcast([P, KD, NB]), ALU.add
                    ).then_inc(bias_done, 1)
                dve.wait_ge(bias_done, 2 * (i + 1))
                w, nb = (column(cols, v).unsqueeze(2).to_broadcast([P, KD, NB])
                         for v in (("L0_cond_ln_g", "L0_cond_ln_b") if i == 0 else films[i - 1][3:]))
                col = keep["film"]
                nc.vector.tensor_scalar(proj[:, i, 0, :, :], proj[:, i, 0, :, :], 1.0, None, ALU.add).then_inc(fold_done, 1)
                dve.wait_ge(fold_done, 3 * i + 1)
                nc.vector.tensor_tensor(col[:, i, 0, :, :], proj[:, i, 0, :, :], w, ALU.mult)
                nc.vector.tensor_tensor(col[:, i, 1, :, :], proj[:, i, 0, :, :], nb, ALU.mult).then_inc(fold_done, 1)
                dve.wait_ge(fold_done, 3 * i + 2)
                nc.vector.tensor_tensor(col[:, i, 1, :, :], col[:, i, 1, :, :], proj[:, i, 1, :, :], ALU.add).then_inc(fold_done, 1)
                if i == 0:
                    dve.wait_ge(gate_done, 1)
                    for b in range(NB):
                        nc.vector.tensor_tensor(keep["gate"][:, b, :], ps_gate[b][:, :], gate_b[:, :], ALU.add)
            dve.wait_ge(fold_done, 12)

        @block.gpsimd
        def _(pool):
            make_identity(pool, keep["ident"], r.sem("ident_done"))
            nc.gpsimd.memset(keep["neg_half"][:, :], -0.5)


def stage_mamba(nc, a, keep, out):
    with ExitStack() as ctx:
        r = Room(nc, ctx, "mamba")
        G = 2
        NG = N // G
        BC_ROWS = 2 * N
        w_in = r.sb("w_in", [P, KD, 2 * DI])
        w_out = r.sb("w_out", [P, CT, D])
        w_x = r.sb("w_x", [P, CT, RANK + BC_ROWS])
        w_dt = r.sb("w_dt", [RANK, DI])
        cols = keep["cols"]
        conv_w = column(cols, "L0_cond_conv_w").rearrange("p (t j) -> p t j", j=CONV)
        conv_b = column(cols, "L0_cond_conv_b")
        dt_b = column(cols, "L0_cond_dt_proj_b")
        d_par = column(cols, "L0_cond_D_param")
        a_log = column(cols, "L0_cond_A_log").rearrange("p (t n) -> p t n", n=N)
        a_exp = r.sb("a_exp", [P, CT, N])
        a_neg = r.sb("a_neg", [P, CT, N])
        pick = r.sb("pick", [2 * BC_ROWS, BC_ROWS], F32R)
        shared = r.sb("shared", [P, 8 * CH])
        x_in = shared[:, 0:TT * D].rearrange("p (t d) -> p t d", t=TT)
        xn_t = shared[:, TT * D:2 * TT * D].rearrange("p (k s) -> p k s", k=KD)
        hc = shared[:, :].rearrange("p (r g s) -> p r g s", r=4, g=G)
        x_ext = r.sb("x_ext", [P, 2, CONV - 1 + CH])
        halo = r.sb("halo", [P, CT, CONV - 1])
        u = r.sb("u", [P, CT, CH])
        zy = r.sb("zy", [P, CT, CH])
        dt_r = r.sb("dt_r", [RANK, CH])
        bc_parts = r.sb("bc_parts", [2 * BC_ROWS, CH], F32R)
        bc = r.sb("bc", [P, BC_ROWS, CH])
        stats = r.sb("stats", [P, TT, 6])
        mv = r.sb("mv", [P, TT, 2])
        rstd = r.sb("rstd", [P, TT])
        var_eps = r.sb("var_eps", [P, TT])
        conv = r.sb("conv", [P, 2, CH])
        dt = conv
        soft = r.sb("soft", [P, CH])
        du = r.sb("du", [P, CH])
        da = r.sb("da", [P, 2, G, CH])
        h = r.sb("h", [P, 2, G, CH])
        state = r.sb("state", [P, CT, N])
        x_res = x_ext[:, :, CONV - 1:]
        bank = [r.ps(f"bank{i}", [P, CH]) for i in range(8)]
        ident, gate, neg_half = keep["ident"], keep["gate"], keep["neg_half"]
        fa, fb = keep["film"][:, 0, 0], keep["film"][:, 0, 1]
        names = ("weights_in x_loaded var_done rstd_done x_normed transposed turned in_mm ext_copied conv_done "
                 "u_done z_done x_mm part_a_done part_b_done bc_mm bc_act_done bc_dve_done dt_mm v_done soft_done dt_done "
                 "du_done da_done h_done hc_done sum_mm gated out_mm residual_in out_done stored own_dve own_act "
                 "setup_done reset_done")
        s = {n: r.sem(n) for n in names.split()}
        block = ctx.enter_context(nc.Block())
        x_rows = a["x"].rearrange("b s d -> (b s) d")
        CG = CT * NG

        @block.sync
        def _(sp):
            sp.dma_start(w_in[:, :, :], a["in_proj_w_T"].rearrange("(k p) n -> p k n", p=P)).then_inc(s["weights_in"], 16)
            sp.dma_start(w_x[:, :, :], a["x_proj_w_T"].rearrange("(k p) n -> p k n", p=P)).then_inc(s["weights_in"], 16)
            sp.dma_start(w_dt[:, :], a["dt_proj_w_T"]).then_inc(s["weights_in"], 16)
            sp.dma_start(w_out[:, :, :], a["out_proj_w_T"].rearrange("(k p) n -> p k n", p=P)).then_inc(s["weights_in"], 16)
            with sp.Fori(0, NB) as b, sp.Fori(0, NC_B) as c:
                it = b * NC_B + c
                sp.wait_ge(s["sum_mm"], it * CG)
                sp.dma_start(x_in, x_rows[bass.ds(it * CH, CH), :].rearrange("(t p) d -> p t d", p=P)).then_inc(s["x_loaded"], 16)
                sp.wait_ge(s["conv_done"], (it + 1) * CT)
                for t in range(TT):
                    if t >= 2:
                        sp.wait_ge(s["stored"], it * 16 * TT + 16 * (t - 1))
                    sp.dma_start(x_res[:, t % 2, :], x_rows[bass.ds(it * CH + t * P, P), :]).then_inc(s["residual_in"], 16)
                    sp.wait_ge(s["out_done"], it * TT + t + 1)
                    sp.dma_start(out[bass.ds(it * CH + t * P, P), :], x_res[:, t % 2, :]).then_inc(s["stored"], 16)
            sp.wait_ge(s["stored"], NCH * TT * 16)

        @block.gpsimd
        def _(pool):
            with pool.Fori(0, NB) as b, pool.Fori(0, NC_B) as c:
                it = b * NC_B + c
                pool.wait_ge(s["var_done"], it + 1)
                nc.gpsimd.tensor_tensor(rstd[:, :], var_eps[:, :], neg_half[:, 0:TT], ALU.pow).then_inc(s["rstd_done"], 1)
                for i in range(CG):
                    g = i % NG
                    pool.wait_ge(s["h_done"], it * CG + i + 1)
                    if i == 0:
                        pool.wait_ge(s["in_mm"], (it + 1) * 2 * CT)
                    elif i >= 4:
                        pool.wait_ge(s["sum_mm"], it * CG + i - 3)
                    nc.gpsimd.tensor_tensor(hc[:, i % 4, :, :], h[:, i % 2, :, :],
                                            bc[:, N + g * G:N + (g + 1) * G, :], ALU.mult).then_inc(s["hc_done"], 1)

        @block.scalar
        def _(act):
            nc.scalar.activation(a_exp[:, :, :], a_log, ACT.Exp).then_inc(s["setup_done"], 1)
            act.wait_ge(s["setup_done"], 1)
            nc.scalar.activation(a_neg[:, :, :], a_exp[:, :, :], ACT.Copy, scale=-1.0).then_inc(s["setup_done"], 1)
            for half in range(2):
                nc.scalar.activation(pick[half * BC_ROWS:(half + 1) * BC_ROWS, :], ident[0:BC_ROWS, 0:BC_ROWS],
                                     ACT.Copy).then_inc(s["setup_done"], 1)
            act.wait_ge(s["setup_done"], 4)
            with act.Fori(0, NB) as b, act.Fori(0, NC_B) as c:
                it = b * NC_B + c
                own = Chain(act, s["own_act"], it, 2 * CT)
                for k in range(KD):
                    act.wait_ge(s["transposed"], it * KD + k + 1)
                    nc.scalar.activation(xn_t[:, k, :], bank[k][:, :], ACT.Identity,
                                         scale=fa[:, k, bass.ds(b, 1)], bias=fb[:, k, bass.ds(b, 1)]).then_inc(s["turned"], 1)
                act.wait_ge(s["stored"], it * 16 * TT)
                for e in range(CT + 1):
                    if e < CT:
                        act.wait_ge(s["in_mm"], it * 2 * CT + e + 1)
                        if e >= 2:
                            act.wait_ge(s["conv_done"], it * CT + e - 1)
                        nc.scalar.activation(x_ext[:, e % 2, CONV - 1:], bank[4 + e % 2][:, :], ACT.Copy).then_inc(s["ext_copied"], 1)
                    if e >= 1:
                        act.wait_ge(s["conv_done"], it * CT + e)
                        nc.scalar.activation(u[:, e - 1, :], conv[:, (e - 1) % 2, :], ACT.Silu).then_inc(s["u_done"], 1)
                act.wait_ge(s["out_mm"], it * TT)
                for e in range(CT):
                    act.wait_ge(s["in_mm"], it * 2 * CT + CT + e + 1)
                    nc.scalar.activation(zy[:, e, :], bank[4 + e % 2][:, :], ACT.Silu).then_inc(s["z_done"], 1)
                act.wait_ge(s["x_mm"], it + 1)
                nc.scalar.activation(dt_r[:, :], bank[6][0:RANK, :], ACT.Copy).then_inc(s["part_a_done"], 1)
                nc.scalar.activation(bc_parts[0:BC_ROWS, :], bank[6][RANK:RANK + BC_ROWS, :], ACT.Copy).then_inc(s["part_a_done"], 1)
                for n in range(0, BC_ROWS, 2):
                    act.wait_ge(s["bc_mm"], it * BC_ROWS + n + 1)
                    nc.scalar.activation(bc[:, n, :], bank[n % 4][:, :], ACT.Copy).then_inc(s["bc_act_done"], 1)

                def softplus(ct):
                    act.wait_ge(s["v_done"], it * CT + ct + 1)
                    own.inc(nc.scalar.activation(soft[:, :], dt[:, ct % 2, :], ACT.Abs))
                    own.wait()
                    own.inc(nc.scalar.activation(soft[:, :], soft[:, :], ACT.Exp, scale=-1.0))
                    own.wait()
                    nc.scalar.activation(soft[:, :], soft[:, :], ACT.Ln, bias=1.0).then_inc(s["soft_done"], 1)

                softplus(0)
                for ct in range(CT):
                    act.wait_ge(s["dt_done"], it * CT + ct + 1)
                    for g in range(NG):
                        i = ct * NG + g
                        act.wait_ge(s["h_done"], it * CG + max(i - 1, 0))
                        for j in range(G):
                            n = g * G + j
                            last = nc.scalar.activation(da[:, i % 2, j, :], dt[:, ct % 2, :], ACT.Exp, scale=a_neg[:, ct, n:n + 1])
                        last.then_inc(s["da_done"], 1)
                        if g == NG // 2 and ct + 1 < CT:
                            softplus(ct + 1)
                own.end()

        @block.vector
        def _(dve):
            with dve.Fori(0, NB) as b:
                nc.vector.memset(halo[:, :, :], 0.0).then_inc(s["reset_done"], 1)
                nc.vector.memset(state[:, :, :], 0.0).then_inc(s["reset_done"], 1)
                with dve.Fori(0, NC_B) as c:
                    it = b * NC_B + c
                    own = Chain(dve, s["own_dve"], it, 2 + 5 * CT + 2 * CT + CG + CG + TT)
                    dve.wait_ge(s["reset_done"], 2 * b + 2)
                    dve.wait_ge(s["x_loaded"], it * 16 + 16)
                    for t in range(TT):
                        st = nc.vector.bn_stats(stats[:, t, :], x_in[:, t, :])
                    own.inc(st)
                    own.wait()
                    nc.vector.memset(var_eps[:, :], 0.0)
                    for t in range(TT):
                        st = nc.vector.bn_aggr(mv[:, t, :], stats[:, t, :])
                    own.inc(st)
                    own.wait()
                    nc.vector.tensor_scalar(var_eps[:, :], mv[:, :, 1], EPS, None, ALU.add).then_inc(s["var_done"], 1)
                    dve.wait_ge(s["rstd_done"], it + 1)
                    for t in range(TT):
                        last = nc.vector.tensor_scalar(x_in[:, t, :], x_in[:, t, :], mv[:, t, 0:1], rstd[:, t:t + 1],
                                                       ALU.subtract, ALU.mult)
                    last.then_inc(s["x_normed"], 1)
                    for e in range(CT):
                        w = e % 2
                        dve.wait_ge(s["ext_copied"], it * CT + e + 1)
                        own.inc(nc.vector.tensor_copy(x_ext[:, w, 0:CONV - 1], halo[:, e, :]))
                        own.wait()
                        own.inc(nc.vector.tensor_copy(halo[:, e, :], x_ext[:, w, CH:CH + CONV - 1]))
                        own.wait()
                        if e >= 2:
                            dve.wait_ge(s["u_done"], it * CT + e - 1)
                        own.inc(nc.vector.tensor_scalar(conv[:, w, :], x_ext[:, w, 0:CH], conv_w[:, e, 0:1], conv_b[:, e:e + 1],
                                                        ALU.mult, ALU.add))
                        for j in range(1, CONV):
                            own.wait()
                            last = nc.vector.scalar_tensor_tensor(out=conv[:, w, :], in0=x_ext[:, w, j:j + CH],
                                                                  scalar=conv_w[:, e, j:j + 1], in1=conv[:, w, :],
                                                                  op0=ALU.mult, op1=ALU.add)
                            if j < CONV - 1:
                                own.inc(last)
                        last.then_inc(s["conv_done"], 1)
                    dve.wait_ge(s["part_a_done"], it * 2 + 2)
                    nc.vector.tensor_tensor(bc_parts[BC_ROWS:2 * BC_ROWS, :], bank[6][RANK:RANK + BC_ROWS, :],
                                            bc_parts[0:BC_ROWS, :].bitcast(F32), ALU.subtract).then_inc(s["part_b_done"], 1)
                    for n in range(1, BC_ROWS, 2):
                        dve.wait_ge(s["bc_mm"], it * BC_ROWS + n + 1)
                        nc.vector.tensor_copy(bc[:, n, :], bank[n % 4][:, :]).then_inc(s["bc_dve_done"], 1)
                    dve.wait_ge(s["bc_act_done"], (it + 1) * N)
                    dve.wait_ge(s["bc_dve_done"], (it + 1) * N)
                    dve.wait_ge(s["u_done"], (it + 1) * CT)
                    dve.wait_ge(s["z_done"], (it + 1) * CT)

                    def take_v(ct):
                        dve.wait_ge(s["dt_mm"], it * CT + ct + 1)
                        if ct >= 2:
                            dve.wait_ge(s["da_done"], it * CG + (ct - 1) * NG)
                        nc.vector.tensor_scalar(dt[:, ct % 2, :], bank[6 + ct % 2][:, :], dt_b[:, ct:ct + 1], None,
                                                ALU.add).then_inc(s["v_done"], 1)

                    def make_dt(ct):
                        dve.wait_ge(s["soft_done"], it * CT + ct + 1)
                        nc.vector.scalar_tensor_tensor(out=dt[:, ct % 2, :], in0=dt[:, ct % 2, :], scalar=0.0, in1=soft[:, :],
                                                       op0=ALU.max, op1=ALU.add).then_inc(s["dt_done"], 1)

                    def save_state(i):
                        ct, g = divmod(i, NG)
                        dve.wait_ge(s["h_done"], it * CG + i + 1)
                        return nc.vector.tensor_copy(state[:, ct, g * G:(g + 1) * G], h[:, i % 2, :, CH - 1])

                    def gate_y(ct):
                        dve.wait_ge(s["sum_mm"], it * CG + (ct + 1) * NG)
                        own.inc(nc.vector.scalar_tensor_tensor(out=u[:, ct, :], in0=u[:, ct, :], scalar=d_par[:, ct:ct + 1],
                                                               in1=bank[4 + ct % 2][:, :], op0=ALU.mult, op1=ALU.add))
                        own.wait()
                        nc.vector.tensor_tensor(zy[:, ct, :], u[:, ct, :], zy[:, ct, :], ALU.mult).then_inc(s["gated"], 1)

                    take_v(0)
                    make_dt(0)
                    for ct in range(CT):
                        dve.wait_ge(s["dt_done"], it * CT + ct + 1)
                        own.inc(nc.vector.tensor_tensor(du[:, :], dt[:, ct % 2, :], u[:, ct, :], ALU.mult))
                        own.wait()
                        for g in range(NG):
                            i = ct * NG + g
                            if i >= 2:
                                dve.wait_ge(s["hc_done"], it * CG + i - 1)
                            own.inc(nc.vector.tensor_tensor(h[:, i % 2, :, :], du[:, :].unsqueeze(1).to_broadcast([P, G, CH]),
                                                            bc[:, g * G:(g + 1) * G, :], ALU.mult))
                            if i >= 1:
                                own.inc(save_state(i - 1))
                            dve.wait_ge(s["da_done"], it * CG + i + 1)
                            own.wait()
                            for j in range(G):
                                last = nc.vector.tensor_tensor_scan(h[:, i % 2, j, :], da[:, i % 2, j, :], h[:, i % 2, j, :],
                                                                    state[:, ct, g * G + j:g * G + j + 1], ALU.mult, ALU.add)
                            last.then_inc(s["h_done"], 1)
                            if g == 2 and ct >= 1:
                                gate_y(ct - 1)
                            if g == NG // 2 - 1 and ct + 1 < CT:
                                take_v(ct + 1)
                            if g == NG // 2 + 1 and ct + 1 < CT:
                                make_dt(ct + 1)
                    own.inc(save_state(CG - 1))
                    own.wait()
                    gate_y(CT - 1)
                    for t in range(TT):
                        dve.wait_ge(s["out_mm"], it * TT + t + 1)
                        own.inc(nc.vector.tensor_tensor(bank[t][:, :], bank[t][:, :], gate[:, bass.ds(b, 1), :].rearrange("p a d -> p (a d)"), ALU.mult))
                        own.wait()
                        dve.wait_ge(s["residual_in"], it * TT * 16 + 16 * (t + 1))
                        nc.vector.tensor_tensor(x_res[:, t % 2, :], bank[t][:, :], x_res[:, t % 2, :], ALU.add).then_inc(s["out_done"], 1)
                    own.end()

        @block.tensor
        def _(pe):
            pe.wait_ge(s["weights_in"], 64)
            pe.wait_ge(s["setup_done"], 4)
            with pe.Fori(0, NB) as b, pe.Fori(0, NC_B) as c:
                it = b * NC_B + c
                pe.wait_ge(s["x_normed"], it + 1)
                pe.wait_ge(s["out_done"], it * TT)
                for k in range(KD):
                    for t in range(TT):
                        mm = nc.tensor.transpose(bank[k][:, t * P:(t + 1) * P], x_in[:, t, k * P:(k + 1) * P], ident[:, :])
                    mm.then_inc(s["transposed"], 1)
                for e in range(2 * CT):
                    if e == 0:
                        pe.wait_ge(s["turned"], (it + 1) * KD)
                    elif 2 <= e < CT + 2:
                        pe.wait_ge(s["ext_copied"], it * CT + e - 1)
                    elif e >= CT + 2:
                        pe.wait_ge(s["z_done"], it * CT + e - CT - 1)
                    for k in range(KD):
                        mm = nc.tensor.matmul(bank[4 + e % 2][:, :], w_in[:, k, e * P:(e + 1) * P], xn_t[:, k, :],
                                              start=(k == 0), stop=(k == KD - 1))
                    mm.then_inc(s["in_mm"], 1)
                for k in range(CT):
                    pe.wait_ge(s["u_done"], it * CT + k + 1)
                    mm = nc.tensor.matmul(bank[6][0:RANK + BC_ROWS, :], w_x[:, k, :], u[:, k, :], start=(k == 0), stop=(k == CT - 1))
                mm.then_inc(s["x_mm"], 1)
                pe.wait_ge(s["part_a_done"], it * 2 + 2)
                pe.wait_ge(s["part_b_done"], it + 1)
                for n in range(BC_ROWS):
                    if n >= 4:
                        done = s["bc_dve_done"] if n % 2 else s["bc_act_done"]
                        pe.wait_ge(done, it * N + n // 2 - 1)
                    nc.tensor.matmul(bank[n % 4][:, :], pick[:, n:n + 1].to_broadcast([2 * BC_ROWS, P]), bc_parts[:, :],
                                     start=True, stop=True).then_inc(s["bc_mm"], 1)

                def project_dt(ct):
                    if ct >= 2:
                        pe.wait_ge(s["dt_done"], it * CT + ct - 1)
                    nc.tensor.matmul(bank[6 + ct % 2][:, :], w_dt[:, ct * P:(ct + 1) * P], dt_r[:, :],
                                     start=True, stop=True).then_inc(s["dt_mm"], 1)

                project_dt(0)
                for ct in range(CT):
                    if ct + 1 < CT:
                        project_dt(ct + 1)
                    if ct < 2:
                        pe.wait_ge(s["z_done"], (it + 1) * CT)
                    else:
                        pe.wait_ge(s["gated"], it * CT + ct - 1)
                    for g in range(NG):
                        i = ct * NG + g
                        pe.wait_ge(s["hc_done"], it * CG + i + 1)
                        for j in range(G):
                            mm = nc.tensor.matmul(bank[4 + ct % 2][:, :], ident[:, :], hc[:, i % 4, j, :],
                                                  start=(g == 0 and j == 0), stop=(g == NG - 1 and j == G - 1))
                        mm.then_inc(s["sum_mm"], 1)
                pe.wait_ge(s["gated"], (it + 1) * CT)
                for t in range(TT):
                    for k in range(CT):
                        mm = nc.tensor.matmul(bank[t][:, :], zy[:, k, t * P:(t + 1) * P], w_out[:, k, :],
                                              start=(k == 0), stop=(k == CT - 1))
                    mm.then_inc(s["out_mm"], 1)



class Norm:

    def __init__(self, r, keep, banks=None):
        self.x = r.sb("norm_x", [P, TT, D])
        self.xn_t = r.sb("norm_xn_t", [P, KD, CH])
        self.stats = r.sb("norm_stats", [P, TT, 6])
        self.mv = r.sb("norm_mv", [P, TT, 2])
        self.var_eps = r.sb("norm_var_eps", [P, TT])
        self.rstd = r.sb("norm_rstd", [P, TT])
        self.bank = banks or [r.ps(f"norm_bank{i}", [P, CH]) for i in range(4)]
        self.ident, self.neg_half = keep["ident"], keep["neg_half"]
        self.x_loaded, self.var_done, self.rstd_done, self.x_normed, self.transposed, self.turned = (
            r.sem(n) for n in ("x_loaded", "var_done", "rstd_done", "x_normed", "transposed", "turned"))


DVE_NORM = 2


def norm_load(sp, m, rows, it):
    sp.wait_ge(m.transposed, it * KD)
    sp.dma_start(m.x[:, :, :], rows[bass.ds(it * CH, CH), :].rearrange("(t p) d -> p t d", p=P)).then_inc(m.x_loaded, 16)


def norm_dve(nc, dve, m, own, it, src):
    for t in range(TT):
        last = nc.vector.bn_stats(m.stats[:, t, :], src(t))
    own.inc(last)
    own.wait()
    nc.vector.memset(m.var_eps[:, :], 0.0)
    for t in range(TT):
        last = nc.vector.bn_aggr(m.mv[:, t, :], m.stats[:, t, :])
    own.inc(last)
    own.wait()
    nc.vector.tensor_scalar(m.var_eps[:, :], m.mv[:, :, 1], EPS, None, ALU.add).then_inc(m.var_done, 1)
    dve.wait_ge(m.rstd_done, it + 1)
    dve.wait_ge(m.transposed, it * KD)
    for t in range(TT):
        last = nc.vector.tensor_scalar(m.x[:, t, :], src(t), m.mv[:, t, 0:1], m.rstd[:, t:t + 1],
                                       ALU.subtract, ALU.mult)
    last.then_inc(m.x_normed, 1)


def norm_pool(nc, pool, m, it):
    pool.wait_ge(m.var_done, it + 1)
    nc.gpsimd.tensor_tensor(m.rstd[:, :], m.var_eps[:, :], m.neg_half[:, 0:TT], ALU.pow).then_inc(m.rstd_done, 1)


def norm_pe(nc, pe, m, it):
    pe.wait_ge(m.x_normed, it + 1)
    pe.wait_ge(m.turned, it * KD)
    for k in range(KD):
        for t in range(TT):
            mm = nc.tensor.transpose(m.bank[k][:, t * P:(t + 1) * P], m.x[:, t, k * P:(k + 1) * P], m.ident[:, :])
        mm.then_inc(m.transposed, 1)


def norm_act(nc, act, m, it, func, scale, bias):
    for k in range(KD):
        act.wait_ge(m.transposed, it * KD + k + 1)
        nc.scalar.activation(m.xn_t[:, k, :], m.bank[k][:, :], func, scale=scale(k), bias=bias(k)).then_inc(m.turned, 1)


H1 = 16
DH1 = D // H1
QT = S // P
NT = NB * QT


def stage_qkv(nc, a, keep, src, parts, mask_parts, v_aug):
    with ExitStack() as ctx:
        r = Room(nc, ctx, "qkv")
        m = Norm(r, keep)
        w = [r.sb(f"w_{n}", [P, KD, D]) for n in "qkv"]
        v_b = r.sb("v_b", [P, D])
        mask = r.sb("mask", [P, NT])
        mrow = r.sb("mrow", [NT, P])
        mrow_parts = r.sb("mrow_parts", [NT, 2, P], F32R)
        vb = r.sb("vb", [P, 2, D])
        full = r.sb("full", [P, 2, CH])
        pair = r.sb("pair", [P, 2, 2, CH], F32R)
        bank = [r.ps(f"bank{i}", [P, CH]) for i in range(4)]
        names = "weights_in small_in ones_done mask_done mask_stored v_mm v_biased v_done qk_mm full_done first_done second_done own_dve"
        s = {n: r.sem(n) for n in names.split()}
        stored = [r.sem(f"stored{i}") for i in range(2)]
        cols = keep["cols"]
        g, bvec = column(cols, "L1_cond_norm_w"), column(cols, "L1_cond_norm_b")
        qk_bias = [column(cols, "L1_cond_q_b"), column(cols, "L1_cond_k_b")]
        block = ctx.enter_context(nc.Block())
        NQ = 2 * KD

        @block.sync
        def _(sp):
            sp.dma_start(w[2][:, :, :], a["L1_cond_v_w"].rearrange("(k p) n -> p k n", p=P)).then_inc(s["weights_in"], 16)
            sp.dma_start(w[0][:, :, :], a["L1_cond_q_w"].rearrange("(k p) n -> p k n", p=P)).then_inc(s["weights_in"], 16)
            sp.dma_start(w[1][:, :, :], a["L1_cond_k_w"].rearrange("(k p) n -> p k n", p=P)).then_inc(s["weights_in"], 16)
            with sp.Fori(0, NCH) as it:
                norm_load(sp, m, src, it)
            sp.wait_ge(s["mask_done"], 3)
            sp.dma_start(mask_parts.rearrange("a (t j) -> t a j", j=P), mrow_parts[:, :, :].bitcast(F32)).then_inc(s["mask_stored"], 16)
            sp.wait_ge(s["mask_stored"], 16)
            for slot in range(2):
                sp.wait_ge(stored[slot], NCH * NQ // 2 * 16)

        @block.gpsimd
        def _(pool):
            nc.gpsimd.memset(v_aug[:, :, :, DH1:DH1 + 1], 1.0).then_inc(s["ones_done"], 1)
            with pool.Fori(0, NCH) as it:
                norm_pool(nc, pool, m, it)
                for i in range(NQ):
                    which, mt = divmod(i, KD)
                    pool.wait_ge(s["second_done"], it * NQ + i + 1)
                    pool.dma_start(parts[which, :, mt * P:(mt + 1) * P, bass.ds(it * CH, CH)].rearrange("a p s -> p a s"),
                                   pair[:, i % 2, :, :].bitcast(F32)).then_inc(stored[i % 2], 16)

        @block.tensor
        def _(pe):
            pe.wait_ge(s["weights_in"], 48)
            with pe.Fori(0, NCH) as it:
                norm_pe(nc, pe, m, it)
                pe.wait_ge(m.turned, (it + 1) * KD)
                for t in range(TT):
                    pe.wait_ge(s["v_biased"], it * TT + t - 1) if t >= 2 else pe.wait_ge(s["v_biased"], it * TT)
                    for k in range(KD):
                        mm = nc.tensor.matmul(bank[t % 2][:, :], m.xn_t[:, k, t * P:(t + 1) * P], w[2][:, k, :],
                                              start=(k == 0), stop=(k == KD - 1))
                    mm.then_inc(s["v_mm"], 1)
                for i in range(NQ):
                    which, mt = divmod(i, KD)
                    pe.wait_ge(s["full_done"], it * NQ + i - 1) if i >= 2 else pe.wait_ge(s["full_done"], it * NQ)
                    for k in range(KD):
                        mm = nc.tensor.matmul(bank[2 + i % 2][:, :], w[which][:, k, mt * P:(mt + 1) * P], m.xn_t[:, k, :],
                                              start=(k == 0), stop=(k == KD - 1))
                    mm.then_inc(s["qk_mm"], 1)

        @block.scalar
        def _(act):
            act.dma_start(v_b[:, :], row_on_all(a["L1_cond_v_b"])).then_inc(s["small_in"], 16)
            act.dma_start(mask[:, :], a["mask_ff1_columns"]).then_inc(s["small_in"], 16)
            act.dma_start(mrow[:, :], a["mask_BxS_ff1"].rearrange("b (t j) -> (b t) j", j=P)).then_inc(s["small_in"], 16)
            act.wait_ge(s["mask_done"], 1)
            nc.scalar.activation(mrow_parts[:, 0, :], mrow[:, :], ACT.Copy).then_inc(s["mask_done"], 1)
            act.wait_ge(s["ones_done"], 1)
            with act.Fori(0, NCH) as it:
                act.wait_ge(s["qk_mm"], it * NQ)
                norm_act(nc, act, m, it, ACT.Identity, lambda k: g[:, k:k + 1], lambda k: bvec[:, k:k + 1])
                for t in range(TT):
                    act.wait_ge(s["v_biased"], it * TT + t + 1)
                    nc.scalar.activation(v_aug[:, bass.ds(it * TT + t, 1), :, 0:DH1].rearrange("p a h e -> p (a h) e"),
                                         vb[:, t % 2, :].rearrange("p (h e) -> p h e", e=DH1), ACT.Copy,
                                         scale=mask[:, bass.ds(it * TT + t, 1)]).then_inc(s["v_done"], 1)
                for i in range(NQ):
                    which, mt = divmod(i, KD)
                    act.wait_ge(s["qk_mm"], it * NQ + i + 1)
                    act.wait_ge(s["second_done"], it * NQ + max(i - 1, 0))
                    nc.scalar.activation(full[:, i % 2, :], bank[2 + i % 2][:, :], ACT.Identity,
                                         bias=qk_bias[which][:, mt:mt + 1]).then_inc(s["full_done"], 1)
                    act.wait_ge(s["full_done"], it * NQ + i + 1)
                    act.wait_ge(stored[i % 2], (it * (NQ // 2) + i // 2) * 16)
                    nc.scalar.activation(pair[:, i % 2, 0, :], full[:, i % 2, :], ACT.Copy).then_inc(s["first_done"], 1)

        @block.vector
        def _(dve):
            dve.wait_ge(s["small_in"], 48)
            nc.vector.tensor_scalar(mrow[:, :], mrow[:, :], 1e6, -1e6, ALU.mult, ALU.add).then_inc(s["mask_done"], 1)
            dve.wait_ge(s["mask_done"], 2)
            nc.vector.tensor_tensor(mrow_parts[:, 1, :], mrow[:, :], mrow_parts[:, 0, :].bitcast(F32), ALU.subtract).then_inc(s["mask_done"], 1)
            with dve.Fori(0, NCH) as it:
                own = Chain(dve, s["own_dve"], it, DVE_NORM)
                dve.wait_ge(m.x_loaded, (it + 1) * 16)
                norm_dve(nc, dve, m, own, it, lambda t: m.x[:, t, :])
                for t in range(TT):
                    dve.wait_ge(s["v_mm"], it * TT + t + 1)
                    dve.wait_ge(s["v_done"], it * TT + max(t - 1, 0))
                    nc.vector.tensor_tensor(vb[:, t % 2, :], bank[t % 2][:, :], v_b[:, :], ALU.add).then_inc(s["v_biased"], 1)
                for i in range(NQ):
                    dve.wait_ge(s["first_done"], it * NQ + i + 1)
                    nc.vector.tensor_tensor(pair[:, i % 2, 1, :], full[:, i % 2, :], pair[:, i % 2, 0, :].bitcast(F32),
                                            ALU.subtract).then_inc(s["second_done"], 1)
                own.end()


def stage_attention(nc, a, keep, parts, mask_parts, max_rows, v_aug, y):
    with ExitStack() as ctx:
        r = Room(nc, ctx, "attn")
        ROWS_MAX, ROWS = 3 * DH1 + 2, 3 * DH1 + 4
        HALF = S // 2
        STEPS = 2 * QT
        NMAX = QT * (S // CH)
        FIRST_MAX, PER_STEP = 3, 3
        TURN_STEP = 26
        JT = HALF // P
        q_st = [r.sb(f"q_stack{i}", [ROWS, S], F32R) for i in range(2)]
        k_st = [r.sb(f"k_stack{i}", [ROWS, S], F32R) for i in range(2)]
        prob = [r.sb(f"prob{i}", [P, HALF]) for i in range(4)]
        mx = r.sb("mx", [P, QT, S // CH])
        m_all = r.sb("m_all", [P, QT])
        m_parts = r.sb("m_parts", [QT, 2, P], F32R)
        rden = r.sb("rden", [P, JT, 1])
        v_h = [r.sb(f"v_h{i}", [P, QT, DH1 + 1]) for i in range(2)]
        o_t = r.sb("o_t", [DH1 + 1, HALF])
        ps_max = [r.ps(f"ps_max{i}", [P, CH]) for i in range(2)]
        ps_s = [r.ps(f"ps_s{i}", [P, HALF]) for i in range(2)]
        ps_o = r.ps("ps_o", [P, HALF])
        o_nat = ps_max[1][:, 0:JT * (DH1 + 1)].rearrange("p (j e) -> p j e", e=DH1 + 1)
        names = ("ones_done stack_in max_in max_mm max_red m_done m_turned m_first m_second m_stored s_mm e_done o_mm o_copied o_turned o_read v_copied own_dve")
        s = {n: r.sem(n) for n in names.split()}
        block = ctx.enter_context(nc.Block())

        def load_stacks(sp, b, h, slot):
            f = h * DH1
            at = bass.ds(b * S, S)
            part = lambda which, p: parts[which, p, bass.ds(f, DH1), at]
            sp.dma_start(k_st[slot][0:DH1, :].bitcast(F32), part(1, 0)).then_inc(s["stack_in"], 16)
            sp.dma_start(k_st[slot][DH1:2 * DH1, :].bitcast(F32), part(1, 1)).then_inc(s["stack_in"], 16)
            sp.dma_start(k_st[slot][2 * DH1:3 * DH1, :].bitcast(F32), part(1, 0)).then_inc(s["stack_in"], 16)
            sp.dma_start(k_st[slot][3 * DH1:3 * DH1 + 2, :].bitcast(F32), mask_parts[:, at]).then_inc(s["stack_in"], 16)
            sp.dma_start(q_st[slot][0:DH1, :].bitcast(F32), part(0, 0)).then_inc(s["stack_in"], 16)
            sp.dma_start(q_st[slot][DH1:2 * DH1, :].bitcast(F32), part(0, 0)).then_inc(s["stack_in"], 16)
            sp.dma_start(q_st[slot][2 * DH1:3 * DH1, :].bitcast(F32), part(0, 1)).then_inc(s["stack_in"], 16)

        NSTACK = 7

        @block.sync
        def _(sp):
            sp.wait_ge(s["ones_done"], 4)

            def max_row(hd, slot):
                sp.wait_ge(s["m_second"], hd + 1)
                sp.dma_start(max_rows[slot].rearrange("a (q j) -> q a j", j=P), m_parts[:, :, :].bitcast(F32)).then_inc(s["m_stored"], 16)
                sp.wait_ge(s["m_stored"], (hd + 1) * 16)
                sp.dma_start(q_st[slot][3 * DH1 + 2:ROWS, :].bitcast(F32), max_rows[slot]).then_inc(s["max_in"], 16)

            def head(b, h, slot, last):
                hd = b * H1 + h
                if not last:
                    sp.wait_ge(s["s_mm"], hd * STEPS)
                    load_stacks(sp, b, h + 1, 1 - slot)
                    max_row(hd + 1, 1 - slot)

            with sp.Fori(0, NB) as b:
                sp.wait_ge(s["s_mm"], b * H1 * STEPS)
                load_stacks(sp, b, 0, 0)
                max_row(b * H1, 0)
                with sp.Fori(0, H1 // 2 - 1) as hp:
                    for j in range(2):
                        head(b, 2 * hp + j, j, False)
                for j in range(2):
                    head(b, H1 - 2 + j, j, j == 1)

        @block.gpsimd
        def _(pool):
            def copy_v(b, h, slot, first=False):
                hd = b * H1 + h
                pool.wait_ge(s["o_mm"], (hd if first else hd - 1) * STEPS)
                nc.gpsimd.tensor_copy(v_h[slot][:, :, :], v_aug[:, bass.ds(b * QT, QT), bass.ds(h, 1), :].rearrange("p t h e -> p t (h e)")
                                      ).then_inc(s["v_copied"], 1)

            with pool.Fori(0, NB) as b:
                copy_v(b, 0, 0, True)
                with pool.Fori(0, H1 // 2 - 1) as hp:
                    copy_v(b, 2 * hp + 1, 1)
                    copy_v(b, 2 * hp + 2, 0)
                copy_v(b, H1 - 1, 1)

        @block.tensor
        def _(pe):
            def max_mm(hd, slot, i, first=False):
                if i == 0:
                    pe.wait_ge(s["stack_in"], (hd + 1) * NSTACK * 16)
                    pe.wait_ge(s["o_read"], (hd if first else hd - 1) * 2)
                    pe.wait_ge(s["m_second"], hd)
                pe.wait_ge(s["max_red"], hd * NMAX + max(i - 1, 0))
                qt, kc = divmod(i, S // CH)
                nc.tensor.matmul(ps_max[i % 2][:, :], q_st[slot][0:ROWS_MAX, qt * P:(qt + 1) * P],
                                 k_st[slot][0:ROWS_MAX, kc * CH:(kc + 1) * CH], start=True, stop=True).then_inc(s["max_mm"], 1)

            def turn_max(hd):
                pe.wait_ge(s["m_done"], hd + 1)
                nc.tensor.transpose(ps_max[0][0:QT, 0:P], m_all[:, :], keep["ident"][:, :]).then_inc(s["m_turned"], 1)

            def score_mm(hd, slot, st):
                half, kt = divmod(st, QT)
                if st == 0:
                    pe.wait_ge(s["max_in"], (hd + 1) * 16)
                pe.wait_ge(s["e_done"], hd * STEPS + max(st - 1, 0))
                for c in range(2):
                    q0 = half * HALF + c * CH
                    mm = nc.tensor.matmul(ps_s[st % 2][:, c * CH:(c + 1) * CH], k_st[slot][0:ROWS, kt * P:(kt + 1) * P],
                                          q_st[slot][0:ROWS, q0:q0 + CH], start=True, stop=True)
                mm.then_inc(s["s_mm"], 1)

            def pv_mm(hd, slot, st):
                half, kt = divmod(st, QT)
                pe.wait_ge(s["e_done"], hd * STEPS + st + 1)
                if st == 0:
                    pe.wait_ge(s["v_copied"], hd + 1)
                if kt == 0:
                    pe.wait_ge(s["o_copied"], hd * 2 + half)
                for c in range(2):
                    mm = nc.tensor.matmul(ps_o[0:DH1 + 1, c * CH:(c + 1) * CH], v_h[slot][:, kt, :],
                                          prob[st % 4][:, c * CH:(c + 1) * CH], start=(kt == 0), stop=(kt == QT - 1))
                mm.then_inc(s["o_mm"], 1)

            def turn_o(hd, half):
                pe.wait_ge(s["o_copied"], hd * 2 + half + 1)
                for j in range(JT):
                    mm = nc.tensor.matmul(o_nat[:, j, :], o_t[:, j * P:(j + 1) * P], keep["ident"][0:DH1 + 1, 0:DH1 + 1],
                                          start=True, stop=True)
                mm.then_inc(s["o_turned"], 1)

            def head(b, h, slot, last):
                hd = b * H1 + h
                for st in range(STEPS):
                    if st + 1 < STEPS:
                        score_mm(hd, slot, st + 1)
                    elif not last:
                        score_mm(hd + 1, 1 - slot, 0)
                    if not last:
                        for i in range(PER_STEP * (st - FIRST_MAX), PER_STEP * (st - FIRST_MAX + 1)):
                            if 0 <= i < NMAX:
                                max_mm(hd + 1, 1 - slot, i)
                        if st == TURN_STEP:
                            turn_max(hd + 1)
                    if st == TURN_STEP + 2:
                        turn_o(hd, 0)
                    pv_mm(hd, slot, st)
                turn_o(hd, 1)

            with pe.Fori(0, NB) as b:
                for i in range(NMAX):
                    max_mm(b * H1, 0, i, True)
                turn_max(b * H1)
                score_mm(b * H1, 0, 0)
                with pe.Fori(0, H1 // 2 - 1) as hp:
                    for j in range(2):
                        head(b, 2 * hp + j, j, False)
                for j in range(2):
                    head(b, H1 - 2 + j, j, j == 1)

        @block.scalar
        def _(act):
            def first_part(hd):
                act.wait_ge(s["m_turned"], hd + 1)
                act.wait_ge(s["m_stored"], hd * 16)
                nc.scalar.activation(m_parts[:, 0, :], ps_max[0][0:QT, 0:P], ACT.Copy, scale=-1.0).then_inc(s["m_first"], 1)

            def head(b, h, last):
                hd = b * H1 + h
                for st in range(STEPS):
                    act.wait_ge(s["s_mm"], hd * STEPS + st + 1)
                    act.wait_ge(s["o_mm"], hd * STEPS + max(st - 3, 0))
                    nc.scalar.activation(prob[st % 4][:, :], ps_s[st % 2][:, :], ACT.Exp).then_inc(s["e_done"], 1)
                    if st == TURN_STEP and not last:
                        first_part(hd + 1)

            with act.Fori(0, NB) as b:
                first_part(b * H1)
                with act.Fori(0, H1 // 2 - 1) as hp:
                    for j in range(2):
                        head(b, 2 * hp + j, False)
                for j in range(2):
                    head(b, H1 - 2 + j, j == 1)

        @block.vector
        def _(dve):
            def reduce(hd, i):
                qt, kc = divmod(i, S // CH)
                dve.wait_ge(s["max_mm"], hd * NMAX + i + 1)
                nc.vector.tensor_reduce(mx[:, qt, kc:kc + 1], ps_max[i % 2][:, :], AX.X, ALU.max).then_inc(s["max_red"], 1)

            def all_max(hd):
                dve.wait_ge(s["max_red"], (hd + 1) * NMAX)
                dve.wait_ge(s["m_turned"], hd)
                nc.vector.tensor_reduce(m_all[:, :], mx[:, :, :], AX.X, ALU.max).then_inc(s["m_done"], 1)

            def second_part(hd):
                dve.wait_ge(s["m_first"], hd + 1)
                nc.vector.scalar_tensor_tensor(out=m_parts[:, 1, :], in0=ps_max[0][0:QT, 0:P], scalar=-1.0,
                                               in1=m_parts[:, 0, :].bitcast(F32), op0=ALU.mult, op1=ALU.subtract
                                               ).then_inc(s["m_second"], 1)

            def copy_o(hd, half):
                dve.wait_ge(s["o_mm"], hd * STEPS + (half + 1) * QT)
                dve.wait_ge(s["o_turned"], hd * 2 + half)
                nc.vector.tensor_copy(o_t[:, :], ps_o[0:DH1 + 1, :]).then_inc(s["o_copied"], 1)

            def normalise(b, h, half):
                hd = b * H1 + h
                dve.wait_ge(s["o_turned"], hd * 2 + half + 1)
                dve.wait_ge(s["o_read"], hd * 2 + half)
                nc.vector.reciprocal(rden[:, :, :], o_nat[:, :, DH1:DH1 + 1]).then_inc(s["own_dve"], 1)
                dve.wait_ge(s["own_dve"], hd * 2 + half + 1)
                nc.vector.tensor_tensor(y[:, bass.ds(b * QT + half * JT, JT), bass.ds(h * DH1, DH1)], o_nat[:, :, 0:DH1],
                                        rden[:, :, :].to_broadcast([P, JT, DH1]), ALU.mult).then_inc(s["o_read"], 1)

            def head(b, h, last):
                hd = b * H1 + h
                for st in range(STEPS):
                    if st == QT:
                        copy_o(hd, 0)
                    if not last:
                        for i in range(PER_STEP * (st - FIRST_MAX), PER_STEP * (st - FIRST_MAX + 1)):
                            if 0 <= i < NMAX:
                                reduce(hd + 1, i)
                            if i == NMAX - 1:
                                all_max(hd + 1)
                    if st == TURN_STEP and not last:
                        second_part(hd + 1)
                    if st == TURN_STEP + 2:
                        normalise(b, h, 0)
                copy_o(hd, 1)
                normalise(b, h, 1)

            for t in range(2):
                nc.vector.memset(q_st[t][3 * DH1:ROWS, :].bitcast(F32), 1.0).then_inc(s["ones_done"], 1)
                nc.vector.memset(k_st[t][3 * DH1:ROWS, :].bitcast(F32), 1.0).then_inc(s["ones_done"], 1)
            with dve.Fori(0, NB) as b:
                for i in range(NMAX):
                    reduce(b * H1, i)
                all_max(b * H1)
                second_part(b * H1)
                with dve.Fori(0, H1 // 2 - 1) as hp:
                    for j in range(2):
                        head(b, 2 * hp + j, False)
                for j in range(2):
                    head(b, H1 - 2 + j, j == 1)


def stage_out(nc, a, keep, film, w_name, b_name, y, src, out):
    with ExitStack() as ctx:
        r = Room(nc, ctx, f"out{film}")
        m = Norm(r, keep)
        w = r.sb("w", [P, KD, D])
        bias = r.sb("bias", [P, D])
        x_res = r.sb("x_res", [P, 4, D])
        bank = [r.ps(f"bank{i}", [P, CH]) for i in range(4)]
        names = "weights_in residual_in o_mm biased out_done stored own_dve"
        s = {n: r.sem(n) for n in names.split()}
        fa, fb = keep["film"][:, film, 0], keep["film"][:, film, 1]
        block = ctx.enter_context(nc.Block())

        @block.sync
        def _(sp):
            sp.dma_start(w[:, :, :], a[w_name].rearrange("(k p) n -> p k n", p=P)).then_inc(s["weights_in"], 16)
            sp.dma_start(bias[:, :], row_on_all(a[b_name])).then_inc(s["weights_in"], 16)
            with sp.Fori(0, NCH) as it:
                sp.wait_ge(s["stored"], it * 16 * TT)
                sp.dma_start(x_res[:, :, :], src[bass.ds(it * CH, CH), :].rearrange("(t p) d -> p t d", p=P)).then_inc(s["residual_in"], 16)
                for t in range(TT):
                    sp.wait_ge(s["out_done"], it * TT + t + 1)
                    sp.dma_start(out[bass.ds(it * CH + t * P, P), :], x_res[:, t, :]).then_inc(s["stored"], 16)
            sp.wait_ge(s["stored"], NCH * TT * 16)

        @block.gpsimd
        def _(pool):
            with pool.Fori(0, NCH) as it:
                norm_pool(nc, pool, m, it)

        @block.tensor
        def _(pe):
            pe.wait_ge(s["weights_in"], 32)
            with pe.Fori(0, NCH) as it:
                norm_pe(nc, pe, m, it)
                pe.wait_ge(m.turned, (it + 1) * KD)
                for t in range(TT):
                    pe.wait_ge(s["out_done"], it * TT)
                    for k in range(KD):
                        mm = nc.tensor.matmul(bank[t][:, :], m.xn_t[:, k, t * P:(t + 1) * P], w[:, k, :],
                                              start=(k == 0), stop=(k == KD - 1))
                    mm.then_inc(s["o_mm"], 1)

        @block.scalar
        def _(act):
            with act.Fori(0, NB) as b, act.Fori(0, NC_B) as c:
                it = b * NC_B + c
                act.wait_ge(s["o_mm"], it * TT)
                norm_act(nc, act, m, it, ACT.Silu, lambda k: fa[:, k, bass.ds(b, 1)], lambda k: fb[:, k, bass.ds(b, 1)])

        @block.vector
        def _(dve):
            dve.wait_ge(s["weights_in"], 32)
            with dve.Fori(0, NCH) as it:
                own = Chain(dve, s["own_dve"], it, DVE_NORM)
                norm_dve(nc, dve, m, own, it, lambda t: y[:, bass.ds(it * TT + t, 1), :].rearrange("p a d -> p (a d)"))
                for t in range(TT):
                    dve.wait_ge(s["o_mm"], it * TT + t + 1)
                    nc.vector.tensor_tensor(bank[t][:, :], bank[t][:, :], bias[:, :], ALU.add).then_inc(s["biased"], 1)
                    dve.wait_ge(s["biased"], it * TT + t + 1)
                    dve.wait_ge(s["residual_in"], (it + 1) * 16)
                    nc.vector.tensor_tensor(x_res[:, t, :], bank[t][:, :], x_res[:, t, :], ALU.add).then_inc(s["out_done"], 1)
                own.end()



def stage_linear(nc, a, keep, layer, heads, names_of, int_mask, over_v, src, out):
    with ExitStack() as ctx:
        r = Room(nc, ctx, f"lin{layer}")
        dh = D // heads
        ident = keep["ident"]
        tb = [r.ps(f"turn_bank{i}", [P, CH]) for i in range(4)]
        mb = [r.ps(f"mm_bank{i}", [P, CH]) for i in range(4)]
        m1 = Norm(r, keep, tb)
        m2 = Norm(Room(nc, ctx, f"lin{layer}_out"), keep, tb)
        w = [r.sb(f"w_{n}", [P, KD, D]) for n in ("q", "k", "v", "out")]
        rows = r.sb("bias_rows", [P, 3, D])
        k_t = r.sb("k_t", [P, KD, S])
        q_t = r.sb("q_t", [P, KD, S])
        v_all = r.sb("v_all", [P, QT, D])
        q = r.sb("q", [P, TT, D])
        q_red = r.sb("q_red", [P, TT * heads])
        q_den = r.sb("q_den", [P, TT * heads])
        vb = r.sb("vb", [P, 2, D])
        mask_row = r.sb("mask_row", [P, CH], I32 if int_mask else F32)
        mask_add = r.sb("mask_add", [P, CH])
        mask_in = r.sb("mask_in", [P, NT], I32 if int_mask else F32)
        mask_col = r.sb("mask_col", [P, NT])
        k_max = r.sb("k_max", [P, KD])
        k_sum = r.sb("k_sum", [P, KD])
        k_rec = r.sb("k_rec", [P, KD])
        kn = r.sb("kn", [P, 4, D])
        blocks = r.sb("blocks", [P, P])
        kv = r.sb("kv", [P, KD, P])
        x_res = r.sb("x_res", [P, TT, D])
        names = ("weights_in small_in blocks_set mask_set q_mm q_biased q_max q_exp q_done q_turned qt_done k_mm k_done v_mm "
                 "v_biased v_done mask_loaded mask_made kmax_done kexp_done k_scaled k_turned kn_act kn_dve kv_mm kv_done y_mm "
                 "o_mm biased out_done residual_in stored own_dve own2_dve")
        s = {n: r.sem(n) for n in names.split()}
        cols = keep["cols"]
        g, bvec, k_bias = (column(cols, names_of[n]) for n in ("norm_w", "norm_b", "bk"))
        fa, fb = keep["film"][:, layer, 0], keep["film"][:, layer, 1]
        mask_name = "mask_BxS_ik0" if int_mask else "mask_BxSx1_fk1"
        mask_flat = a[mask_name].rearrange("b s -> (b s)") if int_mask else a[mask_name].rearrange("b s o -> (b s o)")
        block = ctx.enter_context(nc.Block())

        @block.sync
        def _(sp):
            for i, n in enumerate(("Wq", "Wk", "Wv", "Wo")):
                sp.dma_start(w[i][:, :, :], a[names_of[n]].rearrange("(k p) n -> p k n", p=P)).then_inc(s["weights_in"], 16)
            with sp.Fori(0, NB) as b:
                with sp.Fori(0, NC_B) as c:
                    it = b * NC_B + c
                    norm_load(sp, m1, src, it)
                    sp.wait_ge(s["weights_in"], 64)
                    sp.wait_ge(s["mask_made"], it)
                    sp.dma_start(mask_row[:, :], row_on_all(mask_flat[bass.ds(it * CH, CH)])).then_inc(s["mask_loaded"], 16)
                for c in range(NC_B):
                    it = b * NC_B + c
                    sp.wait_ge(s["stored"], it * 16)
                    sp.dma_start(x_res[:, :, :], src[bass.ds(it * CH, CH), :].rearrange("(t p) d -> p t d", p=P)).then_inc(s["residual_in"], 16)
                    sp.wait_ge(s["out_done"], (it + 1) * TT)
                    sp.dma_start(out[bass.ds(it * CH, CH), :].rearrange("(t p) d -> p t d", p=P), x_res[:, :, :]).then_inc(s["stored"], 16)
            sp.wait_ge(s["stored"], NCH * 16)

        @block.gpsimd
        def _(pool):
            nc.gpsimd.memset(blocks[:, :], 0.0).then_inc(s["blocks_set"], 1)
            pool.wait_ge(s["blocks_set"], 1)
            for i in range(P // dh):
                nc.gpsimd.memset(blocks[i * dh:(i + 1) * dh, i * dh:(i + 1) * dh], 1.0).then_inc(s["blocks_set"], 1)
            with pool.Fori(0, NB) as b:
                with pool.Fori(0, NC_B) as c:
                    norm_pool(nc, pool, m1, b * NC_B + c)
                with pool.Fori(0, NC_B) as c:
                    norm_pool(nc, pool, m2, b * NC_B + c)

        @block.tensor
        def _(pe):
            pe.wait_ge(s["weights_in"], 64)
            with pe.Fori(0, NB) as b:
                with pe.Fori(0, NC_B) as c:
                    it = b * NC_B + c
                    pe.wait_ge(s["out_done"], b * NC_B * TT)
                    pe.wait_ge(s["qt_done"], it * KD)
                    norm_pe(nc, pe, m1, it)
                    pe.wait_ge(m1.turned, (it + 1) * KD)
                    for which, used, made, read in ((0, (0, 1), "q_mm", "q_biased"), (2, (2, 3), "v_mm", "v_biased")):
                        for t in range(TT):
                            pe.wait_ge(s[read], it * TT + max(t - 1, 0))
                            if which == 0 and t < 2:
                                pe.wait_ge(s["k_done"], it * KD)
                            for k in range(KD):
                                mm = nc.tensor.matmul(mb[used[t % 2]][:, :], m1.xn_t[:, k, t * P:(t + 1) * P], w[which][:, k, :],
                                                      start=(k == 0), stop=(k == KD - 1))
                            mm.then_inc(s[made], 1)
                    for mt in range(KD):
                        if mt == 0:
                            pe.wait_ge(s["q_biased"], (it + 1) * TT)
                        pe.wait_ge(s["k_done"], it * KD + max(mt - 1, 0))
                        for k in range(KD):
                            mm = nc.tensor.matmul(mb[mt % 2][:, :], w[1][:, k, mt * P:(mt + 1) * P], m1.xn_t[:, k, :],
                                                  start=(k == 0), stop=(k == KD - 1))
                        mm.then_inc(s["k_mm"], 1)
                    pe.wait_ge(s["q_done"], it + 1)
                    for k in range(KD):
                        for t in range(TT):
                            mm = nc.tensor.transpose(tb[k][:, t * P:(t + 1) * P], q[:, t, k * P:(k + 1) * P], ident[:, :])
                        mm.then_inc(s["q_turned"], 1)
                pe.wait_ge(s["qt_done"], (b + 1) * NC_B * KD)
                pe.wait_ge(s["k_done"], (b + 1) * NC_B * KD)
                pe.wait_ge(s["v_done"], (b + 1) * QT)
                pe.wait_ge(s["kexp_done"], (b + 1) * KD)
                if over_v:
                    pe.wait_ge(s["k_scaled"], (b + 1) * KD)

                def turn_k(tt):
                    if tt >= 4:
                        pe.wait_ge(s["kn_dve" if tt % 2 else "kn_act"], b * (QT // 2) + tt // 2 - 1)
                    for mt in range(KD):
                        mm = nc.tensor.transpose(tb[tt % 4][:, mt * P:(mt + 1) * P], k_t[:, mt, tt * P:(tt + 1) * P], ident[:, :])
                    mm.then_inc(s["k_turned"], 1)

                turn_k(0)
                turn_k(1)
                for tt in range(QT):
                    if tt + 2 < QT:
                        turn_k(tt + 2)
                    pe.wait_ge(s["kn_dve" if tt % 2 else "kn_act"], b * (QT // 2) + tt // 2 + 1)
                    for mt in range(KD):
                        k_part = kn[:, tt % 4, mt * P:(mt + 1) * P]
                        v_part = v_all[:, tt, mt * P:(mt + 1) * P]
                        mm = nc.tensor.matmul(mb[0][:, mt * P:(mt + 1) * P], v_part if over_v else k_part,
                                              k_part if over_v else v_part, start=(tt == 0 and mt == 0),
                                              stop=(tt == QT - 1), skip_group_check=True)
                    mm.then_inc(s["kv_mm"], 1)
                pe.wait_ge(s["kv_done"], (b + 1) * KD)
                for c in range(NC_B):
                    it = b * NC_B + c
                    pe.wait_ge(s["out_done"], it * TT)
                    for t in range(TT):
                        for mt in range(KD):
                            mm = nc.tensor.matmul(mb[t][:, mt * P:(mt + 1) * P], q_t[:, mt, c * CH + t * P:c * CH + (t + 1) * P],
                                                  kv[:, mt, :], start=True, stop=True)
                        mm.then_inc(s["y_mm"], 1)
                    norm_pe(nc, pe, m2, it)
                    pe.wait_ge(m2.turned, (it + 1) * KD)
                    for t in range(TT):
                        for k in range(KD):
                            mm = nc.tensor.matmul(mb[t][:, :], m2.xn_t[:, k, t * P:(t + 1) * P], w[3][:, k, :],
                                                  start=(k == 0), stop=(k == KD - 1))
                        mm.then_inc(s["o_mm"], 1)

        @block.scalar
        def _(act):
            act.dma_start(mask_in[:, :], a["mask_ik0_columns" if int_mask else "mask_fk1_columns"]).then_inc(s["small_in"], 16)
            for i, n in enumerate(("bq", "bv", "bo")):
                act.dma_start(rows[:, i, :], row_on_all(a[names_of[n]])).then_inc(s["small_in"], 16)
            act.wait_ge(s["mask_set"], 1)
            with act.Fori(0, NB) as b:
                with act.Fori(0, NC_B) as c:
                    it = b * NC_B + c
                    act.wait_ge(s["k_mm"], it * KD)
                    norm_act(nc, act, m1, it, ACT.Identity, lambda k: g[:, k:k + 1], lambda k: bvec[:, k:k + 1])
                    act.wait_ge(s["q_max"], it + 1)
                    nc.scalar.activation(q[:, :, :], q[:, :, :], ACT.Exp).then_inc(s["q_exp"], 1)
                    act.wait_ge(s["kv_mm"], b * QT)
                    for t in range(TT):
                        act.wait_ge(s["v_biased"], it * TT + t + 1)
                        nc.scalar.activation(v_all[:, bass.ds(c * TT + t, 1), :].rearrange("p a d -> p (a d)"), vb[:, t % 2, :], ACT.Copy,
                                             scale=mask_col[:, bass.ds(it * TT + t, 1)]).then_inc(s["v_done"], 1)
                    for k in range(KD):
                        act.wait_ge(s["q_turned"], it * KD + k + 1)
                        nc.scalar.activation(q_t[:, k, bass.ds(c * CH, CH)], tb[k][:, :], ACT.Copy).then_inc(s["qt_done"], 1)
                for mt in range(KD):
                    act.wait_ge(s["kmax_done"], b * KD + mt + 1)
                    nc.scalar.activation(k_t[:, mt, :], k_t[:, mt, :], ACT.Exp, bias=k_max[:, mt:mt + 1],
                                         accum_out=k_sum[:, mt:mt + 1]).then_inc(s["kexp_done"], 1)
                for tt in range(0, QT, 2):
                    act.wait_ge(s["k_turned"], b * QT + tt + 1)
                    if tt >= 4:
                        act.wait_ge(s["kv_mm"], b * QT + tt - 3)
                    nc.scalar.activation(kn[:, tt % 4, :], tb[tt % 4][:, :], ACT.Copy).then_inc(s["kn_act"], 1)
                with act.Fori(0, NC_B) as c:
                    it = b * NC_B + c
                    act.wait_ge(s["o_mm"], it * TT)
                    norm_act(nc, act, m2, it, ACT.Silu, lambda k: fa[:, k, bass.ds(b, 1)], lambda k: fb[:, k, bass.ds(b, 1)])

        @block.vector
        def _(dve):
            dve.wait_ge(s["small_in"], 64)
            if int_mask:
                nc.vector.tensor_scalar(mask_col[:, :], mask_in[:, :], 1.0, None, ALU.not_equal).then_inc(s["mask_set"], 1)
            else:
                nc.vector.tensor_copy(mask_col[:, :], mask_in[:, :]).then_inc(s["mask_set"], 1)
            dve.wait_ge(s["blocks_set"], 1 + P // dh)
            with dve.Fori(0, NB) as b:
                with dve.Fori(0, NC_B) as c:
                    it = b * NC_B + c
                    own = Chain(dve, s["own_dve"], it, DVE_NORM + 3)
                    dve.wait_ge(m1.x_loaded, (it + 1) * 16)
                    norm_dve(nc, dve, m1, own, it, lambda t: m1.x[:, t, :])
                    dve.wait_ge(s["mask_loaded"], (it + 1) * 16)
                    dve.wait_ge(s["k_done"], it * KD)
                    if int_mask:
                        nc.vector.tensor_scalar(mask_add[:, :], mask_row[:, :], 1.0, -3.0e38, ALU.is_equal, ALU.mult).then_inc(s["mask_made"], 1)
                    else:
                        nc.vector.tensor_scalar(mask_add[:, :], mask_row[:, :], 1e6, -1e6, ALU.mult, ALU.add).then_inc(s["mask_made"], 1)
                    dve.wait_ge(s["q_turned"], it * KD)
                    for t in range(TT):
                        dve.wait_ge(s["q_mm"], it * TT + t + 1)
                        nc.vector.tensor_tensor(q[:, t, :], mb[t % 2][:, :], rows[:, 0, :], ALU.add).then_inc(s["q_biased"], 1)
                    heads_view = q[:, :, :].rearrange("p t (h e) -> p (t h) e", e=dh)
                    wide = lambda v: v[:, :].unsqueeze(2).to_broadcast([P, TT * heads, dh])
                    dve.wait_ge(s["q_biased"], (it + 1) * TT)
                    own.inc(nc.vector.tensor_reduce(q_red[:, :], heads_view, AX.X, ALU.max))
                    own.wait()
                    nc.vector.tensor_tensor(heads_view, heads_view, wide(q_red), ALU.subtract).then_inc(s["q_max"], 1)
                    for t in range(TT):
                        dve.wait_ge(s["v_mm"], it * TT + t + 1)
                        dve.wait_ge(s["v_done"], it * TT + max(t - 1, 0))
                        nc.vector.tensor_tensor(vb[:, t % 2, :], mb[2 + t % 2][:, :], rows[:, 1, :], ALU.add).then_inc(s["v_biased"], 1)
                        if t == 1:
                            dve.wait_ge(s["q_exp"], it + 1)
                            own.inc(nc.vector.tensor_reduce(q_den[:, :], heads_view, AX.X, ALU.add))
                            own.wait()
                            own.inc(nc.vector.reciprocal(q_den[:, :], q_den[:, :]))
                            own.wait()
                            nc.vector.tensor_tensor(heads_view, heads_view, wide(q_den), ALU.mult).then_inc(s["q_done"], 1)
                    dve.wait_ge(s["mask_made"], it + 1)
                    for mt in range(KD):
                        dve.wait_ge(s["k_mm"], it * KD + mt + 1)
                        nc.vector.scalar_tensor_tensor(out=k_t[:, mt, bass.ds(c * CH, CH)], in0=mb[mt % 2][:, :], scalar=k_bias[:, mt:mt + 1],
                                                       in1=mask_add[:, :], op0=ALU.add, op1=ALU.add).then_inc(s["k_done"], 1)
                    own.end()
                own = Chain(dve, s["own2_dve"], b, KD + 1 + 2 * NC_B)
                dve.wait_ge(s["k_done"], (b + 1) * NC_B * KD)
                for mt in range(KD):
                    own.inc(nc.vector.tensor_reduce(k_max[:, mt:mt + 1], k_t[:, mt, :], AX.X, ALU.max))
                    own.wait()
                    nc.vector.tensor_scalar(k_max[:, mt:mt + 1], k_max[:, mt:mt + 1], -1.0, None, ALU.mult).then_inc(s["kmax_done"], 1)
                dve.wait_ge(s["kexp_done"], (b + 1) * KD)
                own.inc(nc.vector.reciprocal(k_rec[:, :], k_sum[:, :]))
                own.wait()
                for mt in range(KD if over_v else 0):
                    nc.vector.tensor_scalar(k_t[:, mt, :], k_t[:, mt, :], k_rec[:, mt:mt + 1], None, ALU.mult).then_inc(s["k_scaled"], 1)
                for tt in range(1, QT, 2):
                    dve.wait_ge(s["k_turned"], b * QT + tt + 1)
                    if tt >= 4:
                        dve.wait_ge(s["kv_mm"], b * QT + tt - 3)
                    nc.vector.tensor_copy(kn[:, tt % 4, :], tb[tt % 4][:, :]).then_inc(s["kn_dve"], 1)
                dve.wait_ge(s["kv_mm"], (b + 1) * QT)
                own.wait()
                for mt in range(KD):
                    nc.vector.scalar_tensor_tensor(out=kv[:, mt, :], in0=mb[0][:, mt * P:(mt + 1) * P],
                                                   scalar=1.0 if over_v else k_rec[:, mt:mt + 1],
                                                   in1=blocks[:, :], op0=ALU.mult, op1=ALU.mult).then_inc(s["kv_done"], 1)
                for c in range(NC_B):
                    it = b * NC_B + c
                    dve.wait_ge(s["y_mm"], (it + 1) * TT)
                    norm_dve(nc, dve, m2, own, it, lambda t: mb[t][:, :])
                    for t in range(TT):
                        dve.wait_ge(s["o_mm"], it * TT + t + 1)
                        nc.vector.tensor_tensor(mb[t][:, :], mb[t][:, :], rows[:, 2, :], ALU.add).then_inc(s["biased"], 1)
                        dve.wait_ge(s["biased"], it * TT + t + 1)
                        dve.wait_ge(s["residual_in"], (it + 1) * 16)
                        nc.vector.tensor_tensor(x_res[:, t, :], mb[t][:, :], x_res[:, t, :], ALU.add).then_inc(s["out_done"], 1)
                own.end()


NAMES2 = {"norm_w": "L2_cond_norm_scale", "norm_b": "L2_cond_norm_bias", "Wq": "L2_cond_Wq", "Wk": "L2_cond_Wk", "Wv": "L2_cond_Wv",
          "Wo": "L2_cond_film_out_W", "bq": "L2_cond_bq", "bk": "L2_cond_bk", "bv": "L2_cond_bv", "bo": "L2_cond_film_out_b"}
NAMES3 = {"norm_w": "L3_cond_ln_w", "norm_b": "L3_cond_ln_b", "Wq": "L3_cond_Wq", "Wk": "L3_cond_Wk", "Wv": "L3_cond_Wv",
          "Wo": "L3_cond_W_out", "bq": "L3_cond_bq", "bk": "L3_cond_bk", "bv": "L3_cond_bv", "bo": "L3_cond_b_out"}


def build(nc, a, out):
    with ExitStack() as ctx:
        def sb(name, shape):
            return ctx.enter_context(nc.sbuf_tensor(name, shape, F32))

        def dram(name, shape):
            return nc.dram_tensor(name, shape, F32, kind="Internal").ap()

        keep = {"cols": sb("cols", [P, NCOLS]),
                "film": sb("film", [P, NB * 2, 2, KD, NB]),
                "gate": sb("gate", [P, NB, D]),
                "ident": sb("ident", [P, P]),
                "neg_half": sb("neg_half", [P, TT])}
        x1, x2, x3 = (dram(f"x_after_L{i}", [NB * S, D]) for i in range(3))
        qk_parts = dram("qk_parts", [2, 2, D, NB * S])
        mask_parts = dram("mask_parts", [2, NB * S])
        max_rows = dram("max_rows", [2, 2, S])
        stage_condition(nc, a, keep)
        stage_mamba(nc, a, keep, x1)
        with ExitStack() as for_y:
            y = for_y.enter_context(nc.sbuf_tensor("y", [P, NT, D], F32))
            with ExitStack() as for_v:
                v_aug = for_v.enter_context(nc.sbuf_tensor("v_aug", [P, NT, H1, DH1 + 1], F32))
                stage_qkv(nc, a, keep, x1, qk_parts, mask_parts, v_aug)
                stage_attention(nc, a, keep, qk_parts, mask_parts, max_rows, v_aug, y)
            stage_out(nc, a, keep, 1, "L1_cond_out_w", "L1_cond_out_b", y, x1, x2)
        stage_linear(nc, a, keep, 2, 16, NAMES2, True, True, x2, x3)
        stage_linear(nc, a, keep, 3, 8, NAMES3, False, False, x3, out.rearrange("b s d -> (b s) d"))


def kernel(**inputs):
    import numpy as np
    import concourse.bacc as bacc
    from concourse.bass_utils import run_bass_kernel_spmd

    def as_columns(v):
        v = np.asarray(v)
        return np.ascontiguousarray(v.reshape(-1, P, *v.shape[1:]).swapaxes(0, 1).reshape(P, -1))

    sent = {name: np.asarray(v) for name, v in inputs.items()}
    sent["cond_T"] = sent.pop("cond_2048").T
    sent["ada_w_T"] = sent.pop("L0_cond_ada_w").T
    for name in ("in_proj_w", "x_proj_w", "dt_proj_w", "out_proj_w"):
        sent[f"{name}_T"] = sent.pop(f"L0_cond_{name}").T
    sent["columns"] = np.concatenate([as_columns(sent[name]) for name, _ in COLUMNS], axis=1)
    for name, _ in COLUMNS:
        if name != "L0_cond_ada_b":
            del sent[name]
    sent["mask_ff1_columns"] = as_columns(sent["mask_BxS_ff1"].reshape(-1))
    sent["mask_ik0_columns"] = as_columns(sent["mask_BxS_ik0"].reshape(-1))
    sent["mask_fk1_columns"] = as_columns(sent["mask_BxSx1_fk1"].reshape(-1))

    nc = bacc.Bacc("TRN2", target_bir_lowering=False, num_devices=1)
    arrays, a = {}, {}
    for name, v in sent.items():
        v = np.ascontiguousarray(v)
        arrays[f"in_{name}"] = v
        a[name] = nc.dram_tensor(f"in_{name}", v.shape, mybir.dt.from_np(v.dtype), kind="ExternalInput").ap()
    out = nc.dram_tensor("out", (NB, S, D), F32, kind="ExternalOutput").ap()
    build(nc, a, out)
    r = run_bass_kernel_spmd(nc, [arrays], core_ids=[0])
    return r.results[0]["out"]
```

```python
from contextlib import ExitStack

import concourse.bass as bass
from concourse import mybir

F32 = mybir.dt.float32
F32R = mybir.dt.float32r
I32 = mybir.dt.int32
ACT = mybir.ActivationFunctionType
ALU = mybir.AluOpType
AX = mybir.AxisListType

P = 128
NB = 2
S = 2048
D = 512
KD = D // P
CH = 512
NC_B = S // CH
NCH = NB * NC_B
TT = CH // P
DI = 1024
CT = DI // P
N = 16
RANK = 64
CONV = 4
CW = 1024
KC = CW // P
EPS = 1e-5


class Chain:

    def __init__(self, engine, sem, base, per):
        self.engine, self.sem, self.base, self.per, self.n = engine, sem, base, per, 0

    def inc(self, ins):
        ins.then_inc(self.sem, 1)
        self.n += 1

    def wait(self):
        self.engine.wait_ge(self.sem, self.base * self.per + self.n)

    def end(self):
        assert self.n == self.per, (self.sem, self.n, self.per)


class Room:

    def __init__(self, nc, ctx, stage):
        self.nc, self.ctx, self.stage, self.sems = nc, ctx, stage, []
        ctx.callback(self.close)

    def sb(self, name, shape, dt=F32):
        return self.ctx.enter_context(self.nc.sbuf_tensor(f"{self.stage}_{name}", shape, dt))

    def ps(self, name, shape, dt=F32):
        return self.ctx.enter_context(self.nc.psum_tensor(f"{self.stage}_{name}", shape, dt))

    def sem(self, name):
        self.sems.append(self.nc.alloc_semaphore(f"{self.stage}_{name}"))
        return self.sems[-1]

    def close(self):
        self.nc.clear_and_free_semaphores(self.sems)
        self.nc.all_engine_barrier()


COLUMNS = [("L0_cond_ln_g", KD), ("L0_cond_ln_b", KD), ("L0_cond_ada_b", 3 * KD), ("L0_cond_conv_b", CT),
           ("L0_cond_dt_proj_b", CT), ("L0_cond_D_param", CT), ("L0_cond_conv_w", CT * CONV), ("L0_cond_A_log", CT * N),
           ("L1_cond_norm_w", KD), ("L1_cond_norm_b", KD), ("L1_cond_q_b", KD), ("L1_cond_k_b", KD),
           ("L1_cond_emb_b", 2 * KD), ("L1_cond_sb_norm_w", KD), ("L1_cond_sb_norm_b", KD),
           ("L2_cond_norm_scale", KD), ("L2_cond_norm_bias", KD), ("L2_cond_bk", KD),
           ("L2_cond_film_emb_b", 2 * KD), ("L2_cond_film_norm_scale", KD), ("L2_cond_film_norm_bias", KD),
           ("L3_cond_ln_w", KD), ("L3_cond_ln_b", KD), ("L3_cond_bk", KD),
           ("L3_cond_b_emb", 2 * KD), ("L3_cond_ln2_w", KD), ("L3_cond_ln2_b", KD)]
NCOLS = sum(w for _, w in COLUMNS)


def column(cols, name, first=0, count=None):
    at = 0
    for other, width in COLUMNS:
        if other == name:
            return cols[:, at + first:at + (width if count is None else first + count)]
        at += width
    raise KeyError(name)


def row_on_all(vec, parts=P):
    return bass.AP(tensor=vec.tensor, offset=vec.offset, ap=[[0, parts], [1, vec.shape[0]]])


def make_identity(pool, ident, done):
    pool.memset(ident[:, :], 0.0).then_inc(done, 1)
    pool.wait_ge(done, 1)
    pool.affine_select(out=ident[:, :], in_=ident[:, :], compare_op=ALU.not_equal, fill=1.0, base=0,
                       pattern=[[-1, P]], channel_multiplier=1).then_inc(done, 1)


def stage_condition(nc, a, keep):
    with ExitStack() as ctx:
        r = Room(nc, ctx, "cond")
        films = [("L1", a["L1_cond_emb_w"], "L1_cond_emb_b", "L1_cond_sb_norm_w", "L1_cond_sb_norm_b"),
                 ("L2", a["L2_cond_film_emb_W"], "L2_cond_film_emb_b", "L2_cond_film_norm_scale", "L2_cond_film_norm_bias"),
                 ("L3", a["L3_cond_W_emb"], "L3_cond_b_emb", "L3_cond_ln2_w", "L3_cond_ln2_b")]
        cond = r.sb("cond", [P, KC, NB])
        silu = r.sb("silu", [P, KC, NB])
        ada_w = r.sb("ada_w", [P, KC, 3 * D])
        film_w = r.sb("film_w", [P, KC, 2 * D])
        gate_b = r.sb("gate_b", [P, D])
        cols = keep["cols"]
        proj = r.sb("proj", [P, 4, 2, KD, NB])
        ps_col = [r.ps(f"ps_col{i}", [P, 2 * KD, NB]) for i in range(2)]
        ps_gate = [r.ps(f"ps_gate{i}", [P, D]) for i in range(NB)]
        cond_in, ada_in, film_in, small_in = (r.sem(x) for x in ("cond_in", "ada_in", "film_in", "small_in"))
        silu_done, cols_done, gate_done = (r.sem(x) for x in ("silu_done", "cols_done", "gate_done"))
        bias_done, fold_done = (r.sem(x) for x in ("bias_done", "fold_done"))
        block = ctx.enter_context(nc.Block())

        @block.sync
        def _(sp):
            sp.dma_start(cond[:, :, :], a["cond_T"].rearrange("(k p) b -> p k b", p=P)).then_inc(cond_in, 16)
            sp.dma_start(ada_w[:, :, :], a["ada_w_T"].rearrange("(k p) n -> p k n", p=P)).then_inc(ada_in, 16)
            for i, film in enumerate(films):
                if i:
                    sp.wait_ge(cols_done, i + 1)
                sp.dma_start(film_w[:, :, :], film[1].rearrange("(k p) n -> p k n", p=P)).then_inc(film_in, 16)

        @block.scalar
        def _(act):
            act.dma_start(cols[:, :], a["columns"]).then_inc(small_in, 16)
            act.dma_start(gate_b[:, :], row_on_all(a["L0_cond_ada_b"][2 * D:3 * D])).then_inc(small_in, 16)
            act.wait_ge(cond_in, 16)
            nc.scalar.activation(silu[:, :, :], cond[:, :, :], ACT.Silu).then_inc(silu_done, 1)

        @block.tensor
        def _(pe):
            pe.wait_ge(silu_done, 1)
            for i in range(4):
                if i == 0:
                    pe.wait_ge(ada_in, 16)
                else:
                    pe.wait_ge(film_in, 16 * i)
                if i >= 2:
                    pe.wait_ge(bias_done, 2 * (i - 1))
                w = ada_w if i == 0 else film_w
                for t in range(2 * KD):
                    for k in range(KC):
                        mm = nc.tensor.matmul(ps_col[i % 2][:, t, :], w[:, k, t * P:(t + 1) * P], silu[:, k, :],
                                              start=(k == 0), stop=(k == KC - 1))
                mm.then_inc(cols_done, 1)
                if i == 0:
                    for b in range(NB):
                        for k in range(KC):
                            mm = nc.tensor.matmul(ps_gate[b][:, :], silu[:, k, b:b + 1].to_broadcast([P, P]),
                                                  ada_w[:, k, 2 * D:3 * D], start=(k == 0), stop=(k == KC - 1))
                    mm.then_inc(gate_done, 1)

        @block.vector
        def _(dve):
            dve.wait_ge(small_in, 16 * 2)
            for i in range(4):
                dve.wait_ge(cols_done, i + 1)
                bias = column(cols, "L0_cond_ada_b" if i == 0 else films[i - 1][2], 0, 2 * KD)
                for part in range(2):
                    slot = (1 - part) if i == 0 else part
                    nc.vector.tensor_tensor(
                        proj[:, i, slot, :, :], ps_col[i % 2][:, part * KD:(part + 1) * KD, :],
                        bias[:, part * KD:(part + 1) * KD].unsqueeze(2).to_broadcast([P, KD, NB]), ALU.add
                    ).then_inc(bias_done, 1)
                dve.wait_ge(bias_done, 2 * (i + 1))
                w, nb = (column(cols, v).unsqueeze(2).to_broadcast([P, KD, NB])
                         for v in (("L0_cond_ln_g", "L0_cond_ln_b") if i == 0 else films[i - 1][3:]))
                col = keep["film"]
                nc.vector.tensor_scalar(proj[:, i, 0, :, :], proj[:, i, 0, :, :], 1.0, None, ALU.add).then_inc(fold_done, 1)
                dve.wait_ge(fold_done, 3 * i + 1)
                nc.vector.tensor_tensor(col[:, i, 0, :, :], proj[:, i, 0, :, :], w, ALU.mult)
                nc.vector.tensor_tensor(col[:, i, 1, :, :], proj[:, i, 0, :, :], nb, ALU.mult).then_inc(fold_done, 1)
                dve.wait_ge(fold_done, 3 * i + 2)
                nc.vector.tensor_tensor(col[:, i, 1, :, :], col[:, i, 1, :, :], proj[:, i, 1, :, :], ALU.add).then_inc(fold_done, 1)
                if i == 0:
                    dve.wait_ge(gate_done, 1)
                    for b in range(NB):
                        nc.vector.tensor_tensor(keep["gate"][:, b, :], ps_gate[b][:, :], gate_b[:, :], ALU.add)
            dve.wait_ge(fold_done, 12)

        @block.gpsimd
        def _(pool):
            make_identity(pool, keep["ident"], r.sem("ident_done"))
            nc.gpsimd.memset(keep["neg_half"][:, :], -0.5)


def stage_mamba(nc, a, keep, out):
    with ExitStack() as ctx:
        r = Room(nc, ctx, "mamba")
        G = 2
        NG = N // G
        BC_ROWS = 2 * N
        w_in = r.sb("w_in", [P, KD, 2 * DI])
        w_out = r.sb("w_out", [P, CT, D])
        w_x = r.sb("w_x", [P, CT, RANK + BC_ROWS])
        w_dt = r.sb("w_dt", [RANK, DI])
        cols = keep["cols"]
        conv_w = column(cols, "L0_cond_conv_w").rearrange("p (t j) -> p t j", j=CONV)
        conv_b = column(cols, "L0_cond_conv_b")
        dt_b = column(cols, "L0_cond_dt_proj_b")
        d_par = column(cols, "L0_cond_D_param")
        a_log = column(cols, "L0_cond_A_log").rearrange("p (t n) -> p t n", n=N)
        a_exp = r.sb("a_exp", [P, CT, N])
        a_neg = r.sb("a_neg", [P, CT, N])
        pick = r.sb("pick", [2 * BC_ROWS, BC_ROWS], F32R)
        shared = r.sb("shared", [P, 8 * CH])
        x_in = shared[:, 0:TT * D].rearrange("p (t d) -> p t d", t=TT)
        xn_t = shared[:, TT * D:2 * TT * D].rearrange("p (k s) -> p k s", k=KD)
        hc = shared[:, :].rearrange("p (r g s) -> p r g s", r=4, g=G)
        x_ext = r.sb("x_ext", [P, 2, CONV - 1 + CH])
        halo = r.sb("halo", [P, CT, CONV - 1])
        u = r.sb("u", [P, CT, CH])
        zy = r.sb("zy", [P, CT, CH])
        dt_r = r.sb("dt_r", [RANK, CH])
        bc_parts = r.sb("bc_parts", [2 * BC_ROWS, CH], F32R)
        bc = r.sb("bc", [P, BC_ROWS, CH])
        stats = r.sb("stats", [P, TT, 6])
        mv = r.sb("mv", [P, TT, 2])
        rstd = r.sb("rstd", [P, TT])
        var_eps = r.sb("var_eps", [P, TT])
        conv = r.sb("conv", [P, 2, CH])
        dt = conv
        soft = r.sb("soft", [P, CH])
        du = r.sb("du", [P, CH])
        da = r.sb("da", [P, 2, G, CH])
        h = r.sb("h", [P, 2, G, CH])
        state = r.sb("state", [P, CT, N])
        x_res = x_ext[:, :, CONV - 1:]
        bank = [r.ps(f"bank{i}", [P, CH]) for i in range(8)]
        ident, gate, neg_half = keep["ident"], keep["gate"], keep["neg_half"]
        fa, fb = keep["film"][:, 0, 0], keep["film"][:, 0, 1]
        names = ("weights_in x_loaded var_done rstd_done x_normed transposed turned in_mm ext_copied conv_done "
                 "u_done z_done x_mm part_a_done part_b_done bc_mm bc_act_done bc_dve_done dt_mm v_done soft_done dt_done "
                 "du_done da_done h_done hc_done sum_mm gated out_mm residual_in out_done stored own_dve own_act "
                 "setup_done reset_done")
        s = {n: r.sem(n) for n in names.split()}
        block = ctx.enter_context(nc.Block())
        x_rows = a["x"].rearrange("b s d -> (b s) d")
        CG = CT * NG

        @block.sync
        def _(sp):
            sp.dma_start(w_in[:, :, :], a["in_proj_w_T"].rearrange("(k p) n -> p k n", p=P)).then_inc(s["weights_in"], 16)
            sp.dma_start(w_x[:, :, :], a["x_proj_w_T"].rearrange("(k p) n -> p k n", p=P)).then_inc(s["weights_in"], 16)
            sp.dma_start(w_dt[:, :], a["dt_proj_w_T"]).then_inc(s["weights_in"], 16)
            sp.dma_start(w_out[:, :, :], a["out_proj_w_T"].rearrange("(k p) n -> p k n", p=P)).then_inc(s["weights_in"], 16)
            with sp.Fori(0, NB) as b, sp.Fori(0, NC_B) as c:
                it = b * NC_B + c
                sp.wait_ge(s["sum_mm"], it * CG)
                sp.dma_start(x_in, x_rows[bass.ds(it * CH, CH), :].rearrange("(t p) d -> p t d", p=P)).then_inc(s["x_loaded"], 16)
                sp.wait_ge(s["conv_done"], (it + 1) * CT)
                for t in range(TT):
                    if t >= 2:
                        sp.wait_ge(s["stored"], it * 16 * TT + 16 * (t - 1))
                    sp.dma_start(x_res[:, t % 2, :], x_rows[bass.ds(it * CH + t * P, P), :]).then_inc(s["residual_in"], 16)
                    sp.wait_ge(s["out_done"], it * TT + t + 1)
                    sp.dma_start(out[bass.ds(it * CH + t * P, P), :], x_res[:, t % 2, :]).then_inc(s["stored"], 16)
            sp.wait_ge(s["stored"], NCH * TT * 16)

        @block.gpsimd
        def _(pool):
            with pool.Fori(0, NB) as b, pool.Fori(0, NC_B) as c:
                it = b * NC_B + c
                pool.wait_ge(s["var_done"], it + 1)
                nc.gpsimd.tensor_tensor(rstd[:, :], var_eps[:, :], neg_half[:, 0:TT], ALU.pow).then_inc(s["rstd_done"], 1)
                for i in range(CG):
                    g = i % NG
                    pool.wait_ge(s["h_done"], it * CG + i + 1)
                    if i == 0:
                        pool.wait_ge(s["in_mm"], (it + 1) * 2 * CT)
                    elif i >= 4:
                        pool.wait_ge(s["sum_mm"], it * CG + i - 3)
                    nc.gpsimd.tensor_tensor(hc[:, i % 4, :, :], h[:, i % 2, :, :],
                                            bc[:, N + g * G:N + (g + 1) * G, :], ALU.mult).then_inc(s["hc_done"], 1)

        @block.scalar
        def _(act):
            nc.scalar.activation(a_exp[:, :, :], a_log, ACT.Exp).then_inc(s["setup_done"], 1)
            act.wait_ge(s["setup_done"], 1)
            nc.scalar.activation(a_neg[:, :, :], a_exp[:, :, :], ACT.Copy, scale=-1.0).then_inc(s["setup_done"], 1)
            for half in range(2):
                nc.scalar.activation(pick[half * BC_ROWS:(half + 1) * BC_ROWS, :], ident[0:BC_ROWS, 0:BC_ROWS],
                                     ACT.Copy).then_inc(s["setup_done"], 1)
            act.wait_ge(s["setup_done"], 4)
            with act.Fori(0, NB) as b, act.Fori(0, NC_B) as c:
                it = b * NC_B + c
                own = Chain(act, s["own_act"], it, 2 * CT)
                for k in range(KD):
                    act.wait_ge(s["transposed"], it * KD + k + 1)
                    nc.scalar.activation(xn_t[:, k, :], bank[k][:, :], ACT.Identity,
                                         scale=fa[:, k, bass.ds(b, 1)], bias=fb[:, k, bass.ds(b, 1)]).then_inc(s["turned"], 1)
                act.wait_ge(s["stored"], it * 16 * TT)
                for e in range(CT + 1):
                    if e < CT:
                        act.wait_ge(s["in_mm"], it * 2 * CT + e + 1)
                        if e >= 2:
                            act.wait_ge(s["conv_done"], it * CT + e - 1)
                        nc.scalar.activation(x_ext[:, e % 2, CONV - 1:], bank[4 + e % 2][:, :], ACT.Copy).then_inc(s["ext_copied"], 1)
                    if e >= 1:
                        act.wait_ge(s["conv_done"], it * CT + e)
                        nc.scalar.activation(u[:, e - 1, :], conv[:, (e - 1) % 2, :], ACT.Silu).then_inc(s["u_done"], 1)
                act.wait_ge(s["out_mm"], it * TT)
                for e in range(CT):
                    act.wait_ge(s["in_mm"], it * 2 * CT + CT + e + 1)
                    nc.scalar.activation(zy[:, e, :], bank[4 + e % 2][:, :], ACT.Silu).then_inc(s["z_done"], 1)
                act.wait_ge(s["x_mm"], it + 1)
                nc.scalar.activation(dt_r[:, :], bank[6][0:RANK, :], ACT.Copy).then_inc(s["part_a_done"], 1)
                nc.scalar.activation(bc_parts[0:BC_ROWS, :], bank[6][RANK:RANK + BC_ROWS, :], ACT.Copy).then_inc(s["part_a_done"], 1)
                for n in range(0, BC_ROWS, 2):
                    act.wait_ge(s["bc_mm"], it * BC_ROWS + n + 1)
                    nc.scalar.activation(bc[:, n, :], bank[n % 4][:, :], ACT.Copy).then_inc(s["bc_act_done"], 1)

                def softplus(ct):
                    act.wait_ge(s["v_done"], it * CT + ct + 1)
                    own.inc(nc.scalar.activation(soft[:, :], dt[:, ct % 2, :], ACT.Abs))
                    own.wait()
                    own.inc(nc.scalar.activation(soft[:, :], soft[:, :], ACT.Exp, scale=-1.0))
                    own.wait()
                    nc.scalar.activation(soft[:, :], soft[:, :], ACT.Ln, bias=1.0).then_inc(s["soft_done"], 1)

                softplus(0)
                for ct in range(CT):
                    act.wait_ge(s["dt_done"], it * CT + ct + 1)
                    for g in range(NG):
                        i = ct * NG + g
                        act.wait_ge(s["h_done"], it * CG + max(i - 1, 0))
                        for j in range(G):
                            n = g * G + j
                            last = nc.scalar.activation(da[:, i % 2, j, :], dt[:, ct % 2, :], ACT.Exp, scale=a_neg[:, ct, n:n + 1])
                        last.then_inc(s["da_done"], 1)
                        if g == NG // 2 and ct + 1 < CT:
                            softplus(ct + 1)
                own.end()

        @block.vector
        def _(dve):
            with dve.Fori(0, NB) as b:
                nc.vector.memset(halo[:, :, :], 0.0).then_inc(s["reset_done"], 1)
                nc.vector.memset(state[:, :, :], 0.0).then_inc(s["reset_done"], 1)
                with dve.Fori(0, NC_B) as c:
                    it = b * NC_B + c
                    own = Chain(dve, s["own_dve"], it, 2 + 5 * CT + 2 * CT + CG + CG + TT)
                    dve.wait_ge(s["reset_done"], 2 * b + 2)
                    dve.wait_ge(s["x_loaded"], it * 16 + 16)
                    for t in range(TT):
                        st = nc.vector.bn_stats(stats[:, t, :], x_in[:, t, :])
                    own.inc(st)
                    own.wait()
                    nc.vector.memset(var_eps[:, :], 0.0)
                    for t in range(TT):
                        st = nc.vector.bn_aggr(mv[:, t, :], stats[:, t, :])
                    own.inc(st)
                    own.wait()
                    nc.vector.tensor_scalar(var_eps[:, :], mv[:, :, 1], EPS, None, ALU.add).then_inc(s["var_done"], 1)
                    dve.wait_ge(s["rstd_done"], it + 1)
                    for t in range(TT):
                        last = nc.vector.tensor_scalar(x_in[:, t, :], x_in[:, t, :], mv[:, t, 0:1], rstd[:, t:t + 1],
                                                       ALU.subtract, ALU.mult)
                    last.then_inc(s["x_normed"], 1)
                    for e in range(CT):
                        w = e % 2
                        dve.wait_ge(s["ext_copied"], it * CT + e + 1)
                        own.inc(nc.vector.tensor_copy(x_ext[:, w, 0:CONV - 1], halo[:, e, :]))
                        own.wait()
                        own.inc(nc.vector.tensor_copy(halo[:, e, :], x_ext[:, w, CH:CH + CONV - 1]))
                        own.wait()
                        if e >= 2:
                            dve.wait_ge(s["u_done"], it * CT + e - 1)
                        own.inc(nc.vector.tensor_scalar(conv[:, w, :], x_ext[:, w, 0:CH], conv_w[:, e, 0:1], conv_b[:, e:e + 1],
                                                        ALU.mult, ALU.add))
                        for j in range(1, CONV):
                            own.wait()
                            last = nc.vector.scalar_tensor_tensor(out=conv[:, w, :], in0=x_ext[:, w, j:j + CH],
                                                                  scalar=conv_w[:, e, j:j + 1], in1=conv[:, w, :],
                                                                  op0=ALU.mult, op1=ALU.add)
                            if j < CONV - 1:
                                own.inc(last)
                        last.then_inc(s["conv_done"], 1)
                    dve.wait_ge(s["part_a_done"], it * 2 + 2)
                    nc.vector.tensor_tensor(bc_parts[BC_ROWS:2 * BC_ROWS, :], bank[6][RANK:RANK + BC_ROWS, :],
                                            bc_parts[0:BC_ROWS, :].bitcast(F32), ALU.subtract).then_inc(s["part_b_done"], 1)
                    for n in range(1, BC_ROWS, 2):
                        dve.wait_ge(s["bc_mm"], it * BC_ROWS + n + 1)
                        nc.vector.tensor_copy(bc[:, n, :], bank[n % 4][:, :]).then_inc(s["bc_dve_done"], 1)
                    dve.wait_ge(s["bc_act_done"], (it + 1) * N)
                    dve.wait_ge(s["bc_dve_done"], (it + 1) * N)
                    dve.wait_ge(s["u_done"], (it + 1) * CT)
                    dve.wait_ge(s["z_done"], (it + 1) * CT)

                    def take_v(ct):
                        dve.wait_ge(s["dt_mm"], it * CT + ct + 1)
                        if ct >= 2:
                            dve.wait_ge(s["da_done"], it * CG + (ct - 1) * NG)
                        nc.vector.tensor_scalar(dt[:, ct % 2, :], bank[6 + ct % 2][:, :], dt_b[:, ct:ct + 1], None,
                                                ALU.add).then_inc(s["v_done"], 1)

                    def make_dt(ct):
                        dve.wait_ge(s["soft_done"], it * CT + ct + 1)
                        nc.vector.scalar_tensor_tensor(out=dt[:, ct % 2, :], in0=dt[:, ct % 2, :], scalar=0.0, in1=soft[:, :],
                                                       op0=ALU.max, op1=ALU.add).then_inc(s["dt_done"], 1)

                    def save_state(i):
                        ct, g = divmod(i, NG)
                        dve.wait_ge(s["h_done"], it * CG + i + 1)
                        return nc.vector.tensor_copy(state[:, ct, g * G:(g + 1) * G], h[:, i % 2, :, CH - 1])

                    def gate_y(ct):
                        dve.wait_ge(s["sum_mm"], it * CG + (ct + 1) * NG)
                        own.inc(nc.vector.scalar_tensor_tensor(out=u[:, ct, :], in0=u[:, ct, :], scalar=d_par[:, ct:ct + 1],
                                                               in1=bank[4 + ct % 2][:, :], op0=ALU.mult, op1=ALU.add))
                        own.wait()
                        nc.vector.tensor_tensor(zy[:, ct, :], u[:, ct, :], zy[:, ct, :], ALU.mult).then_inc(s["gated"], 1)

                    take_v(0)
                    make_dt(0)
                    for ct in range(CT):
                        dve.wait_ge(s["dt_done"], it * CT + ct + 1)
                        own.inc(nc.vector.tensor_tensor(du[:, :], dt[:, ct % 2, :], u[:, ct, :], ALU.mult))
                        own.wait()
                        for g in range(NG):
                            i = ct * NG + g
                            if i >= 2:
                                dve.wait_ge(s["hc_done"], it * CG + i - 1)
                            own.inc(nc.vector.tensor_tensor(h[:, i % 2, :, :], du[:, :].unsqueeze(1).to_broadcast([P, G, CH]),
                                                            bc[:, g * G:(g + 1) * G, :], ALU.mult))
                            if i >= 1:
                                own.inc(save_state(i - 1))
                            dve.wait_ge(s["da_done"], it * CG + i + 1)
                            own.wait()
                            for j in range(G):
                                last = nc.vector.tensor_tensor_scan(h[:, i % 2, j, :], da[:, i % 2, j, :], h[:, i % 2, j, :],
                                                                    state[:, ct, g * G + j:g * G + j + 1], ALU.mult, ALU.add)
                            last.then_inc(s["h_done"], 1)
                            if g == 2 and ct >= 1:
                                gate_y(ct - 1)
                            if g == NG // 2 - 1 and ct + 1 < CT:
                                take_v(ct + 1)
                            if g == NG // 2 + 1 and ct + 1 < CT:
                                make_dt(ct + 1)
                    own.inc(save_state(CG - 1))
                    own.wait()
                    gate_y(CT - 1)
                    for t in range(TT):
                        dve.wait_ge(s["out_mm"], it * TT + t + 1)
                        own.inc(nc.vector.tensor_tensor(bank[t][:, :], bank[t][:, :], gate[:, bass.ds(b, 1), :].rearrange("p a d -> p (a d)"), ALU.mult))
                        own.wait()
                        dve.wait_ge(s["residual_in"], it * TT * 16 + 16 * (t + 1))
                        nc.vector.tensor_tensor(x_res[:, t % 2, :], bank[t][:, :], x_res[:, t % 2, :], ALU.add).then_inc(s["out_done"], 1)
                    own.end()

        @block.tensor
        def _(pe):
            pe.wait_ge(s["weights_in"], 64)
            pe.wait_ge(s["setup_done"], 4)
            with pe.Fori(0, NB) as b, pe.Fori(0, NC_B) as c:
                it = b * NC_B + c
                pe.wait_ge(s["x_normed"], it + 1)
                pe.wait_ge(s["out_done"], it * TT)
                for k in range(KD):
                    for t in range(TT):
                        mm = nc.tensor.transpose(bank[k][:, t * P:(t + 1) * P], x_in[:, t, k * P:(k + 1) * P], ident[:, :])
                    mm.then_inc(s["transposed"], 1)
                for e in range(2 * CT):
                    if e == 0:
                        pe.wait_ge(s["turned"], (it + 1) * KD)
                    elif 2 <= e < CT + 2:
                        pe.wait_ge(s["ext_copied"], it * CT + e - 1)
                    elif e >= CT + 2:
                        pe.wait_ge(s["z_done"], it * CT + e - CT - 1)
                    for k in range(KD):
                        mm = nc.tensor.matmul(bank[4 + e % 2][:, :], w_in[:, k, e * P:(e + 1) * P], xn_t[:, k, :],
                                              start=(k == 0), stop=(k == KD - 1))
                    mm.then_inc(s["in_mm"], 1)
                for k in range(CT):
                    pe.wait_ge(s["u_done"], it * CT + k + 1)
                    mm = nc.tensor.matmul(bank[6][0:RANK + BC_ROWS, :], w_x[:, k, :], u[:, k, :], start=(k == 0), stop=(k == CT - 1))
                mm.then_inc(s["x_mm"], 1)
                pe.wait_ge(s["part_a_done"], it * 2 + 2)
                pe.wait_ge(s["part_b_done"], it + 1)
                for n in range(BC_ROWS):
                    if n >= 4:
                        done = s["bc_dve_done"] if n % 2 else s["bc_act_done"]
                        pe.wait_ge(done, it * N + n // 2 - 1)
                    nc.tensor.matmul(bank[n % 4][:, :], pick[:, n:n + 1].to_broadcast([2 * BC_ROWS, P]), bc_parts[:, :],
                                     start=True, stop=True).then_inc(s["bc_mm"], 1)

                def project_dt(ct):
                    if ct >= 2:
                        pe.wait_ge(s["dt_done"], it * CT + ct - 1)
                    nc.tensor.matmul(bank[6 + ct % 2][:, :], w_dt[:, ct * P:(ct + 1) * P], dt_r[:, :],
                                     start=True, stop=True).then_inc(s["dt_mm"], 1)

                project_dt(0)
                for ct in range(CT):
                    if ct + 1 < CT:
                        project_dt(ct + 1)
                    if ct < 2:
                        pe.wait_ge(s["z_done"], (it + 1) * CT)
                    else:
                        pe.wait_ge(s["gated"], it * CT + ct - 1)
                    for g in range(NG):
                        i = ct * NG + g
                        pe.wait_ge(s["hc_done"], it * CG + i + 1)
                        for j in range(G):
                            mm = nc.tensor.matmul(bank[4 + ct % 2][:, :], ident[:, :], hc[:, i % 4, j, :],
                                                  start=(g == 0 and j == 0), stop=(g == NG - 1 and j == G - 1))
                        mm.then_inc(s["sum_mm"], 1)
                pe.wait_ge(s["gated"], (it + 1) * CT)
                for t in range(TT):
                    for k in range(CT):
                        mm = nc.tensor.matmul(bank[t][:, :], zy[:, k, t * P:(t + 1) * P], w_out[:, k, :],
                                              start=(k == 0), stop=(k == CT - 1))
                    mm.then_inc(s["out_mm"], 1)



class Norm:

    def __init__(self, r, keep, banks=None):
        self.x = r.sb("norm_x", [P, TT, D])
        self.xn_t = r.sb("norm_xn_t", [P, KD, CH])
        self.stats = r.sb("norm_stats", [P, TT, 6])
        self.mv = r.sb("norm_mv", [P, TT, 2])
        self.var_eps = r.sb("norm_var_eps", [P, TT])
        self.rstd = r.sb("norm_rstd", [P, TT])
        self.bank = banks or [r.ps(f"norm_bank{i}", [P, CH]) for i in range(4)]
        self.ident, self.neg_half = keep["ident"], keep["neg_half"]
        self.x_loaded, self.var_done, self.rstd_done, self.x_normed, self.transposed, self.turned = (
            r.sem(n) for n in ("x_loaded", "var_done", "rstd_done", "x_normed", "transposed", "turned"))


DVE_NORM = 2


def norm_load(sp, m, rows, it):
    sp.wait_ge(m.transposed, it * KD)
    sp.dma_start(m.x[:, :, :], rows[bass.ds(it * CH, CH), :].rearrange("(t p) d -> p t d", p=P)).then_inc(m.x_loaded, 16)


def norm_dve(nc, dve, m, own, it, src):
    for t in range(TT):
        last = nc.vector.bn_stats(m.stats[:, t, :], src(t))
    own.inc(last)
    own.wait()
    nc.vector.memset(m.var_eps[:, :], 0.0)
    for t in range(TT):
        last = nc.vector.bn_aggr(m.mv[:, t, :], m.stats[:, t, :])
    own.inc(last)
    own.wait()
    nc.vector.tensor_scalar(m.var_eps[:, :], m.mv[:, :, 1], EPS, None, ALU.add).then_inc(m.var_done, 1)
    dve.wait_ge(m.rstd_done, it + 1)
    dve.wait_ge(m.transposed, it * KD)
    for t in range(TT):
        last = nc.vector.tensor_scalar(m.x[:, t, :], src(t), m.mv[:, t, 0:1], m.rstd[:, t:t + 1],
                                       ALU.subtract, ALU.mult)
    last.then_inc(m.x_normed, 1)


def norm_pool(nc, pool, m, it):
    pool.wait_ge(m.var_done, it + 1)
    nc.gpsimd.tensor_tensor(m.rstd[:, :], m.var_eps[:, :], m.neg_half[:, 0:TT], ALU.pow).then_inc(m.rstd_done, 1)


def norm_pe(nc, pe, m, it):
    pe.wait_ge(m.x_normed, it + 1)
    pe.wait_ge(m.turned, it * KD)
    for k in range(KD):
        for t in range(TT):
            mm = nc.tensor.transpose(m.bank[k][:, t * P:(t + 1) * P], m.x[:, t, k * P:(k + 1) * P], m.ident[:, :])
        mm.then_inc(m.transposed, 1)


def norm_act(nc, act, m, it, func, scale, bias):
    for k in range(KD):
        act.wait_ge(m.transposed, it * KD + k + 1)
        nc.scalar.activation(m.xn_t[:, k, :], m.bank[k][:, :], func, scale=scale(k), bias=bias(k)).then_inc(m.turned, 1)


H1 = 16
DH1 = D // H1
QT = S // P
NT = NB * QT


def stage_qkv(nc, a, keep, src, parts, mask_parts, v):
    with ExitStack() as ctx:
        r = Room(nc, ctx, "qkv")
        m = Norm(r, keep)
        w = [r.sb(f"w_{n}", [P, KD, D]) for n in "qkv"]
        v_b = r.sb("v_b", [P, D])
        mask = r.sb("mask", [P, NT])
        mrow = r.sb("mrow", [NT, P])
        mrow_parts = r.sb("mrow_parts", [NT, 2, P], F32R)
        vb = r.sb("vb", [P, 2, D])
        full = r.sb("full", [P, 2, CH])
        pair = r.sb("pair", [P, 2, 2, CH], F32R)
        bank = [r.ps(f"bank{i}", [P, CH]) for i in range(4)]
        names = "weights_in small_in mask_done mask_stored v_mm v_biased v_done qk_mm full_done first_done second_done own_dve"
        s = {n: r.sem(n) for n in names.split()}
        stored = [r.sem(f"stored{i}") for i in range(2)]
        cols = keep["cols"]
        g, bvec = column(cols, "L1_cond_norm_w"), column(cols, "L1_cond_norm_b")
        qk_bias = [column(cols, "L1_cond_q_b"), column(cols, "L1_cond_k_b")]
        block = ctx.enter_context(nc.Block())
        NQ = 2 * KD

        @block.sync
        def _(sp):
            sp.dma_start(w[2][:, :, :], a["L1_cond_v_w"].rearrange("(k p) n -> p k n", p=P)).then_inc(s["weights_in"], 16)
            sp.dma_start(w[0][:, :, :], a["L1_cond_q_w"].rearrange("(k p) n -> p k n", p=P)).then_inc(s["weights_in"], 16)
            sp.dma_start(w[1][:, :, :], a["L1_cond_k_w"].rearrange("(k p) n -> p k n", p=P)).then_inc(s["weights_in"], 16)
            with sp.Fori(0, NCH) as it:
                norm_load(sp, m, src, it)
            sp.wait_ge(s["mask_done"], 3)
            sp.dma_start(mask_parts.rearrange("a (t j) -> t a j", j=P), mrow_parts[:, :, :].bitcast(F32)).then_inc(s["mask_stored"], 16)
            sp.wait_ge(s["mask_stored"], 16)
            for slot in range(2):
                sp.wait_ge(stored[slot], NCH * NQ // 2 * 16)

        @block.gpsimd
        def _(pool):
            with pool.Fori(0, NCH) as it:
                norm_pool(nc, pool, m, it)
                for i in range(NQ):
                    which, mt = divmod(i, KD)
                    pool.wait_ge(s["second_done"], it * NQ + i + 1)
                    pool.dma_start(parts[which, :, mt * P:(mt + 1) * P, bass.ds(it * CH, CH)].rearrange("a p s -> p a s"),
                                   pair[:, i % 2, :, :].bitcast(F32)).then_inc(stored[i % 2], 16)

        @block.tensor
        def _(pe):
            pe.wait_ge(s["weights_in"], 48)
            with pe.Fori(0, NCH) as it:
                norm_pe(nc, pe, m, it)
                pe.wait_ge(m.turned, (it + 1) * KD)
                for t in range(TT):
                    pe.wait_ge(s["v_biased"], it * TT + t - 1) if t >= 2 else pe.wait_ge(s["v_biased"], it * TT)
                    for k in range(KD):
                        mm = nc.tensor.matmul(bank[t % 2][:, :], m.xn_t[:, k, t * P:(t + 1) * P], w[2][:, k, :],
                                              start=(k == 0), stop=(k == KD - 1))
                    mm.then_inc(s["v_mm"], 1)
                for i in range(NQ):
                    which, mt = divmod(i, KD)
                    pe.wait_ge(s["full_done"], it * NQ + i - 1) if i >= 2 else pe.wait_ge(s["full_done"], it * NQ)
                    for k in range(KD):
                        mm = nc.tensor.matmul(bank[2 + i % 2][:, :], w[which][:, k, mt * P:(mt + 1) * P], m.xn_t[:, k, :],
                                              start=(k == 0), stop=(k == KD - 1))
                    mm.then_inc(s["qk_mm"], 1)

        @block.scalar
        def _(act):
            act.dma_start(v_b[:, :], row_on_all(a["L1_cond_v_b"])).then_inc(s["small_in"], 16)
            act.dma_start(mask[:, :], a["mask_ff1_columns"]).then_inc(s["small_in"], 16)
            act.dma_start(mrow[:, :], a["mask_BxS_ff1"].rearrange("b (t j) -> (b t) j", j=P)).then_inc(s["small_in"], 16)
            act.wait_ge(s["mask_done"], 1)
            nc.scalar.activation(mrow_parts[:, 0, :], mrow[:, :], ACT.Copy).then_inc(s["mask_done"], 1)
            with act.Fori(0, NB) as b, act.Fori(0, NC_B) as c:
                it = b * NC_B + c
                act.wait_ge(s["qk_mm"], it * NQ)
                norm_act(nc, act, m, it, ACT.Identity, lambda k: g[:, k:k + 1], lambda k: bvec[:, k:k + 1])
                for t in range(TT):
                    act.wait_ge(s["v_biased"], it * TT + t + 1)
                    nc.scalar.activation(v[:, bass.ds(c * TT + t, 1), bass.ds(b * D, D)].rearrange("p a d -> p (a d)"),
                                         vb[:, t % 2, :], ACT.Copy,
                                         scale=mask[:, bass.ds(it * TT + t, 1)]).then_inc(s["v_done"], 1)
                for i in range(NQ):
                    which, mt = divmod(i, KD)
                    act.wait_ge(s["qk_mm"], it * NQ + i + 1)
                    act.wait_ge(s["second_done"], it * NQ + max(i - 1, 0))
                    nc.scalar.activation(full[:, i % 2, :], bank[2 + i % 2][:, :], ACT.Identity,
                                         bias=qk_bias[which][:, mt:mt + 1]).then_inc(s["full_done"], 1)
                    act.wait_ge(s["full_done"], it * NQ + i + 1)
                    act.wait_ge(stored[i % 2], (it * (NQ // 2) + i // 2) * 16)
                    nc.scalar.activation(pair[:, i % 2, 0, :], full[:, i % 2, :], ACT.Copy).then_inc(s["first_done"], 1)

        @block.vector
        def _(dve):
            dve.wait_ge(s["small_in"], 48)
            nc.vector.tensor_scalar(mrow[:, :], mrow[:, :], 1e6, -1e6, ALU.mult, ALU.add).then_inc(s["mask_done"], 1)
            dve.wait_ge(s["mask_done"], 2)
            nc.vector.tensor_tensor(mrow_parts[:, 1, :], mrow[:, :], mrow_parts[:, 0, :].bitcast(F32), ALU.subtract).then_inc(s["mask_done"], 1)
            with dve.Fori(0, NCH) as it:
                own = Chain(dve, s["own_dve"], it, DVE_NORM)
                dve.wait_ge(m.x_loaded, (it + 1) * 16)
                norm_dve(nc, dve, m, own, it, lambda t: m.x[:, t, :])
                for t in range(TT):
                    dve.wait_ge(s["v_mm"], it * TT + t + 1)
                    dve.wait_ge(s["v_done"], it * TT + max(t - 1, 0))
                    nc.vector.tensor_tensor(vb[:, t % 2, :], bank[t % 2][:, :], v_b[:, :], ALU.add).then_inc(s["v_biased"], 1)
                for i in range(NQ):
                    dve.wait_ge(s["first_done"], it * NQ + i + 1)
                    nc.vector.tensor_tensor(pair[:, i % 2, 1, :], full[:, i % 2, :], pair[:, i % 2, 0, :].bitcast(F32),
                                            ALU.subtract).then_inc(s["second_done"], 1)
                own.end()


def stage_attention(nc, a, keep, parts, mask_parts, max_rows, v, y):
    with ExitStack() as ctx:
        r = Room(nc, ctx, "attn")
        ROWS_MAX, ROWS = 3 * DH1 + 2, 3 * DH1 + 4
        VW = 2 * DH1 + 1
        HALF = S // 2
        STEPS = 2 * QT
        NMAX = QT * (S // CH)
        FIRST_MAX, MAX_STEPS = 3, 25
        TURN_MAX, TURN_0 = 28, 30
        BUILD_V = 4
        HEADS = NB * H1
        JT = HALF // P
        SLOTS = 3
        DVE_COLS = 320
        q_st = [r.sb(f"q_stack{i}", [ROWS, S], F32R) for i in range(2)]
        k_st = [r.sb(f"k_stack{i}", [ROWS, S], F32R) for i in range(2)]
        prob = [r.sb(f"prob{i}", [P, HALF]) for i in range(SLOTS)]
        prob_a = [r.sb(f"prob_a{i}", [P, HALF], F32R) for i in range(2)]
        prob_b = [r.sb(f"prob_b{i}", [P, HALF], F32R) for i in range(2)]
        mx = r.sb("mx", [P, QT, S // CH])
        m_all = r.sb("m_all", [P, QT])
        m_parts = r.sb("m_parts", [QT, 2, P], F32R)
        rden = r.sb("rden", [P, JT, 1])
        v_h = [r.sb(f"v_h{i}", [P, QT, VW], F32R) for i in range(2)]
        fold = r.sb("fold", [VW, DH1 + 1])
        o_t = r.sb("o_t", [VW, HALF])
        ps_max = [r.ps(f"ps_max{i}", [P, CH]) for i in range(2)]
        ps_s = [r.ps(f"ps_s{i}", [P, HALF]) for i in range(2)]
        ps_o = r.ps("ps_o", [P, HALF])
        o_nat = ps_max[1][:, 0:JT * (DH1 + 1)].rearrange("p (j e) -> p j e", e=DH1 + 1)
        names = ("stack_free stack_in max_in max_mm max_red m_done m_turned m_first m_second m_stored s_mm e_done a_done "
                 "b_done_pool b_done_dve o_mm o_copied o_turned o_read v_first v_copied fold_set own_dve")
        s = {n: r.sem(n) for n in names.split()}
        block = ctx.enter_context(nc.Block())

        def load_stacks(sp, b, h, slot):
            f = h * DH1
            at = bass.ds(b * S, S)
            part = lambda which, p: parts[which, p, bass.ds(f, DH1), at]
            sp.dma_start(k_st[slot][0:DH1, :].bitcast(F32), part(1, 0)).then_inc(s["stack_in"], 16)
            sp.dma_start(k_st[slot][DH1:2 * DH1, :].bitcast(F32), part(1, 1)).then_inc(s["stack_in"], 16)
            sp.dma_start(k_st[slot][2 * DH1:3 * DH1, :].bitcast(F32), part(1, 0)).then_inc(s["stack_in"], 16)
            sp.dma_start(k_st[slot][3 * DH1:3 * DH1 + 2, :].bitcast(F32), mask_parts[:, at]).then_inc(s["stack_in"], 16)
            sp.dma_start(q_st[slot][0:DH1, :].bitcast(F32), part(0, 0)).then_inc(s["stack_in"], 16)
            sp.dma_start(q_st[slot][DH1:2 * DH1, :].bitcast(F32), part(0, 0)).then_inc(s["stack_in"], 16)
            sp.dma_start(q_st[slot][2 * DH1:3 * DH1, :].bitcast(F32), part(0, 1)).then_inc(s["stack_in"], 16)

        NSTACK = 7

        def each_head(engine, head):
            head(0, 0, True, False)
            with engine.Fori(0, HEADS // 2 - 1) as i:
                head(2 * i + 1, 1, False, False)
                head(2 * i + 2, 0, False, False)
            head(HEADS - 1, 1, False, True)

        def max_tiles(st):
            return [i for i in range(NMAX) if FIRST_MAX + i * MAX_STEPS // NMAX == st]

        def slot_free(hd, st):
            return hd * STEPS + (st - SLOTS + 1 if st >= SLOTS else min(st, 1) - 1)

        @block.sync
        def _(sp):
            with sp.Fori(0, NB) as b, sp.Fori(0, H1 // 2) as hp:
                for slot in range(2):
                    hd = b * H1 + 2 * hp + slot
                    sp.wait_ge(s["stack_free"], hd + 2)
                    load_stacks(sp, b, 2 * hp + slot, slot)
                    sp.wait_ge(s["m_second"], hd + 1)
                    sp.dma_start(max_rows[slot].rearrange("a (q j) -> q a j", j=P), m_parts[:, :, :].bitcast(F32)).then_inc(s["m_stored"], 16)
                    sp.wait_ge(s["m_stored"], (hd + 1) * 16)
                    sp.dma_start(q_st[slot][3 * DH1 + 2:ROWS, :].bitcast(F32), max_rows[slot]).then_inc(s["max_in"], 16)

        @block.gpsimd
        def _(pool):
            def first_v(hd, slot):
                nc.gpsimd.tensor_copy(v_h[slot][:, :, 0:DH1], v[:, :, bass.ds(hd * DH1, DH1)]).then_inc(s["v_first"], 1)

            def second_v(hd, slot):
                nc.gpsimd.tensor_tensor(v_h[slot][:, :, DH1:2 * DH1], v[:, :, bass.ds(hd * DH1, DH1)], v_h[slot][:, :, 0:DH1].bitcast(F32),
                                        ALU.subtract).then_inc(s["v_copied"], 1)

            def head(hd, slot, first, last):
                for st in range(STEPS):
                    if st == BUILD_V and not last:
                        pool.wait_ge(s["o_mm"], hd * STEPS)
                        first_v(hd + 1, 1 - slot)
                        pool.wait_ge(s["v_first"], hd + 2)
                    pool.wait_ge(s["a_done"], hd * STEPS + st + 1)
                    if not (first and st < 2):
                        pool.wait_ge(s["o_mm"], hd * STEPS + st - 1)
                    nc.gpsimd.tensor_tensor(prob_b[st % 2][:, CH:], prob[st % SLOTS][:, CH:],
                                            prob_a[st % 2][:, CH:].bitcast(F32), ALU.subtract).then_inc(s["b_done_pool"], 1)
                    nc.gpsimd.tensor_tensor(prob_b[st % 2][:, DVE_COLS:CH], prob[st % SLOTS][:, DVE_COLS:CH],
                                            prob_a[st % 2][:, DVE_COLS:CH].bitcast(F32), ALU.subtract).then_inc(s["b_done_pool"], 1)
                    if st == BUILD_V and not last:
                        second_v(hd + 1, 1 - slot)

            for slot in range(2):
                nc.gpsimd.memset(v_h[slot][:, :, 2 * DH1:VW].bitcast(F32), 1.0)
            first_v(0, 0)
            pool.wait_ge(s["v_first"], 1)
            second_v(0, 0)
            each_head(pool, head)

        @block.tensor
        def _(pe):
            def max_mm(hd, slot, i, first=False):
                if i == 0:
                    pe.wait_ge(s["stack_in"], (hd + 1) * NSTACK * 16)
                    pe.wait_ge(s["m_second"], hd)
                    if not first:
                        pe.wait_ge(s["o_read"], (hd - 1) * 2)
                pe.wait_ge(s["max_red"], hd * NMAX + max(i - 1, 0))
                qt, kc = divmod(i, S // CH)
                nc.tensor.matmul(ps_max[i % 2][:, :], q_st[slot][0:ROWS_MAX, qt * P:(qt + 1) * P],
                                 k_st[slot][0:ROWS_MAX, kc * CH:(kc + 1) * CH], start=True, stop=True).then_inc(s["max_mm"], 1)

            def turn_max(hd):
                pe.wait_ge(s["m_done"], hd + 1)
                nc.tensor.transpose(ps_max[0][0:QT, 0:P], m_all[:, :], keep["ident"][:, :]).then_inc(s["m_turned"], 1)

            def score_mm(hd, slot, st):
                half, kt = divmod(st, QT)
                if st == 0:
                    pe.wait_ge(s["max_in"], (hd + 1) * 16)
                pe.wait_ge(s["a_done"], hd * STEPS + max(st - 1, 0))
                for c in range(2):
                    q0 = half * HALF + c * CH
                    mm = nc.tensor.matmul(ps_s[st % 2][:, c * CH:(c + 1) * CH], k_st[slot][0:ROWS, kt * P:(kt + 1) * P],
                                          q_st[slot][0:ROWS, q0:q0 + CH], start=True, stop=True)
                    if st == 0 and c == 0:
                        mm.then_inc(s["stack_free"], 1)
                mm.then_inc(s["s_mm"], 1)

            def pv_mm(hd, slot, st, c):
                half, kt = divmod(st, QT)
                if st == 0 and c == 0:
                    pe.wait_ge(s["v_copied"], hd + 1)
                if kt == 0:
                    pe.wait_ge(s["o_copied"], hd * 4 + (c + 1 if half else 0))
                pe.wait_ge(s["a_done"], hd * STEPS + st + 1)
                cols = slice(c * CH, (c + 1) * CH)
                nc.tensor.matmul(ps_o[0:VW, cols], v_h[slot][:, kt, :], prob_a[st % 2][:, cols], start=(kt == 0), stop=False)

            def pv_rest(hd, slot, st, c):
                half, kt = divmod(st, QT)
                cols = slice(c * CH, (c + 1) * CH)
                pe.wait_ge(s["b_done_pool"], (hd * STEPS + st) * 2 + (1 if c else 2))
                if not c:
                    pe.wait_ge(s["b_done_dve"], hd * STEPS + st + 1)
                mm = nc.tensor.matmul(ps_o[0:VW, cols], v_h[slot][:, kt, :], prob_b[st % 2][:, cols],
                                      start=False, stop=(kt == QT - 1))
                if not c:
                    mm.then_inc(s["o_mm"], 1)

            def turn_o(done):
                pe.wait_ge(s["o_copied"], (done + 1) * 2)
                for j in range(JT):
                    mm = nc.tensor.matmul(o_nat[:, j, :], o_t[:, j * P:(j + 1) * P], fold[:, :], start=True, stop=True)
                mm.then_inc(s["o_turned"], 1)

            def head(hd, slot, first, last):
                for st in range(STEPS):
                    if st + 1 < STEPS:
                        score_mm(hd, slot, st + 1)
                    elif not last:
                        score_mm(hd + 1, 1 - slot, 0)
                    tiles = [] if last else max_tiles(st)
                    if st == 2 and not first:
                        turn_o(hd * 2 - 1)
                    before = (hd, slot, st - 1) if st else (hd - 1, 1 - slot, STEPS - 1)
                    for j in range(4):
                        if j < 3:
                            for i in tiles[j:j + 1]:
                                max_mm(hd + 1, 1 - slot, i)
                        if st or not first:
                            if j < 2:
                                pv_mm(*before, j)
                            else:
                                pv_rest(*before, 3 - j)
                    if st == TURN_MAX and not last:
                        turn_max(hd + 1)
                    if st == TURN_0:
                        turn_o(hd * 2)
                if last:
                    for c in range(2):
                        pv_mm(hd, slot, STEPS - 1, c)
                    for c in (1, 0):
                        pv_rest(hd, slot, STEPS - 1, c)
                    turn_o(hd * 2 + 1)

            for i in range(NMAX):
                max_mm(0, 0, i, True)
            turn_max(0)
            pe.wait_ge(s["fold_set"], 1)
            score_mm(0, 0, 0)
            each_head(pe, head)

        @block.scalar
        def _(act):
            def first_part(hd):
                act.wait_ge(s["m_turned"], hd + 1)
                act.wait_ge(s["m_stored"], hd * 16)
                nc.scalar.activation(m_parts[:, 0, :], ps_max[0][0:QT, 0:P], ACT.Copy, scale=-1.0).then_inc(s["m_first"], 1)

            def head(hd, slot, first, last):
                for st in range(STEPS):
                    act.wait_ge(s["s_mm"], hd * STEPS + st + 1)
                    if not (first and st < SLOTS):
                        act.wait_ge(s["b_done_pool"], slot_free(hd, st) * 2)
                        act.wait_ge(s["b_done_dve"], slot_free(hd, st))
                    nc.scalar.activation(prob[st % SLOTS][:, :], ps_s[st % 2][:, :], ACT.Exp).then_inc(s["e_done"], 1)
                    if not (first and st < 2):
                        act.wait_ge(s["o_mm"], hd * STEPS + st - 1)
                    nc.scalar.activation(prob_a[st % 2][:, :], ps_s[st % 2][:, :], ACT.Exp).then_inc(s["a_done"], 1)
                    if st == TURN_MAX and not last:
                        first_part(hd + 1)

            ident = keep["ident"]
            nc.scalar.activation(fold[0:DH1, 0:DH1], ident[0:DH1, 0:DH1], ACT.Copy)
            nc.scalar.activation(fold[DH1:2 * DH1, 0:DH1], ident[DH1:2 * DH1, DH1:2 * DH1], ACT.Copy)
            nc.scalar.activation(fold[0:2 * DH1, DH1:DH1 + 1], ident[0:2 * DH1, 2 * DH1:VW], ACT.Copy)
            nc.scalar.activation(fold[2 * DH1:VW, :], ident[2 * DH1:VW, DH1:2 * DH1 + 1], ACT.Copy).then_inc(s["fold_set"], 1)
            first_part(0)
            each_head(act, head)

        @block.vector
        def _(dve):
            def reduce(hd, i):
                qt, kc = divmod(i, S // CH)
                dve.wait_ge(s["max_mm"], hd * NMAX + i + 1)
                nc.vector.tensor_reduce(mx[:, qt, kc:kc + 1], ps_max[i % 2][:, :], AX.X, ALU.max).then_inc(s["max_red"], 1)

            def all_max(hd):
                dve.wait_ge(s["max_red"], (hd + 1) * NMAX)
                dve.wait_ge(s["m_turned"], hd)
                nc.vector.tensor_reduce(m_all[:, :], mx[:, :, :], AX.X, ALU.max).then_inc(s["m_done"], 1)

            def second_part(hd):
                dve.wait_ge(s["m_first"], hd + 1)
                nc.vector.scalar_tensor_tensor(out=m_parts[:, 1, :], in0=ps_max[0][0:QT, 0:P], scalar=-1.0,
                                               in1=m_parts[:, 0, :].bitcast(F32), op0=ALU.mult, op1=ALU.subtract
                                               ).then_inc(s["m_second"], 1)

            def copy_o(steps_done, done):
                dve.wait_ge(s["o_mm"], steps_done)
                if not (isinstance(done, int) and done == 0):
                    dve.wait_ge(s["o_turned"], done)
                for c in range(2):
                    nc.vector.tensor_copy(o_t[:, c * CH:(c + 1) * CH], ps_o[0:VW, c * CH:(c + 1) * CH]).then_inc(s["o_copied"], 1)

            def normalise(hd, half, done):
                dve.wait_ge(s["o_turned"], done + 1)
                dve.wait_ge(s["o_read"], done)
                nc.vector.reciprocal(rden[:, :, :], o_nat[:, :, DH1:DH1 + 1]).then_inc(s["own_dve"], 1)
                dve.wait_ge(s["own_dve"], done + 1)
                nc.vector.tensor_tensor(y[:, half * JT:(half + 1) * JT, bass.ds(hd * DH1, DH1)], o_nat[:, :, 0:DH1],
                                        rden[:, :, :].to_broadcast([P, JT, DH1]), ALU.mult).then_inc(s["o_read"], 1)

            def what_is_left(hd, st):
                dve.wait_ge(s["a_done"], hd * STEPS + st + 1)
                if not (isinstance(hd, int) and hd == 0 and st < 2):
                    dve.wait_ge(s["o_mm"], hd * STEPS + st - 1)
                nc.vector.tensor_tensor(prob_b[st % 2][:, 0:DVE_COLS], prob[st % SLOTS][:, 0:DVE_COLS],
                                        prob_a[st % 2][:, 0:DVE_COLS].bitcast(F32), ALU.subtract).then_inc(s["b_done_dve"], 1)

            def head(hd, slot, first, last):
                for st in range(STEPS):
                    if st:
                        what_is_left(hd, st - 1)
                    elif not first:
                        what_is_left(hd - 1, STEPS - 1)
                    if st == 1 and not first:
                        copy_o(hd * STEPS, hd * 2 - 1)
                    if st == 2 and not first:
                        normalise(hd - 1, 1, hd * 2 - 1)
                    if st == QT + 1:
                        copy_o(hd * STEPS + QT, hd * 2)
                    tiles = [] if last else max_tiles(st)
                    for i in tiles:
                        reduce(hd + 1, i)
                    if NMAX - 1 in tiles:
                        all_max(hd + 1)
                    if st == TURN_MAX and not last:
                        second_part(hd + 1)
                    if st == TURN_0 + 1:
                        normalise(hd, 0, hd * 2)
                if last:
                    what_is_left(hd, STEPS - 1)
                    copy_o(HEADS * STEPS, hd * 2 + 1)
                    normalise(hd, 1, hd * 2 + 1)

            for t in range(2):
                nc.vector.memset(q_st[t][3 * DH1:ROWS, :].bitcast(F32), 1.0)
                nc.vector.memset(k_st[t][3 * DH1:ROWS, :].bitcast(F32), 1.0).then_inc(s["stack_free"], 1)
            for i in range(NMAX):
                reduce(0, i)
            all_max(0)
            second_part(0)
            each_head(dve, head)


def stage_out(nc, a, keep, film, w_name, b_name, y, src, out):
    with ExitStack() as ctx:
        r = Room(nc, ctx, f"out{film}")
        m = Norm(r, keep)
        w = r.sb("w", [P, KD, D])
        bias = r.sb("bias", [P, D])
        x_res = r.sb("x_res", [P, 4, D])
        bank = [r.ps(f"bank{i}", [P, CH]) for i in range(4)]
        names = "weights_in residual_in o_mm biased out_done stored own_dve"
        s = {n: r.sem(n) for n in names.split()}
        fa, fb = keep["film"][:, film, 0], keep["film"][:, film, 1]
        block = ctx.enter_context(nc.Block())

        @block.sync
        def _(sp):
            sp.dma_start(w[:, :, :], a[w_name].rearrange("(k p) n -> p k n", p=P)).then_inc(s["weights_in"], 16)
            sp.dma_start(bias[:, :], row_on_all(a[b_name])).then_inc(s["weights_in"], 16)
            with sp.Fori(0, NCH) as it:
                sp.wait_ge(s["stored"], it * 16 * TT)
                sp.dma_start(x_res[:, :, :], src[bass.ds(it * CH, CH), :].rearrange("(t p) d -> p t d", p=P)).then_inc(s["residual_in"], 16)
                for t in range(TT):
                    sp.wait_ge(s["out_done"], it * TT + t + 1)
                    sp.dma_start(out[bass.ds(it * CH + t * P, P), :], x_res[:, t, :]).then_inc(s["stored"], 16)
            sp.wait_ge(s["stored"], NCH * TT * 16)

        @block.gpsimd
        def _(pool):
            with pool.Fori(0, NCH) as it:
                norm_pool(nc, pool, m, it)

        @block.tensor
        def _(pe):
            pe.wait_ge(s["weights_in"], 32)
            with pe.Fori(0, NCH) as it:
                norm_pe(nc, pe, m, it)
                pe.wait_ge(m.turned, (it + 1) * KD)
                for t in range(TT):
                    pe.wait_ge(s["out_done"], it * TT)
                    for k in range(KD):
                        mm = nc.tensor.matmul(bank[t][:, :], m.xn_t[:, k, t * P:(t + 1) * P], w[:, k, :],
                                              start=(k == 0), stop=(k == KD - 1))
                    mm.then_inc(s["o_mm"], 1)

        @block.scalar
        def _(act):
            with act.Fori(0, NB) as b, act.Fori(0, NC_B) as c:
                it = b * NC_B + c
                act.wait_ge(s["o_mm"], it * TT)
                norm_act(nc, act, m, it, ACT.Silu, lambda k: fa[:, k, bass.ds(b, 1)], lambda k: fb[:, k, bass.ds(b, 1)])

        @block.vector
        def _(dve):
            dve.wait_ge(s["weights_in"], 32)
            with dve.Fori(0, NB) as b, dve.Fori(0, NC_B) as c:
                it = b * NC_B + c
                own = Chain(dve, s["own_dve"], it, DVE_NORM)
                norm_dve(nc, dve, m, own, it, lambda t: y[:, bass.ds(c * TT + t, 1), bass.ds(b * D, D)].rearrange("p a d -> p (a d)"))
                for t in range(TT):
                    dve.wait_ge(s["o_mm"], it * TT + t + 1)
                    nc.vector.tensor_tensor(bank[t][:, :], bank[t][:, :], bias[:, :], ALU.add).then_inc(s["biased"], 1)
                    dve.wait_ge(s["biased"], it * TT + t + 1)
                    dve.wait_ge(s["residual_in"], (it + 1) * 16)
                    nc.vector.tensor_tensor(x_res[:, t, :], bank[t][:, :], x_res[:, t, :], ALU.add).then_inc(s["out_done"], 1)
                own.end()



def stage_linear(nc, a, keep, layer, heads, names_of, int_mask, over_v, src, out):
    with ExitStack() as ctx:
        r = Room(nc, ctx, f"lin{layer}")
        dh = D // heads
        ident = keep["ident"]
        tb = [r.ps(f"turn_bank{i}", [P, CH]) for i in range(4)]
        mb = [r.ps(f"mm_bank{i}", [P, CH]) for i in range(4)]
        m1 = Norm(r, keep, tb)
        m2 = Norm(Room(nc, ctx, f"lin{layer}_out"), keep, tb)
        w = [r.sb(f"w_{n}", [P, KD, D]) for n in ("q", "k", "v", "out")]
        rows = r.sb("bias_rows", [P, 3, D])
        k_t = r.sb("k_t", [P, KD, S])
        q_t = r.sb("q_t", [P, KD, S])
        v_all = r.sb("v_all", [P, QT, D])
        q = r.sb("q", [P, TT, D])
        q_red = r.sb("q_red", [P, TT * heads])
        q_den = r.sb("q_den", [P, TT * heads])
        vb = r.sb("vb", [P, 2, D])
        mask_row = r.sb("mask_row", [P, CH], I32 if int_mask else F32)
        mask_add = r.sb("mask_add", [P, CH])
        mask_in = r.sb("mask_in", [P, NT], I32 if int_mask else F32)
        mask_col = r.sb("mask_col", [P, NT])
        k_max = r.sb("k_max", [P, KD])
        k_sum = r.sb("k_sum", [P, KD])
        k_rec = r.sb("k_rec", [P, KD])
        kn = r.sb("kn", [P, 4, D])
        blocks = r.sb("blocks", [P, P])
        kv = r.sb("kv", [P, KD, P])
        x_res = r.sb("x_res", [P, TT, D])
        names = ("weights_in small_in blocks_set mask_set q_mm q_biased q_max q_exp q_done q_turned qt_done k_mm k_done v_mm "
                 "v_biased v_done mask_loaded mask_made kmax_done kexp_done k_scaled k_turned kn_act kn_dve kv_mm kv_done y_mm "
                 "o_mm biased out_done residual_in stored own_dve own2_dve")
        s = {n: r.sem(n) for n in names.split()}
        cols = keep["cols"]
        g, bvec, k_bias = (column(cols, names_of[n]) for n in ("norm_w", "norm_b", "bk"))
        fa, fb = keep["film"][:, layer, 0], keep["film"][:, layer, 1]
        mask_name = "mask_BxS_ik0" if int_mask else "mask_BxSx1_fk1"
        mask_flat = a[mask_name].rearrange("b s -> (b s)") if int_mask else a[mask_name].rearrange("b s o -> (b s o)")
        block = ctx.enter_context(nc.Block())

        @block.sync
        def _(sp):
            for i, n in enumerate(("Wq", "Wk", "Wv", "Wo")):
                sp.dma_start(w[i][:, :, :], a[names_of[n]].rearrange("(k p) n -> p k n", p=P)).then_inc(s["weights_in"], 16)
            with sp.Fori(0, NB) as b:
                with sp.Fori(0, NC_B) as c:
                    it = b * NC_B + c
                    norm_load(sp, m1, src, it)
                    sp.wait_ge(s["weights_in"], 64)
                    sp.wait_ge(s["mask_made"], it)
                    sp.dma_start(mask_row[:, :], row_on_all(mask_flat[bass.ds(it * CH, CH)])).then_inc(s["mask_loaded"], 16)
                for c in range(NC_B):
                    it = b * NC_B + c
                    sp.wait_ge(s["stored"], it * 16)
                    sp.dma_start(x_res[:, :, :], src[bass.ds(it * CH, CH), :].rearrange("(t p) d -> p t d", p=P)).then_inc(s["residual_in"], 16)
                    sp.wait_ge(s["out_done"], (it + 1) * TT)
                    sp.dma_start(out[bass.ds(it * CH, CH), :].rearrange("(t p) d -> p t d", p=P), x_res[:, :, :]).then_inc(s["stored"], 16)
            sp.wait_ge(s["stored"], NCH * 16)

        @block.gpsimd
        def _(pool):
            nc.gpsimd.memset(blocks[:, :], 0.0).then_inc(s["blocks_set"], 1)
            pool.wait_ge(s["blocks_set"], 1)
            for i in range(P // dh):
                nc.gpsimd.memset(blocks[i * dh:(i + 1) * dh, i * dh:(i + 1) * dh], 1.0).then_inc(s["blocks_set"], 1)
            with pool.Fori(0, NB) as b:
                with pool.Fori(0, NC_B) as c:
                    norm_pool(nc, pool, m1, b * NC_B + c)
                with pool.Fori(0, NC_B) as c:
                    norm_pool(nc, pool, m2, b * NC_B + c)

        @block.tensor
        def _(pe):
            pe.wait_ge(s["weights_in"], 64)
            with pe.Fori(0, NB) as b:
                with pe.Fori(0, NC_B) as c:
                    it = b * NC_B + c
                    pe.wait_ge(s["out_done"], b * NC_B * TT)
                    pe.wait_ge(s["qt_done"], it * KD)
                    norm_pe(nc, pe, m1, it)
                    pe.wait_ge(m1.turned, (it + 1) * KD)
                    for which, used, made, read in ((0, (0, 1), "q_mm", "q_biased"), (2, (2, 3), "v_mm", "v_biased")):
                        for t in range(TT):
                            pe.wait_ge(s[read], it * TT + max(t - 1, 0))
                            if which == 0 and t < 2:
                                pe.wait_ge(s["k_done"], it * KD)
                            for k in range(KD):
                                mm = nc.tensor.matmul(mb[used[t % 2]][:, :], m1.xn_t[:, k, t * P:(t + 1) * P], w[which][:, k, :],
                                                      start=(k == 0), stop=(k == KD - 1))
                            mm.then_inc(s[made], 1)
                    for mt in range(KD):
                        if mt == 0:
                            pe.wait_ge(s["q_biased"], (it + 1) * TT)
                        pe.wait_ge(s["k_done"], it * KD + max(mt - 1, 0))
                        for k in range(KD):
                            mm = nc.tensor.matmul(mb[mt % 2][:, :], w[1][:, k, mt * P:(mt + 1) * P], m1.xn_t[:, k, :],
                                                  start=(k == 0), stop=(k == KD - 1))
                        mm.then_inc(s["k_mm"], 1)
                    pe.wait_ge(s["q_done"], it + 1)
                    for k in range(KD):
                        for t in range(TT):
                            mm = nc.tensor.transpose(tb[k][:, t * P:(t + 1) * P], q[:, t, k * P:(k + 1) * P], ident[:, :])
                        mm.then_inc(s["q_turned"], 1)
                pe.wait_ge(s["qt_done"], (b + 1) * NC_B * KD)
                pe.wait_ge(s["k_done"], (b + 1) * NC_B * KD)
                pe.wait_ge(s["v_done"], (b + 1) * QT)
                pe.wait_ge(s["kexp_done"], (b + 1) * KD)
                if over_v:
                    pe.wait_ge(s["k_scaled"], (b + 1) * KD)

                def turn_k(tt):
                    if tt >= 4:
                        pe.wait_ge(s["kn_dve" if tt % 2 else "kn_act"], b * (QT // 2) + tt // 2 - 1)
                    for mt in range(KD):
                        mm = nc.tensor.transpose(tb[tt % 4][:, mt * P:(mt + 1) * P], k_t[:, mt, tt * P:(tt + 1) * P], ident[:, :])
                    mm.then_inc(s["k_turned"], 1)

                turn_k(0)
                turn_k(1)
                for tt in range(QT):
                    if tt + 2 < QT:
                        turn_k(tt + 2)
                    pe.wait_ge(s["kn_dve" if tt % 2 else "kn_act"], b * (QT // 2) + tt // 2 + 1)
                    for mt in range(KD):
                        k_part = kn[:, tt % 4, mt * P:(mt + 1) * P]
                        v_part = v_all[:, tt, mt * P:(mt + 1) * P]
                        mm = nc.tensor.matmul(mb[0][:, mt * P:(mt + 1) * P], v_part if over_v else k_part,
                                              k_part if over_v else v_part, start=(tt == 0 and mt == 0),
                                              stop=(tt == QT - 1), skip_group_check=True)
                    mm.then_inc(s["kv_mm"], 1)
                pe.wait_ge(s["kv_done"], (b + 1) * KD)
                for c in range(NC_B):
                    it = b * NC_B + c
                    pe.wait_ge(s["out_done"], it * TT)
                    for t in range(TT):
                        for mt in range(KD):
                            mm = nc.tensor.matmul(mb[t][:, mt * P:(mt + 1) * P], q_t[:, mt, c * CH + t * P:c * CH + (t + 1) * P],
                                                  kv[:, mt, :], start=True, stop=True)
                        mm.then_inc(s["y_mm"], 1)
                    norm_pe(nc, pe, m2, it)
                    pe.wait_ge(m2.turned, (it + 1) * KD)
                    for t in range(TT):
                        for k in range(KD):
                            mm = nc.tensor.matmul(mb[t][:, :], m2.xn_t[:, k, t * P:(t + 1) * P], w[3][:, k, :],
                                                  start=(k == 0), stop=(k == KD - 1))
                        mm.then_inc(s["o_mm"], 1)

        @block.scalar
        def _(act):
            act.dma_start(mask_in[:, :], a["mask_ik0_columns" if int_mask else "mask_fk1_columns"]).then_inc(s["small_in"], 16)
            for i, n in enumerate(("bq", "bv", "bo")):
                act.dma_start(rows[:, i, :], row_on_all(a[names_of[n]])).then_inc(s["small_in"], 16)
            act.wait_ge(s["mask_set"], 1)
            with act.Fori(0, NB) as b:
                with act.Fori(0, NC_B) as c:
                    it = b * NC_B + c
                    act.wait_ge(s["k_mm"], it * KD)
                    norm_act(nc, act, m1, it, ACT.Identity, lambda k: g[:, k:k + 1], lambda k: bvec[:, k:k + 1])
                    act.wait_ge(s["q_max"], it + 1)
                    nc.scalar.activation(q[:, :, :], q[:, :, :], ACT.Exp).then_inc(s["q_exp"], 1)
                    act.wait_ge(s["kv_mm"], b * QT)
                    for t in range(TT):
                        act.wait_ge(s["v_biased"], it * TT + t + 1)
                        nc.scalar.activation(v_all[:, bass.ds(c * TT + t, 1), :].rearrange("p a d -> p (a d)"), vb[:, t % 2, :], ACT.Copy,
                                             scale=mask_col[:, bass.ds(it * TT + t, 1)]).then_inc(s["v_done"], 1)
                    for k in range(KD):
                        act.wait_ge(s["q_turned"], it * KD + k + 1)
                        nc.scalar.activation(q_t[:, k, bass.ds(c * CH, CH)], tb[k][:, :], ACT.Copy).then_inc(s["qt_done"], 1)
                for mt in range(KD):
                    act.wait_ge(s["kmax_done"], b * KD + mt + 1)
                    nc.scalar.activation(k_t[:, mt, :], k_t[:, mt, :], ACT.Exp, bias=k_max[:, mt:mt + 1],
                                         accum_out=k_sum[:, mt:mt + 1]).then_inc(s["kexp_done"], 1)
                for tt in range(0, QT, 2):
                    act.wait_ge(s["k_turned"], b * QT + tt + 1)
                    if tt >= 4:
                        act.wait_ge(s["kv_mm"], b * QT + tt - 3)
                    nc.scalar.activation(kn[:, tt % 4, :], tb[tt % 4][:, :], ACT.Copy).then_inc(s["kn_act"], 1)
                with act.Fori(0, NC_B) as c:
                    it = b * NC_B + c
                    act.wait_ge(s["o_mm"], it * TT)
                    norm_act(nc, act, m2, it, ACT.Silu, lambda k: fa[:, k, bass.ds(b, 1)], lambda k: fb[:, k, bass.ds(b, 1)])

        @block.vector
        def _(dve):
            dve.wait_ge(s["small_in"], 64)
            if int_mask:
                nc.vector.tensor_scalar(mask_col[:, :], mask_in[:, :], 1.0, None, ALU.not_equal).then_inc(s["mask_set"], 1)
            else:
                nc.vector.tensor_copy(mask_col[:, :], mask_in[:, :]).then_inc(s["mask_set"], 1)
            dve.wait_ge(s["blocks_set"], 1 + P // dh)
            with dve.Fori(0, NB) as b:
                with dve.Fori(0, NC_B) as c:
                    it = b * NC_B + c
                    own = Chain(dve, s["own_dve"], it, DVE_NORM + 3)
                    dve.wait_ge(m1.x_loaded, (it + 1) * 16)
                    norm_dve(nc, dve, m1, own, it, lambda t: m1.x[:, t, :])
                    dve.wait_ge(s["mask_loaded"], (it + 1) * 16)
                    dve.wait_ge(s["k_done"], it * KD)
                    if int_mask:
                        nc.vector.tensor_scalar(mask_add[:, :], mask_row[:, :], 1.0, -3.0e38, ALU.is_equal, ALU.mult).then_inc(s["mask_made"], 1)
                    else:
                        nc.vector.tensor_scalar(mask_add[:, :], mask_row[:, :], 1e6, -1e6, ALU.mult, ALU.add).then_inc(s["mask_made"], 1)
                    dve.wait_ge(s["q_turned"], it * KD)
                    for t in range(TT):
                        dve.wait_ge(s["q_mm"], it * TT + t + 1)
                        nc.vector.tensor_tensor(q[:, t, :], mb[t % 2][:, :], rows[:, 0, :], ALU.add).then_inc(s["q_biased"], 1)
                    heads_view = q[:, :, :].rearrange("p t (h e) -> p (t h) e", e=dh)
                    wide = lambda v: v[:, :].unsqueeze(2).to_broadcast([P, TT * heads, dh])
                    dve.wait_ge(s["q_biased"], (it + 1) * TT)
                    own.inc(nc.vector.tensor_reduce(q_red[:, :], heads_view, AX.X, ALU.max))
                    own.wait()
                    nc.vector.tensor_tensor(heads_view, heads_view, wide(q_red), ALU.subtract).then_inc(s["q_max"], 1)
                    for t in range(TT):
                        dve.wait_ge(s["v_mm"], it * TT + t + 1)
                        dve.wait_ge(s["v_done"], it * TT + max(t - 1, 0))
                        nc.vector.tensor_tensor(vb[:, t % 2, :], mb[2 + t % 2][:, :], rows[:, 1, :], ALU.add).then_inc(s["v_biased"], 1)
                        if t == 1:
                            dve.wait_ge(s["q_exp"], it + 1)
                            own.inc(nc.vector.tensor_reduce(q_den[:, :], heads_view, AX.X, ALU.add))
                            own.wait()
                            own.inc(nc.vector.reciprocal(q_den[:, :], q_den[:, :]))
                            own.wait()
                            nc.vector.tensor_tensor(heads_view, heads_view, wide(q_den), ALU.mult).then_inc(s["q_done"], 1)
                    dve.wait_ge(s["mask_made"], it + 1)
                    for mt in range(KD):
                        dve.wait_ge(s["k_mm"], it * KD + mt + 1)
                        nc.vector.scalar_tensor_tensor(out=k_t[:, mt, bass.ds(c * CH, CH)], in0=mb[mt % 2][:, :], scalar=k_bias[:, mt:mt + 1],
                                                       in1=mask_add[:, :], op0=ALU.add, op1=ALU.add).then_inc(s["k_done"], 1)
                    own.end()
                own = Chain(dve, s["own2_dve"], b, KD + 1 + 2 * NC_B)
                dve.wait_ge(s["k_done"], (b + 1) * NC_B * KD)
                for mt in range(KD):
                    own.inc(nc.vector.tensor_reduce(k_max[:, mt:mt + 1], k_t[:, mt, :], AX.X, ALU.max))
                    own.wait()
                    nc.vector.tensor_scalar(k_max[:, mt:mt + 1], k_max[:, mt:mt + 1], -1.0, None, ALU.mult).then_inc(s["kmax_done"], 1)
                dve.wait_ge(s["kexp_done"], (b + 1) * KD)
                own.inc(nc.vector.reciprocal(k_rec[:, :], k_sum[:, :]))
                own.wait()
                for mt in range(KD if over_v else 0):
                    nc.vector.tensor_scalar(k_t[:, mt, :], k_t[:, mt, :], k_rec[:, mt:mt + 1], None, ALU.mult).then_inc(s["k_scaled"], 1)
                for tt in range(1, QT, 2):
                    dve.wait_ge(s["k_turned"], b * QT + tt + 1)
                    if tt >= 4:
                        dve.wait_ge(s["kv_mm"], b * QT + tt - 3)
                    nc.vector.tensor_copy(kn[:, tt % 4, :], tb[tt % 4][:, :]).then_inc(s["kn_dve"], 1)
                dve.wait_ge(s["kv_mm"], (b + 1) * QT)
                own.wait()
                for mt in range(KD):
                    nc.vector.scalar_tensor_tensor(out=kv[:, mt, :], in0=mb[0][:, mt * P:(mt + 1) * P],
                                                   scalar=1.0 if over_v else k_rec[:, mt:mt + 1],
                                                   in1=blocks[:, :], op0=ALU.mult, op1=ALU.mult).then_inc(s["kv_done"], 1)
                for c in range(NC_B):
                    it = b * NC_B + c
                    dve.wait_ge(s["y_mm"], (it + 1) * TT)
                    norm_dve(nc, dve, m2, own, it, lambda t: mb[t][:, :])
                    for t in range(TT):
                        dve.wait_ge(s["o_mm"], it * TT + t + 1)
                        nc.vector.tensor_tensor(mb[t][:, :], mb[t][:, :], rows[:, 2, :], ALU.add).then_inc(s["biased"], 1)
                        dve.wait_ge(s["biased"], it * TT + t + 1)
                        dve.wait_ge(s["residual_in"], (it + 1) * 16)
                        nc.vector.tensor_tensor(x_res[:, t, :], mb[t][:, :], x_res[:, t, :], ALU.add).then_inc(s["out_done"], 1)
                own.end()


NAMES2 = {"norm_w": "L2_cond_norm_scale", "norm_b": "L2_cond_norm_bias", "Wq": "L2_cond_Wq", "Wk": "L2_cond_Wk", "Wv": "L2_cond_Wv",
          "Wo": "L2_cond_film_out_W", "bq": "L2_cond_bq", "bk": "L2_cond_bk", "bv": "L2_cond_bv", "bo": "L2_cond_film_out_b"}
NAMES3 = {"norm_w": "L3_cond_ln_w", "norm_b": "L3_cond_ln_b", "Wq": "L3_cond_Wq", "Wk": "L3_cond_Wk", "Wv": "L3_cond_Wv",
          "Wo": "L3_cond_W_out", "bq": "L3_cond_bq", "bk": "L3_cond_bk", "bv": "L3_cond_bv", "bo": "L3_cond_b_out"}


def build(nc, a, out):
    with ExitStack() as ctx:
        def sb(name, shape):
            return ctx.enter_context(nc.sbuf_tensor(name, shape, F32))

        def dram(name, shape):
            return nc.dram_tensor(name, shape, F32, kind="Internal").ap()

        keep = {"cols": sb("cols", [P, NCOLS]),
                "film": sb("film", [P, NB * 2, 2, KD, NB]),
                "gate": sb("gate", [P, NB, D]),
                "ident": sb("ident", [P, P]),
                "neg_half": sb("neg_half", [P, TT])}
        x1, x2, x3 = (dram(f"x_after_L{i}", [NB * S, D]) for i in range(3))
        qk_parts = dram("qk_parts", [2, 2, D, NB * S])
        mask_parts = dram("mask_parts", [2, NB * S])
        max_rows = dram("max_rows", [2, 2, S])
        stage_condition(nc, a, keep)
        stage_mamba(nc, a, keep, x1)
        with ExitStack() as for_y:
            y = for_y.enter_context(nc.sbuf_tensor("y", [P, QT, NB * D], F32))
            with ExitStack() as for_v:
                v = for_v.enter_context(nc.sbuf_tensor("v", [P, QT, NB * D], F32))
                stage_qkv(nc, a, keep, x1, qk_parts, mask_parts, v)
                stage_attention(nc, a, keep, qk_parts, mask_parts, max_rows, v, y)
            stage_out(nc, a, keep, 1, "L1_cond_out_w", "L1_cond_out_b", y, x1, x2)
        stage_linear(nc, a, keep, 2, 16, NAMES2, True, True, x2, x3)
        stage_linear(nc, a, keep, 3, 8, NAMES3, False, False, x3, out.rearrange("b s d -> (b s) d"))


def kernel(**inputs):
    import numpy as np
    import concourse.bacc as bacc
    from concourse.bass_utils import run_bass_kernel_spmd

    def as_columns(v):
        v = np.asarray(v)
        return np.ascontiguousarray(v.reshape(-1, P, *v.shape[1:]).swapaxes(0, 1).reshape(P, -1))

    sent = {name: np.asarray(v) for name, v in inputs.items()}
    sent["cond_T"] = sent.pop("cond_2048").T
    sent["ada_w_T"] = sent.pop("L0_cond_ada_w").T
    for name in ("in_proj_w", "x_proj_w", "dt_proj_w", "out_proj_w"):
        sent[f"{name}_T"] = sent.pop(f"L0_cond_{name}").T
    sent["columns"] = np.concatenate([as_columns(sent[name]) for name, _ in COLUMNS], axis=1)
    for name, _ in COLUMNS:
        if name != "L0_cond_ada_b":
            del sent[name]
    sent["mask_ff1_columns"] = as_columns(sent["mask_BxS_ff1"].reshape(-1))
    sent["mask_ik0_columns"] = as_columns(sent["mask_BxS_ik0"].reshape(-1))
    sent["mask_fk1_columns"] = as_columns(sent["mask_BxSx1_fk1"].reshape(-1))

    nc = bacc.Bacc("TRN2", target_bir_lowering=False, num_devices=1)
    arrays, a = {}, {}
    for name, v in sent.items():
        v = np.ascontiguousarray(v)
        arrays[f"in_{name}"] = v
        a[name] = nc.dram_tensor(f"in_{name}", v.shape, mybir.dt.from_np(v.dtype), kind="ExternalInput").ap()
    out = nc.dram_tensor("out", (NB, S, D), F32, kind="ExternalOutput").ap()
    build(nc, a, out)
    r = run_bass_kernel_spmd(nc, [arrays], core_ids=[0])
    return r.results[0]["out"]
```

```python
from contextlib import ExitStack

import concourse.bass as bass
from concourse import mybir

F32 = mybir.dt.float32
F32R = mybir.dt.float32r
I32 = mybir.dt.int32
ACT = mybir.ActivationFunctionType
ALU = mybir.AluOpType
AX = mybir.AxisListType

P = 128
NB = 2
S = 2048
D = 512
KD = D // P
CH = 512
NC_B = S // CH
NCH = NB * NC_B
TT = CH // P
DI = 1024
CT = DI // P
N = 16
RANK = 64
CONV = 4
CW = 1024
KC = CW // P
EPS = 1e-5


class Chain:

    def __init__(self, engine, sem, base, per):
        self.engine, self.sem, self.base, self.per, self.n = engine, sem, base, per, 0

    def inc(self, ins):
        ins.then_inc(self.sem, 1)
        self.n += 1

    def wait(self):
        self.engine.wait_ge(self.sem, self.so_far())

    def so_far(self):
        return self.base * self.per + self.n

    def end(self):
        assert self.n == self.per, (self.sem, self.n, self.per)


class Room:

    def __init__(self, nc, ctx, stage):
        self.nc, self.ctx, self.stage, self.sems = nc, ctx, stage, []
        ctx.callback(self.close)

    def sb(self, name, shape, dt=F32):
        return self.ctx.enter_context(self.nc.sbuf_tensor(f"{self.stage}_{name}", shape, dt))

    def ps(self, name, shape, dt=F32):
        return self.ctx.enter_context(self.nc.psum_tensor(f"{self.stage}_{name}", shape, dt))

    def sem(self, name):
        self.sems.append(self.nc.alloc_semaphore(f"{self.stage}_{name}"))
        return self.sems[-1]

    def close(self):
        self.nc.clear_and_free_semaphores(self.sems)
        self.nc.all_engine_barrier()


COLUMNS = [("L0_cond_ln_g", KD), ("L0_cond_ln_b", KD), ("L0_cond_ada_b", 3 * KD), ("L0_cond_conv_b", CT),
           ("L0_cond_dt_proj_b", CT), ("L0_cond_D_param", CT), ("L0_cond_conv_w", CT * CONV), ("L0_cond_A_log", CT * N),
           ("L1_cond_norm_w", KD), ("L1_cond_norm_b", KD), ("L1_cond_q_b", KD), ("L1_cond_k_b", KD),
           ("L1_cond_emb_b", 2 * KD), ("L1_cond_sb_norm_w", KD), ("L1_cond_sb_norm_b", KD),
           ("L2_cond_norm_scale", KD), ("L2_cond_norm_bias", KD), ("L2_cond_bk", KD),
           ("L2_cond_film_emb_b", 2 * KD), ("L2_cond_film_norm_scale", KD), ("L2_cond_film_norm_bias", KD),
           ("L3_cond_ln_w", KD), ("L3_cond_ln_b", KD), ("L3_cond_bk", KD),
           ("L3_cond_b_emb", 2 * KD), ("L3_cond_ln2_w", KD), ("L3_cond_ln2_b", KD)]
NCOLS = sum(w for _, w in COLUMNS)


def column(cols, name, first=0, count=None):
    at = 0
    for other, width in COLUMNS:
        if other == name:
            return cols[:, at + first:at + (width if count is None else first + count)]
        at += width
    raise KeyError(name)


def row_on_all(vec, parts=P):
    return bass.AP(tensor=vec.tensor, offset=vec.offset, ap=[[0, parts], [1, vec.shape[0]]])


def make_identity(pool, ident, done):
    pool.memset(ident[:, :], 0.0).then_inc(done, 1)
    pool.wait_ge(done, 1)
    pool.affine_select(out=ident[:, :], in_=ident[:, :], compare_op=ALU.not_equal, fill=1.0, base=0,
                       pattern=[[-1, P]], channel_multiplier=1).then_inc(done, 1)


FILMS = [("ada_w_T", "L0_cond_ada_b", "L0_cond_ln_g", "L0_cond_ln_b"),
         ("L1_cond_emb_w", "L1_cond_emb_b", "L1_cond_sb_norm_w", "L1_cond_sb_norm_b"),
         ("L2_cond_film_emb_W", "L2_cond_film_emb_b", "L2_cond_film_norm_scale", "L2_cond_film_norm_bias"),
         ("L3_cond_W_emb", "L3_cond_b_emb", "L3_cond_ln2_w", "L3_cond_ln2_b")]


class Film:

    def __init__(self, r, keep, layer, w, bank):
        self.keep, self.layer, self.w = keep, layer, w
        self.ps = bank[:, 0:2 * KD * NB].rearrange("p (t b) -> p t b", b=NB)
        self.proj = r.sb(f"film{layer}_proj", [P, 2, KD, NB])
        self.loaded, self.made, self.biased, self.folded = (
            r.sem(f"film{layer}_{n}") for n in ("loaded", "made", "biased", "folded"))


def film_load(sp, f, a):
    sp.dma_start(f.w, a[FILMS[f.layer][0]].rearrange("(k p) n -> p k n", p=P)).then_inc(f.loaded, 16)


def film_pe(nc, pe, f):
    pe.wait_ge(f.loaded, 16)
    silu = f.keep["silu"]
    for t in range(2 * KD):
        for k in range(KC):
            mm = nc.tensor.matmul(f.ps[:, t, :], f.w[:, k, t * P:(t + 1) * P], silu[:, k, :],
                                  start=(k == 0), stop=(k == KC - 1))
    mm.then_inc(f.made, 1)


def film_dve(nc, dve, f):
    _, bias, norm_w, norm_b = FILMS[f.layer]
    cols, col = f.keep["cols"], f.keep["film"][:, f.layer]
    on_batches = lambda v: v.unsqueeze(2).to_broadcast([P, KD, NB])
    dve.wait_ge(f.made, 1)
    for part in range(2):
        slot = part if f.layer else 1 - part
        nc.vector.tensor_tensor(f.proj[:, slot, :, :], f.ps[:, part * KD:(part + 1) * KD, :],
                                on_batches(column(cols, bias, part * KD, KD)), ALU.add).then_inc(f.biased, 1)
    dve.wait_ge(f.biased, 2)
    nc.vector.tensor_scalar(f.proj[:, 0, :, :], f.proj[:, 0, :, :], 1.0, None, ALU.add).then_inc(f.folded, 1)
    dve.wait_ge(f.folded, 1)
    nc.vector.tensor_tensor(col[:, 0, :, :], f.proj[:, 0, :, :], on_batches(column(cols, norm_w)), ALU.mult)
    nc.vector.tensor_tensor(col[:, 1, :, :], f.proj[:, 0, :, :], on_batches(column(cols, norm_b)), ALU.mult).then_inc(f.folded, 1)
    dve.wait_ge(f.folded, 2)
    nc.vector.tensor_tensor(col[:, 1, :, :], col[:, 1, :, :], f.proj[:, 1, :, :], ALU.add).then_inc(f.folded, 1)
    dve.wait_ge(f.folded, 3)


def stage_condition(nc, a, keep):
    with ExitStack() as ctx:
        r = Room(nc, ctx, "cond")
        cond = r.sb("cond", [P, KC, NB])
        ada_w = r.sb("ada_w", [P, KC, 3 * D])
        gate_b = r.sb("gate_b", [P, D])
        film = Film(r, keep, 0, ada_w[:, :, :], r.ps("bank", [P, D]))
        ps_gate = [r.ps(f"ps_gate{i}", [P, D]) for i in range(NB)]
        cond_in, small_in, silu_done, gate_done = (r.sem(x) for x in ("cond_in", "small_in", "silu_done", "gate_done"))
        silu = keep["silu"]
        block = ctx.enter_context(nc.Block())

        @block.sync
        def _(sp):
            sp.dma_start(cond[:, :, :], a["cond_T"].rearrange("(k p) b -> p k b", p=P)).then_inc(cond_in, 16)
            film_load(sp, film, a)

        @block.scalar
        def _(act):
            act.dma_start(keep["cols"][:, :], a["columns"]).then_inc(small_in, 16)
            act.dma_start(gate_b[:, :], row_on_all(a["L0_cond_ada_b"][2 * D:3 * D])).then_inc(small_in, 16)
            act.wait_ge(cond_in, 16)
            nc.scalar.activation(silu[:, :, :], cond[:, :, :], ACT.Silu).then_inc(silu_done, 1)

        @block.tensor
        def _(pe):
            pe.wait_ge(silu_done, 1)
            film_pe(nc, pe, film)
            for b in range(NB):
                for k in range(KC):
                    mm = nc.tensor.matmul(ps_gate[b][:, :], silu[:, k, b:b + 1].to_broadcast([P, P]),
                                          ada_w[:, k, 2 * D:3 * D], start=(k == 0), stop=(k == KC - 1))
            mm.then_inc(gate_done, 1)

        @block.vector
        def _(dve):
            dve.wait_ge(small_in, 16 * 2)
            film_dve(nc, dve, film)
            dve.wait_ge(gate_done, 1)
            for b in range(NB):
                nc.vector.tensor_tensor(keep["gate"][:, b, :], ps_gate[b][:, :], gate_b[:, :], ALU.add)

        @block.gpsimd
        def _(pool):
            make_identity(pool, keep["ident"], r.sem("ident_done"))
            nc.gpsimd.memset(keep["neg_half"][:, :], -0.5)


def stage_mamba(nc, a, keep, out):
    with ExitStack() as ctx:
        r = Room(nc, ctx, "mamba")
        G = 2
        NG = N // G
        CG = CT * NG
        BC_ROWS = 2 * N
        SLOTS = 3
        OUT_STEPS = {1 + 3 * t: t for t in range(TT)}
        Z_STEPS = {22 + 6 * p: (2 * p, 2 * p + 1) for p in range(CT // 2)}
        READ = 2
        GATE_STEPS = [max(NG * (e + 1) + READ + 2, i + 8) for i, es in Z_STEPS.items() for e in es][:CT - 1]
        STATS, RSTD, NORMED, TURN = 36, 39, 42, 47
        OUT_BEHIND = 9
        BEHIND = 5
        w_u = r.sb("w_u", [P, KD, DI])
        w_zo = r.sb("w_zo", [P, KD * DI])
        w_z = w_zo[:, :].rearrange("p (k n) -> p k n", k=KD)
        w_out = w_zo[:, :].rearrange("p (k n) -> p k n", k=CT)
        w_x = r.sb("w_x", [P, CT, RANK + BC_ROWS])
        w_dt = r.sb("w_dt", [RANK, DI])
        cols = keep["cols"]
        conv_w = column(cols, "L0_cond_conv_w").rearrange("p (t j) -> p t j", j=CONV)
        conv_b = column(cols, "L0_cond_conv_b")
        dt_b = column(cols, "L0_cond_dt_proj_b")
        d_par = column(cols, "L0_cond_D_param")
        a_log = column(cols, "L0_cond_A_log").rearrange("p (t n) -> p t n", n=N)
        a_neg = r.sb("a_neg", [P, CT, N])
        pick = r.sb("pick", [2 * BC_ROWS, BC_ROWS], F32R)
        x_in = r.sb("x_in", [P, TT, D])
        xn_t = r.sb("xn_t", [P, KD, CH])
        x_ext = r.sb("x_ext", [P, 2, CONV - 1 + CH])
        halo = r.sb("halo", [P, CT, CONV - 1])
        u = r.sb("u", [P, CT, CH])
        zy = r.sb("zy", [P, CT, CH])
        dt_r = r.sb("dt_r", [RANK, CH])
        bc_parts = r.sb("bc_parts", [2 * BC_ROWS, CH], F32R)
        bc = r.sb("bc", [P, BC_ROWS, CH])
        stats = r.sb("stats", [P, TT, 6])
        mv = r.sb("mv", [P, TT, 2])
        rstd = r.sb("rstd", [P, TT])
        var_eps = r.sb("var_eps", [P, TT])
        conv = r.sb("conv", [P, 2, CH])
        dt = conv
        soft = r.sb("soft", [P, CH])
        du = r.sb("du", [P, CH])
        da = r.sb("da", [P, 2, G, CH])
        da = [da[:, 0, :, :], da[:, 1, :, :], x_ext[:, :, CONV - 1:]]
        h = r.sb("h", [P, SLOTS, G, CH])
        hc = r.sb("hc", [P, SLOTS, G, CH])
        state = r.sb("state", [P, CT, N])
        film = r.sb("film", [P, 2, KD])
        bank = [r.ps(f"bank{i}", [P, CH]) for i in range(8)]
        ident, gate, neg_half = keep["ident"], keep["gate"], keep["neg_half"]
        fa, fb = keep["film"][:, 0, 0], keep["film"][:, 0, 1]
        names = ("weights_in wz_in wo_in x_loaded var_done rstd_done x_normed transposed turned in_mm ext_copied conv_done "
                 "u_done z_mm z_done x_mm part_a_done part_b_done bc_mm bc_act_done bc_dve_done dt_mm v_done soft_done dt_done "
                 "da_done h_done hc_done sum_mm y_read gated out_mm out_gated residual_in out_done stored own_dve own_norm own_act "
                 "setup_done reset_done film_set")
        s = {n: r.sem(n) for n in names.split()}
        block = ctx.enter_context(nc.Block())
        x_rows = a["x"].rearrange("b s d -> (b s) d")
        in_w = a["in_proj_w_T"].rearrange("(k p) n -> p k n", p=P)

        def each_chunk(engine, start, chunk):
            with engine.Fori(0, NB) as b:
                start(b)
                chunk(b, 0, True, True)
                with engine.Fori(0, NC_B - 2) as c:
                    chunk(b, c + 1, False, True)
                chunk(b, NC_B - 1, False, False)

        def rows(it):
            return x_rows[bass.ds(it * CH, CH), :].rearrange("(t p) d -> p t d", p=P)

        @block.sync
        def _(sp):
            def start(b):
                sp.wait_ge(s["stored"], b * NC_B * TT * 16)
                sp.dma_start(x_in[:, :, :], rows(b * NC_B)).then_inc(s["x_loaded"], 16)

            def project_back(it):
                sp.dma_start(x_in[:, :, :], rows(it)).then_inc(s["residual_in"], 16)
                for t in range(TT):
                    sp.wait_ge(s["out_done"], it * TT + t + 1)
                    sp.dma_start(out[bass.ds(it * CH + t * P, P), :], x_in[:, t, :]).then_inc(s["stored"], 16)

            def chunk(b, c, first, more):
                it = b * NC_B + c
                sp.wait_ge(s["transposed"], (it + 1) * KD)
                if not first:
                    project_back(it - 1)
                    sp.wait_ge(s["out_mm"], it * TT)
                sp.dma_start(w_z, in_w[:, :, DI:2 * DI]).then_inc(s["wz_in"], 16)
                if more:
                    sp.wait_ge(s["stored"], it * 16 * TT)
                    sp.dma_start(x_in[:, :, :], rows(it + 1)).then_inc(s["x_loaded"], 16)
                sp.wait_ge(s["z_mm"], (it + 1) * CT)
                sp.dma_start(w_out, a["out_proj_w_T"].rearrange("(k p) n -> p k n", p=P)).then_inc(s["wo_in"], 16)
                if not more:
                    sp.wait_ge(s["stored"], it * 16 * TT)
                    project_back(it)

            each_chunk(sp, start, chunk)
            sp.wait_ge(s["stored"], NCH * TT * 16)

        @block.gpsimd
        def _(pool):
            def make_rstd(it):
                pool.wait_ge(s["var_done"], it + 1)
                nc.gpsimd.tensor_tensor(rstd[:, :], var_eps[:, :], neg_half[:, 0:TT], ALU.pow).then_inc(s["rstd_done"], 1)

            def gate_y(it, ct):
                pool.wait_ge(s["y_read"], it * CT + ct + 1)
                pool.wait_ge(s["z_done"], it * CT + ct + 1)
                nc.gpsimd.tensor_tensor(zy[:, ct, :], u[:, ct, :], zy[:, ct, :], ALU.mult).then_inc(s["gated"], 1)

            def chunk(b, c, first, more):
                it = b * NC_B + c
                for i in range(CG):
                    ct, g = divmod(i, NG)
                    pool.wait_ge(s["h_done"], it * CG + i + 1)
                    pool.wait_ge(s["sum_mm"], it * CG + max(i - SLOTS + 1, 0))
                    nc.gpsimd.tensor_tensor(hc[:, i % SLOTS, :, :], h[:, i % SLOTS, :, :],
                                            bc[:, N + g * G:N + (g + 1) * G, :], ALU.mult).then_inc(s["hc_done"], 1)
                    if i == RSTD and more:
                        make_rstd(it + 1)
                    for e in range(CT - 1):
                        if GATE_STEPS[e] == i:
                            gate_y(it, e)
                gate_y(it, CT - 1)

            each_chunk(pool, lambda b: make_rstd(b * NC_B), chunk)

        @block.scalar
        def _(act):
            act.dma_start(w_u[:, :, :], in_w[:, :, 0:DI]).then_inc(s["weights_in"], 16)
            act.dma_start(w_x[:, :, :], a["x_proj_w_T"].rearrange("(k p) n -> p k n", p=P)).then_inc(s["weights_in"], 16)
            act.dma_start(w_dt[:, :], a["dt_proj_w_T"]).then_inc(s["weights_in"], 16)
            nc.scalar.activation(a_neg[:, :, :], a_log, ACT.Exp).then_inc(s["setup_done"], 1)
            act.wait_ge(s["setup_done"], 1)
            nc.scalar.activation(a_neg[:, :, :], a_neg[:, :, :], ACT.Copy, scale=-1.0).then_inc(s["setup_done"], 1)
            for half in range(2):
                nc.scalar.activation(pick[half * BC_ROWS:(half + 1) * BC_ROWS, :], ident[0:BC_ROWS, 0:BC_ROWS],
                                     ACT.Copy).then_inc(s["setup_done"], 1)
            act.wait_ge(s["setup_done"], 4)

            def turn(it, k):
                act.wait_ge(s["transposed"], it * KD + k + 1)
                nc.scalar.activation(xn_t[:, k, :], bank[k][:, :], ACT.Identity,
                                     scale=film[:, 0, k:k + 1], bias=film[:, 1, k:k + 1]).then_inc(s["turned"], 1)

            def start(b):
                act.wait_ge(s["turned"], b * NC_B * KD)
                for i, v in enumerate((fa, fb)):
                    nc.scalar.activation(film[:, i, :].unsqueeze(2), v[:, :, bass.ds(b, 1)], ACT.Copy).then_inc(s["film_set"], 1)
                act.wait_ge(s["film_set"], 2 * b + 2)
                for k in range(KD):
                    turn(b * NC_B, k)

            def chunk(b, c, first, more):
                it = b * NC_B + c
                own = Chain(act, s["own_act"], it, 2 * CT)
                for e in range(CT + 1):
                    if e < CT:
                        act.wait_ge(s["in_mm"], it * CT + e + 1)
                        if e >= 2:
                            act.wait_ge(s["conv_done"], it * CT + e - 1)
                        nc.scalar.activation(x_ext[:, e % 2, CONV - 1:], bank[4 + e % 2][:, :], ACT.Copy).then_inc(s["ext_copied"], 1)
                    if e == 1:
                        act.wait_ge(s["gated"], it * CT)
                    if e >= 1:
                        act.wait_ge(s["conv_done"], it * CT + e)
                        nc.scalar.activation(u[:, e - 1, :], conv[:, (e - 1) % 2, :], ACT.Silu).then_inc(s["u_done"], 1)
                act.wait_ge(s["x_mm"], it + 1)
                nc.scalar.activation(dt_r[:, :], bank[6][0:RANK, :], ACT.Copy).then_inc(s["part_a_done"], 1)
                nc.scalar.activation(bc_parts[0:BC_ROWS, :], bank[6][RANK:RANK + BC_ROWS, :], ACT.Copy).then_inc(s["part_a_done"], 1)

                def softplus(ct):
                    act.wait_ge(s["dt_mm"], it * CT + ct + 1)
                    if ct < 2:
                        act.wait_ge(s["u_done"], (it + 1) * CT)
                    nc.scalar.activation(dt[:, ct % 2, :], bank[6 + ct % 2][:, :], ACT.Identity,
                                         bias=dt_b[:, ct:ct + 1]).then_inc(s["v_done"], 1)
                    if ct >= 1:
                        act.wait_ge(s["dt_done"], it * CT + ct)
                    act.wait_ge(s["v_done"], it * CT + ct + 1)
                    own.inc(nc.scalar.activation(soft[:, :], dt[:, ct % 2, :], ACT.Abs))
                    own.wait()
                    own.inc(nc.scalar.activation(soft[:, :], soft[:, :], ACT.Exp, scale=-1.0))
                    own.wait()
                    nc.scalar.activation(soft[:, :], soft[:, :], ACT.Ln, bias=1.0).then_inc(s["soft_done"], 1)

                softplus(0)
                for n in range(0, BC_ROWS, 2):
                    act.wait_ge(s["bc_mm"], it * BC_ROWS + n + 1)
                    nc.scalar.activation(bc[:, n, :], bank[n % 4][:, :], ACT.Copy).then_inc(s["bc_act_done"], 1)
                for i in range(CG):
                    ct, g = divmod(i, NG)
                    if g == 0:
                        act.wait_ge(s["dt_done"], it * CT + ct + 1)
                    act.wait_ge(s["h_done"], it * CG + max(i - SLOTS + 1, 0))
                    for j in range(G):
                        n = g * G + j
                        last = nc.scalar.activation(da[i % SLOTS][:, j, :], dt[:, ct % 2, :], ACT.Exp, scale=a_neg[:, ct, n:n + 1])
                    last.then_inc(s["da_done"], 1)
                    if g == 2 and ct + 1 < CT:
                        if ct >= 1:
                            act.wait_ge(s["da_done"], it * CG + ct * NG)
                        softplus(ct + 1)
                    for e in Z_STEPS.get(i - BEHIND, ()):
                        act.wait_ge(s["z_mm"], it * CT + e + 1)
                        nc.scalar.activation(zy[:, e, :], bank[e % 2][:, :], ACT.Silu).then_inc(s["z_done"], 1)
                    if more and i - BEHIND in range(TURN, TURN + 2 * KD, 2):
                        turn(it + 1, (i - BEHIND - TURN) // 2)
                own.end()

            each_chunk(act, start, chunk)

        @block.vector
        def _(dve):
            def norm_stats(it):
                own = Chain(dve, s["own_norm"], it, 2)
                dve.wait_ge(s["x_loaded"], it * 16 + 16)
                for t in range(TT):
                    st = nc.vector.bn_stats(stats[:, t, :], x_in[:, t, :])
                own.inc(st)
                own.wait()
                nc.vector.memset(var_eps[:, :], 0.0)
                for t in range(TT):
                    st = nc.vector.bn_aggr(mv[:, t, :], stats[:, t, :])
                own.inc(st)
                own.wait()
                nc.vector.tensor_scalar(var_eps[:, :], mv[:, :, 1], EPS, None, ALU.add).then_inc(s["var_done"], 1)
                own.end()

            def add_residual(b, it, t):
                dve.wait_ge(s["out_mm"], it * TT + t + 1)
                nc.vector.tensor_tensor(bank[t][:, :], bank[t][:, :], gate[:, bass.ds(b, 1), :].rearrange("p a d -> p (a d)"),
                                        ALU.mult).then_inc(s["out_gated"], 1)
                dve.wait_ge(s["out_gated"], it * TT + t + 1)
                dve.wait_ge(s["residual_in"], (it + 1) * 16)
                nc.vector.tensor_tensor(x_in[:, t, :], bank[t][:, :], x_in[:, t, :], ALU.add).then_inc(s["out_done"], 1)

            def normalise(it):
                dve.wait_ge(s["rstd_done"], it + 1)
                for t in range(TT):
                    last = nc.vector.tensor_scalar(x_in[:, t, :], x_in[:, t, :], mv[:, t, 0:1], rstd[:, t:t + 1],
                                                   ALU.subtract, ALU.mult)
                last.then_inc(s["x_normed"], 1)

            def start(b):
                nc.vector.memset(halo[:, :, :], 0.0).then_inc(s["reset_done"], 1)
                nc.vector.memset(state[:, :, :], 0.0).then_inc(s["reset_done"], 1)
                norm_stats(b * NC_B)
                normalise(b * NC_B)

            def chunk(b, c, first, more):
                it = b * NC_B + c
                own = Chain(dve, s["own_dve"], it, 5 * CT + CT + CG + CG)
                dve.wait_ge(s["reset_done"], 2 * b + 2)
                for e in range(CT):
                    w = e % 2
                    dve.wait_ge(s["ext_copied"], it * CT + e + 1)
                    own.inc(nc.vector.tensor_copy(x_ext[:, w, 0:CONV - 1], halo[:, e, :]))
                    own.wait()
                    own.inc(nc.vector.tensor_copy(halo[:, e, :], x_ext[:, w, CH:CH + CONV - 1]))
                    own.wait()
                    if e >= 2:
                        dve.wait_ge(s["u_done"], it * CT + e - 1)
                    own.inc(nc.vector.tensor_scalar(conv[:, w, :], x_ext[:, w, 0:CH], conv_w[:, e, 0:1], conv_b[:, e:e + 1],
                                                    ALU.mult, ALU.add))
                    for j in range(1, CONV):
                        own.wait()
                        last = nc.vector.scalar_tensor_tensor(out=conv[:, w, :], in0=x_ext[:, w, j:j + CH],
                                                              scalar=conv_w[:, e, j:j + 1], in1=conv[:, w, :],
                                                              op0=ALU.mult, op1=ALU.add)
                        if j < CONV - 1:
                            own.inc(last)
                    last.then_inc(s["conv_done"], 1)
                dve.wait_ge(s["part_a_done"], it * 2 + 2)
                nc.vector.tensor_tensor(bc_parts[BC_ROWS:2 * BC_ROWS, :], bank[6][RANK:RANK + BC_ROWS, :],
                                        bc_parts[0:BC_ROWS, :].bitcast(F32), ALU.subtract).then_inc(s["part_b_done"], 1)

                def make_dt(ct):
                    dve.wait_ge(s["soft_done"], it * CT + ct + 1)
                    nc.vector.scalar_tensor_tensor(out=dt[:, ct % 2, :], in0=dt[:, ct % 2, :], scalar=0.0, in1=soft[:, :],
                                                   op0=ALU.max, op1=ALU.add).then_inc(s["dt_done"], 1)

                for n in range(1, BC_ROWS, 2):
                    dve.wait_ge(s["bc_mm"], it * BC_ROWS + n + 1)
                    nc.vector.tensor_copy(bc[:, n, :], bank[n % 4][:, :]).then_inc(s["bc_dve_done"], 1)
                    if n == 5:
                        make_dt(0)
                dve.wait_ge(s["bc_act_done"], (it + 1) * N)
                dve.wait_ge(s["bc_dve_done"], (it + 1) * N)
                dve.wait_ge(s["u_done"], (it + 1) * CT)

                saved = []

                def drive(i):
                    ct, g = divmod(i, NG)
                    if g == 0:
                        dve.wait_ge(s["dt_done"], it * CT + ct + 1)
                        if ct:
                            own.wait()
                        own.inc(nc.vector.tensor_tensor(du[:, :], dt[:, ct % 2, :], u[:, ct, :], ALU.mult))
                        own.wait()
                    dve.wait_ge(s["hc_done"], it * CG + max(i - SLOTS + 1, 0))
                    if i >= SLOTS:
                        dve.wait_ge(own.sem, saved[i - SLOTS])
                    own.inc(nc.vector.tensor_tensor(h[:, i % SLOTS, :, :], du[:, :].unsqueeze(1).to_broadcast([P, G, CH]),
                                                    bc[:, g * G:(g + 1) * G, :], ALU.mult))

                def save_state(i):
                    ct, g = divmod(i, NG)
                    dve.wait_ge(s["h_done"], it * CG + i + 1)
                    own.inc(nc.vector.tensor_copy(state[:, ct, g * G:(g + 1) * G], h[:, i % SLOTS, :, CH - 1]))
                    saved.append(own.so_far())

                def read_y(ct):
                    dve.wait_ge(s["sum_mm"], it * CG + (ct + 1) * NG)
                    nc.vector.scalar_tensor_tensor(out=u[:, ct, :], in0=u[:, ct, :], scalar=d_par[:, ct:ct + 1],
                                                   in1=bank[4 + ct % 2][:, :], op0=ALU.mult, op1=ALU.add
                                                   ).then_inc(s["y_read"], 1)

                drive(0)
                for i in range(CG):
                    ct, g = divmod(i, NG)
                    driven = own.so_far()
                    if i + 1 < CG:
                        drive(i + 1)
                    if i >= 1:
                        save_state(i - 1)
                    dve.wait_ge(s["da_done"], it * CG + i + 1)
                    dve.wait_ge(own.sem, driven)
                    for j in range(G):
                        last = nc.vector.tensor_tensor_scan(h[:, i % SLOTS, j, :], da[i % SLOTS][:, j, :], h[:, i % SLOTS, j, :],
                                                            state[:, ct, g * G + j:g * G + j + 1], ALU.mult, ALU.add)
                    last.then_inc(s["h_done"], 1)
                    if g == READ and ct >= 1:
                        read_y(ct - 1)
                    if g == NG // 2 + 1 and ct + 1 < CT:
                        make_dt(ct + 1)
                    if not first and i - OUT_BEHIND in OUT_STEPS:
                        add_residual(b, it - 1, OUT_STEPS[i - OUT_BEHIND])
                    if i == STATS and more:
                        norm_stats(it + 1)
                    if i == NORMED and more:
                        normalise(it + 1)
                save_state(CG - 1)
                read_y(CT - 1)
                own.end()
                if not more:
                    for t in range(TT):
                        add_residual(b, it, t)

            each_chunk(dve, start, chunk)

        @block.tensor
        def _(pe):
            pe.wait_ge(s["setup_done"], 4)

            def transpose_x(it, k):
                if k == 0:
                    pe.wait_ge(s["x_normed"], it + 1)
                for t in range(TT):
                    mm = nc.tensor.transpose(bank[k][:, t * P:(t + 1) * P], x_in[:, t, k * P:(k + 1) * P], ident[:, :])
                mm.then_inc(s["transposed"], 1)

            def project_back(it, t):
                if t == 0:
                    pe.wait_ge(s["wo_in"], (it + 1) * 16)
                    pe.wait_ge(s["gated"], (it + 1) * CT)
                for k in range(CT):
                    mm = nc.tensor.matmul(bank[t][:, :], zy[:, k, t * P:(t + 1) * P], w_out[:, k, :],
                                          start=(k == 0), stop=(k == CT - 1))
                mm.then_inc(s["out_mm"], 1)

            def start(b):
                pe.wait_ge(s["out_done"], b * NC_B * TT)
                for k in range(KD):
                    transpose_x(b * NC_B, k)

            def chunk(b, c, first, more):
                it = b * NC_B + c
                pe.wait_ge(s["weights_in"], 48)
                pe.wait_ge(s["turned"], (it + 1) * KD)
                pe.wait_ge(s["y_read"], it * CT)
                for e in range(CT):
                    if e >= 2:
                        pe.wait_ge(s["ext_copied"], it * CT + e - 1)
                    for k in range(KD):
                        mm = nc.tensor.matmul(bank[4 + e % 2][:, :], w_u[:, k, e * P:(e + 1) * P], xn_t[:, k, :],
                                              start=(k == 0), stop=(k == KD - 1))
                    mm.then_inc(s["in_mm"], 1)
                for k in range(CT):
                    pe.wait_ge(s["u_done"], it * CT + k + 1)
                    mm = nc.tensor.matmul(bank[6][0:RANK + BC_ROWS, :], w_x[:, k, :], u[:, k, :], start=(k == 0), stop=(k == CT - 1))
                mm.then_inc(s["x_mm"], 1)
                pe.wait_ge(s["part_a_done"], it * 2 + 2)
                pe.wait_ge(s["part_b_done"], it + 1)

                def project_dt(ct):
                    if ct >= 2:
                        pe.wait_ge(s["v_done"], it * CT + ct - 1)
                    nc.tensor.matmul(bank[6 + ct % 2][:, :], w_dt[:, ct * P:(ct + 1) * P], dt_r[:, :],
                                     start=True, stop=True).then_inc(s["dt_mm"], 1)

                project_dt(0)
                project_dt(1)
                for n in range(BC_ROWS):
                    if n >= 4:
                        done = s["bc_dve_done"] if n % 2 else s["bc_act_done"]
                        pe.wait_ge(done, it * N + n // 2 - 1)
                    nc.tensor.matmul(bank[n % 4][:, :], pick[:, n:n + 1].to_broadcast([2 * BC_ROWS, P]), bc_parts[:, :],
                                     start=True, stop=True).then_inc(s["bc_mm"], 1)
                for i in range(CG):
                    ct, g = divmod(i, NG)
                    if g == 0:
                        if ct >= 2:
                            pe.wait_ge(s["y_read"], it * CT + ct - 1)
                    if g == 1 and ct + 2 < CT:
                        project_dt(ct + 2)
                    pe.wait_ge(s["hc_done"], it * CG + i + 1)
                    for j in range(G):
                        mm = nc.tensor.matmul(bank[4 + ct % 2][:, :], ident[:, :], hc[:, i % SLOTS, j, :],
                                              start=(g == 0 and j == 0), stop=(g == NG - 1 and j == G - 1))
                    mm.then_inc(s["sum_mm"], 1)
                    if i in OUT_STEPS and not first:
                        if OUT_STEPS[i] == 0:
                            pe.wait_ge(s["bc_act_done"], (it + 1) * N)
                            pe.wait_ge(s["bc_dve_done"], (it + 1) * N)
                        project_back(it - 1, OUT_STEPS[i])
                    for e in Z_STEPS.get(i, ()):
                        if e == 0:
                            pe.wait_ge(s["wz_in"], (it + 1) * 16)
                            if first:
                                pe.wait_ge(s["bc_act_done"], (it + 1) * N)
                                pe.wait_ge(s["bc_dve_done"], (it + 1) * N)
                            else:
                                pe.wait_ge(s["out_done"], it * TT)
                        elif e >= 2:
                            pe.wait_ge(s["z_done"], it * CT + e - 1)
                        for k in range(KD):
                            mm = nc.tensor.matmul(bank[e % 2][:, :], w_z[:, k, e * P:(e + 1) * P], xn_t[:, k, :],
                                                  start=(k == 0), stop=(k == KD - 1))
                        mm.then_inc(s["z_mm"], 1)
                    if more and i in range(TURN, TURN + 2 * KD, 2):
                        k = (i - TURN) // 2
                        if k == 0:
                            pe.wait_ge(s["z_done"], (it + 1) * CT)
                        transpose_x(it + 1, k)
                if not more:
                    pe.wait_ge(s["z_done"], (it + 1) * CT)
                    for t in range(TT):
                        project_back(it, t)

            each_chunk(pe, start, chunk)



class Norm:

    def __init__(self, r, keep, banks=None):
        self.x = r.sb("norm_x", [P, TT, D])
        self.xn_t = r.sb("norm_xn_t", [P, KD, CH])
        self.stats = r.sb("norm_stats", [P, TT, 6])
        self.mv = r.sb("norm_mv", [P, TT, 2])
        self.var_eps = r.sb("norm_var_eps", [P, TT])
        self.rstd = r.sb("norm_rstd", [P, TT])
        self.bank = banks or [r.ps(f"norm_bank{i}", [P, CH]) for i in range(4)]
        self.ident, self.neg_half = keep["ident"], keep["neg_half"]
        self.x_loaded, self.var_done, self.rstd_done, self.x_normed, self.transposed, self.turned = (
            r.sem(n) for n in ("x_loaded", "var_done", "rstd_done", "x_normed", "transposed", "turned"))


DVE_NORM = 2


def norm_load(sp, m, rows, it):
    sp.wait_ge(m.transposed, it * KD)
    sp.dma_start(m.x[:, :, :], rows[bass.ds(it * CH, CH), :].rearrange("(t p) d -> p t d", p=P)).then_inc(m.x_loaded, 16)


def norm_dve(nc, dve, m, own, it, src):
    for t in range(TT):
        last = nc.vector.bn_stats(m.stats[:, t, :], src(t))
    own.inc(last)
    own.wait()
    nc.vector.memset(m.var_eps[:, :], 0.0)
    for t in range(TT):
        last = nc.vector.bn_aggr(m.mv[:, t, :], m.stats[:, t, :])
    own.inc(last)
    own.wait()
    nc.vector.tensor_scalar(m.var_eps[:, :], m.mv[:, :, 1], EPS, None, ALU.add).then_inc(m.var_done, 1)
    dve.wait_ge(m.rstd_done, it + 1)
    dve.wait_ge(m.transposed, it * KD)
    for t in range(TT):
        last = nc.vector.tensor_scalar(m.x[:, t, :], src(t), m.mv[:, t, 0:1], m.rstd[:, t:t + 1],
                                       ALU.subtract, ALU.mult)
    last.then_inc(m.x_normed, 1)


def norm_pool(nc, pool, m, it):
    pool.wait_ge(m.var_done, it + 1)
    nc.gpsimd.tensor_tensor(m.rstd[:, :], m.var_eps[:, :], m.neg_half[:, 0:TT], ALU.pow).then_inc(m.rstd_done, 1)


def norm_pe(nc, pe, m, it, bank=None, read=None):
    pe.wait_ge(m.x_normed, it + 1)
    pe.wait_ge(m.turned, it * KD)
    for k in range(KD):
        if read:
            pe.wait_ge(*read(k))
        for t in range(TT):
            mm = nc.tensor.transpose((bank or m.bank)[k][:, t * P:(t + 1) * P], m.x[:, t, k * P:(k + 1) * P], m.ident[:, :])
        mm.then_inc(m.transposed, 1)


def norm_act(nc, act, m, it, func, scale, bias, bank=None):
    for k in range(KD):
        act.wait_ge(m.transposed, it * KD + k + 1)
        nc.scalar.activation(m.xn_t[:, k, :], (bank or m.bank)[k][:, :], func, scale=scale(k), bias=bias(k)).then_inc(m.turned, 1)


def take_film(nc, act, m, batch_film, film, b, film_set):
    act.wait_ge(m.turned, b * NC_B * KD)
    for i, v in enumerate(film):
        nc.scalar.activation(batch_film[:, i, :].unsqueeze(2), v[:, :, bass.ds(b, 1)], ACT.Copy).then_inc(film_set, 1)
    act.wait_ge(film_set, 2 * b + 2)


def each_chunk(engine, b, start, chunk):
    start(b * NC_B)
    with engine.Fori(0, NC_B - 1) as c:
        chunk(b * NC_B + c, c, True)
    chunk(b * NC_B + NC_B - 1, NC_B - 1, False)


H1 = 16
DH1 = D // H1
QT = S // P
NT = NB * QT


def stage_qkv(nc, a, keep, src, parts, mask_parts, v, spare):
    with ExitStack() as ctx:
        r = Room(nc, ctx, "qkv")
        m = Norm(r, keep)
        w = [r.sb(f"w_{n}", [P, KD, D]) for n in "qkv"]
        v_b = r.sb("v_b", [P, D])
        mask = r.sb("mask", [P, NT])
        mrow = r.sb("mrow", [NT, P])
        mrow_parts = r.sb("mrow_parts", [NT, 2, P], F32R)
        vb = r.sb("vb", [P, 2, D])
        full = r.sb("full", [P, 2, CH])
        pair = r.sb("pair", [P, 2, 2, CH], F32R)
        bank = [r.ps(f"bank{i}", [P, CH]) for i in range(4)]
        w_in = [r.sem(f"w_in_{n}") for n in "qkv"]
        names = "small_in mask_done mask_stored v_mm v_biased v_done qk_mm full_done first_done second_done own_dve"
        s = {n: r.sem(n) for n in names.split()}
        stored = [r.sem(f"stored{i}") for i in range(2)]
        cols = keep["cols"]
        g, bvec = column(cols, "L1_cond_norm_w"), column(cols, "L1_cond_norm_b")
        qk_bias = [column(cols, "L1_cond_q_b"), column(cols, "L1_cond_k_b")]
        block = ctx.enter_context(nc.Block())
        NQ = 2 * KD
        NORM_AT = 1
        films = [Film(r, keep, i + 1, spare[:, i * (QT // 2):(i + 1) * (QT // 2), :], bank[i]) for i in range(2)]

        @block.sync
        def _(sp):

            def chunk(it, c, more):
                if more:
                    norm_load(sp, m, src, it + 1)

            with sp.Fori(0, NB) as b:
                each_chunk(sp, b, lambda it: norm_load(sp, m, src, it), chunk)
            sp.wait_ge(s["mask_done"], 3)
            sp.dma_start(mask_parts.rearrange("a (t j) -> t a j", j=P), mrow_parts[:, :, :].bitcast(F32)).then_inc(s["mask_stored"], 16)
            sp.wait_ge(s["mask_stored"], 16)
            for slot in range(2):
                sp.wait_ge(stored[slot], NCH * NQ // 2 * 16)

        @block.gpsimd
        def _(pool):
            def chunk(it, c, more):
                for i in range(NQ):
                    which, mt = divmod(i, KD)
                    pool.wait_ge(s["second_done"], it * NQ + i + 1)
                    pool.dma_start(parts[which, :, mt * P:(mt + 1) * P, bass.ds(it * CH, CH)].rearrange("a p s -> p a s"),
                                   pair[:, i % 2, :, :].bitcast(F32)).then_inc(stored[i % 2], 16)
                    if i == NORM_AT and more:
                        norm_pool(nc, pool, m, it + 1)

            with pool.Fori(0, NB) as b:
                each_chunk(pool, b, lambda it: norm_pool(nc, pool, m, it), chunk)

        @block.tensor
        def _(pe):

            def chunk(it, c, more):
                pe.wait_ge(m.turned, (it + 1) * KD)
                pe.wait_ge(w_in[2], 16)
                for t in range(TT):
                    pe.wait_ge(s["v_biased"], it * TT + t - 1) if t >= 2 else pe.wait_ge(s["v_biased"], it * TT)
                    for k in range(KD):
                        mm = nc.tensor.matmul(bank[t % 2][:, :], m.xn_t[:, k, t * P:(t + 1) * P], w[2][:, k, :],
                                              start=(k == 0), stop=(k == KD - 1))
                    mm.then_inc(s["v_mm"], 1)
                for i in range(NQ):
                    which, mt = divmod(i, KD)
                    if mt == 0:
                        pe.wait_ge(w_in[which], 16)
                    pe.wait_ge(s["full_done"], it * NQ + i - 1) if i >= 2 else pe.wait_ge(s["full_done"], it * NQ)
                    for k in range(KD):
                        mm = nc.tensor.matmul(bank[2 + i % 2][:, :], w[which][:, k, mt * P:(mt + 1) * P], m.xn_t[:, k, :],
                                              start=(k == 0), stop=(k == KD - 1))
                    mm.then_inc(s["qk_mm"], 1)
                if more:
                    norm_pe(nc, pe, m, it + 1)

            with pe.Fori(0, NB) as b:
                each_chunk(pe, b, lambda it: norm_pe(nc, pe, m, it), chunk)
            pe.wait_ge(s["v_biased"], NCH * TT)
            for film in films:
                film_pe(nc, pe, film)

        @block.scalar
        def _(act):
            act.dma_start(v_b[:, :], row_on_all(a["L1_cond_v_b"])).then_inc(s["small_in"], 16)
            act.dma_start(mask[:, :], a["mask_ff1_columns"]).then_inc(s["small_in"], 16)
            act.dma_start(mrow[:, :], a["mask_BxS_ff1"].rearrange("b (t j) -> (b t) j", j=P)).then_inc(s["small_in"], 16)
            for i, n in ((2, "v"), (0, "q"), (1, "k")):
                act.dma_start(w[i][:, :, :], a[f"L1_cond_{n}_w"].rearrange("(k p) n -> p k n", p=P)).then_inc(w_in[i], 16)
            act.wait_ge(m.x_loaded, 16)
            for film in films:
                film_load(act, film, a)
            act.wait_ge(s["mask_done"], 1)
            nc.scalar.activation(mrow_parts[:, 0, :], mrow[:, :], ACT.Copy).then_inc(s["mask_done"], 1)

            def norm(it):
                act.wait_ge(s["qk_mm"], it * NQ)
                norm_act(nc, act, m, it, ACT.Identity, lambda k: g[:, k:k + 1], lambda k: bvec[:, k:k + 1])

            with act.Fori(0, NB) as b:
                def chunk(it, c, more):
                    for t in range(TT):
                        act.wait_ge(s["v_biased"], it * TT + t + 1)
                        nc.scalar.activation(v[:, bass.ds(c * TT + t, 1), bass.ds(b * D, D)].rearrange("p a d -> p (a d)"),
                                             vb[:, t % 2, :], ACT.Copy,
                                             scale=mask[:, bass.ds(it * TT + t, 1)]).then_inc(s["v_done"], 1)
                    for i in range(NQ):
                        which, mt = divmod(i, KD)
                        act.wait_ge(s["qk_mm"], it * NQ + i + 1)
                        act.wait_ge(s["second_done"], it * NQ + max(i - 1, 0))
                        nc.scalar.activation(full[:, i % 2, :], bank[2 + i % 2][:, :], ACT.Identity,
                                             bias=qk_bias[which][:, mt:mt + 1]).then_inc(s["full_done"], 1)
                        act.wait_ge(s["full_done"], it * NQ + i + 1)
                        act.wait_ge(stored[i % 2], (it * (NQ // 2) + i // 2) * 16)
                        nc.scalar.activation(pair[:, i % 2, 0, :], full[:, i % 2, :], ACT.Copy).then_inc(s["first_done"], 1)
                    if more:
                        norm(it + 1)

                each_chunk(act, b, norm, chunk)

        @block.vector
        def _(dve):
            dve.wait_ge(s["small_in"], 48)
            nc.vector.tensor_scalar(mrow[:, :], mrow[:, :], 1e6, -1e6, ALU.mult, ALU.add).then_inc(s["mask_done"], 1)
            dve.wait_ge(s["mask_done"], 2)
            nc.vector.tensor_tensor(mrow_parts[:, 1, :], mrow[:, :], mrow_parts[:, 0, :].bitcast(F32), ALU.subtract).then_inc(s["mask_done"], 1)

            def norm(it):
                own = Chain(dve, s["own_dve"], it, DVE_NORM)
                dve.wait_ge(m.x_loaded, (it + 1) * 16)
                norm_dve(nc, dve, m, own, it, lambda t: m.x[:, t, :])
                own.end()

            def chunk(it, c, more):
                for t in range(TT):
                    dve.wait_ge(s["v_mm"], it * TT + t + 1)
                    dve.wait_ge(s["v_done"], it * TT + max(t - 1, 0))
                    nc.vector.tensor_tensor(vb[:, t % 2, :], bank[t % 2][:, :], v_b[:, :], ALU.add).then_inc(s["v_biased"], 1)
                for i in range(NQ):
                    dve.wait_ge(s["first_done"], it * NQ + i + 1)
                    nc.vector.tensor_tensor(pair[:, i % 2, 1, :], full[:, i % 2, :], pair[:, i % 2, 0, :].bitcast(F32),
                                            ALU.subtract).then_inc(s["second_done"], 1)
                    if i == NORM_AT and more:
                        norm(it + 1)

            with dve.Fori(0, NB) as b:
                each_chunk(dve, b, norm, chunk)
            for film in films:
                film_dve(nc, dve, film)


def stage_attention(nc, a, keep, parts, mask_parts, max_rows, v, y):
    with ExitStack() as ctx:
        r = Room(nc, ctx, "attn")
        ROWS_MAX, ROWS = 3 * DH1 + 2, 3 * DH1 + 4
        VW = 2 * DH1 + 1
        HALF = S // 2
        STEPS = 2 * QT
        NMAX = QT * (S // CH)
        FIRST_MAX, MAX_STEPS = 3, 25
        TURN_MAX, TURN_0 = 28, 30
        BUILD_V = 4
        HEADS = NB * H1
        JT = HALF // P
        SLOTS = 3
        DVE_COLS = 448
        q_st = [r.sb(f"q_stack{i}", [ROWS, S], F32R) for i in range(2)]
        k_st = [r.sb(f"k_stack{i}", [ROWS, S], F32R) for i in range(2)]
        prob = [r.sb(f"prob{i}", [P, HALF]) for i in range(SLOTS)]
        prob_a = [r.sb(f"prob_a{i}", [P, HALF], F32R) for i in range(2)]
        prob_b = [r.sb(f"prob_b{i}", [P, HALF], F32R) for i in range(2)]
        mx = r.sb("mx", [P, QT, S // CH])
        m_all = r.sb("m_all", [P, QT])
        m_parts = r.sb("m_parts", [QT, 2, P], F32R)
        rden = r.sb("rden", [P, JT, 1])
        v_h = [r.sb(f"v_h{i}", [P, QT, VW], F32R) for i in range(2)]
        fold = r.sb("fold", [VW, DH1 + 1])
        o_t = r.sb("o_t", [VW, HALF])
        ps_max = [r.ps(f"ps_max{i}", [P, CH]) for i in range(2)]
        ps_s = [r.ps(f"ps_s{i}", [P, HALF]) for i in range(2)]
        ps_o = r.ps("ps_o", [P, HALF])
        o_nat = ps_max[1][:, 0:JT * (DH1 + 1)].rearrange("p (j e) -> p j e", e=DH1 + 1)
        names = ("stack_free stack_in max_in max_mm max_red m_done m_turned m_first m_second m_stored s_mm e_done a_done "
                 "b_done_pool b_done_dve o_mm o_copied o_turned o_read v_first v_copied fold_set own_dve")
        s = {n: r.sem(n) for n in names.split()}
        block = ctx.enter_context(nc.Block())

        def load_stacks(sp, b, h, slot):
            f = h * DH1
            at = bass.ds(b * S, S)
            part = lambda which, p: parts[which, p, bass.ds(f, DH1), at]
            sp.dma_start(k_st[slot][0:DH1, :].bitcast(F32), part(1, 0)).then_inc(s["stack_in"], 16)
            sp.dma_start(k_st[slot][DH1:2 * DH1, :].bitcast(F32), part(1, 1)).then_inc(s["stack_in"], 16)
            sp.dma_start(k_st[slot][2 * DH1:3 * DH1, :].bitcast(F32), part(1, 0)).then_inc(s["stack_in"], 16)
            sp.dma_start(k_st[slot][3 * DH1:3 * DH1 + 2, :].bitcast(F32), mask_parts[:, at]).then_inc(s["stack_in"], 16)
            sp.dma_start(q_st[slot][0:DH1, :].bitcast(F32), part(0, 0)).then_inc(s["stack_in"], 16)
            sp.dma_start(q_st[slot][DH1:2 * DH1, :].bitcast(F32), part(0, 0)).then_inc(s["stack_in"], 16)
            sp.dma_start(q_st[slot][2 * DH1:3 * DH1, :].bitcast(F32), part(0, 1)).then_inc(s["stack_in"], 16)

        NSTACK = 7

        def each_head(engine, head):
            head(0, 0, True, False)
            with engine.Fori(0, HEADS // 2 - 1) as i:
                head(2 * i + 1, 1, False, False)
                head(2 * i + 2, 0, False, False)
            head(HEADS - 1, 1, False, True)

        def max_tiles(st):
            return [i for i in range(NMAX) if FIRST_MAX + i * MAX_STEPS // NMAX == st]

        def slot_free(hd, st):
            return hd * STEPS + (st - SLOTS + 1 if st >= SLOTS else min(st, 1) - 1)

        @block.sync
        def _(sp):
            with sp.Fori(0, NB) as b, sp.Fori(0, H1 // 2) as hp:
                for slot in range(2):
                    hd = b * H1 + 2 * hp + slot
                    sp.wait_ge(s["stack_free"], hd + 2)
                    load_stacks(sp, b, 2 * hp + slot, slot)
                    sp.wait_ge(s["m_second"], hd + 1)
                    sp.dma_start(max_rows[slot].rearrange("a (q j) -> q a j", j=P), m_parts[:, :, :].bitcast(F32)).then_inc(s["m_stored"], 16)
                    sp.wait_ge(s["m_stored"], (hd + 1) * 16)
                    sp.dma_start(q_st[slot][3 * DH1 + 2:ROWS, :].bitcast(F32), max_rows[slot]).then_inc(s["max_in"], 16)

        @block.gpsimd
        def _(pool):
            def first_v(hd, slot):
                nc.gpsimd.tensor_copy(v_h[slot][:, :, 0:DH1], v[:, :, bass.ds(hd * DH1, DH1)]).then_inc(s["v_first"], 1)

            def second_v(hd, slot):
                nc.gpsimd.tensor_tensor(v_h[slot][:, :, DH1:2 * DH1], v[:, :, bass.ds(hd * DH1, DH1)], v_h[slot][:, :, 0:DH1].bitcast(F32),
                                        ALU.subtract).then_inc(s["v_copied"], 1)

            def head(hd, slot, first, last):
                for st in range(STEPS):
                    if st == BUILD_V and not last:
                        pool.wait_ge(s["o_mm"], hd * STEPS)
                        first_v(hd + 1, 1 - slot)
                        pool.wait_ge(s["v_first"], hd + 2)
                    pool.wait_ge(s["a_done"], hd * STEPS + st + 1)
                    if not (first and st < 2):
                        pool.wait_ge(s["o_mm"], hd * STEPS + st - 1)
                    nc.gpsimd.tensor_tensor(prob_b[st % 2][:, CH:], prob[st % SLOTS][:, CH:],
                                            prob_a[st % 2][:, CH:].bitcast(F32), ALU.subtract).then_inc(s["b_done_pool"], 1)
                    nc.gpsimd.tensor_tensor(prob_b[st % 2][:, DVE_COLS:CH], prob[st % SLOTS][:, DVE_COLS:CH],
                                            prob_a[st % 2][:, DVE_COLS:CH].bitcast(F32), ALU.subtract).then_inc(s["b_done_pool"], 1)
                    if st == BUILD_V and not last:
                        second_v(hd + 1, 1 - slot)

            for slot in range(2):
                nc.gpsimd.memset(v_h[slot][:, :, 2 * DH1:VW].bitcast(F32), 1.0)
            first_v(0, 0)
            pool.wait_ge(s["v_first"], 1)
            second_v(0, 0)
            each_head(pool, head)

        @block.tensor
        def _(pe):
            def max_mm(hd, slot, i, first=False):
                if i == 0:
                    pe.wait_ge(s["stack_in"], (hd + 1) * NSTACK * 16)
                    pe.wait_ge(s["m_second"], hd)
                    if not first:
                        pe.wait_ge(s["o_read"], (hd - 1) * 2)
                pe.wait_ge(s["max_red"], hd * NMAX + max(i - 1, 0))
                qt, kc = divmod(i, S // CH)
                nc.tensor.matmul(ps_max[i % 2][:, :], q_st[slot][0:ROWS_MAX, qt * P:(qt + 1) * P],
                                 k_st[slot][0:ROWS_MAX, kc * CH:(kc + 1) * CH], start=True, stop=True).then_inc(s["max_mm"], 1)

            def turn_max(hd):
                pe.wait_ge(s["m_done"], hd + 1)
                nc.tensor.transpose(ps_max[0][0:QT, 0:P], m_all[:, :], keep["ident"][:, :]).then_inc(s["m_turned"], 1)

            def score_mm(hd, slot, st):
                half, kt = divmod(st, QT)
                if st == 0:
                    pe.wait_ge(s["max_in"], (hd + 1) * 16)
                pe.wait_ge(s["a_done"], hd * STEPS + max(st - 1, 0))
                for c in range(2):
                    q0 = half * HALF + c * CH
                    mm = nc.tensor.matmul(ps_s[st % 2][:, c * CH:(c + 1) * CH], k_st[slot][0:ROWS, kt * P:(kt + 1) * P],
                                          q_st[slot][0:ROWS, q0:q0 + CH], start=True, stop=True)
                    if st == 0 and c == 0:
                        mm.then_inc(s["stack_free"], 1)
                mm.then_inc(s["s_mm"], 1)

            def pv_mm(hd, slot, st, c):
                half, kt = divmod(st, QT)
                if st == 0 and c == 0:
                    pe.wait_ge(s["v_copied"], hd + 1)
                if kt == 0:
                    pe.wait_ge(s["o_copied"], hd * 4 + (c + 1 if half else 0))
                pe.wait_ge(s["a_done"], hd * STEPS + st + 1)
                cols = slice(c * CH, (c + 1) * CH)
                nc.tensor.matmul(ps_o[0:VW, cols], v_h[slot][:, kt, :], prob_a[st % 2][:, cols], start=(kt == 0), stop=False)

            def pv_rest(hd, slot, st, c):
                half, kt = divmod(st, QT)
                cols = slice(c * CH, (c + 1) * CH)
                pe.wait_ge(s["b_done_pool"], (hd * STEPS + st) * 2 + (1 if c else 2))
                if not c:
                    pe.wait_ge(s["b_done_dve"], hd * STEPS + st + 1)
                mm = nc.tensor.matmul(ps_o[0:VW, cols], v_h[slot][:, kt, :], prob_b[st % 2][:, cols],
                                      start=False, stop=(kt == QT - 1))
                if not c:
                    mm.then_inc(s["o_mm"], 1)

            def turn_o(done):
                pe.wait_ge(s["o_copied"], (done + 1) * 2)
                for j in range(JT):
                    mm = nc.tensor.matmul(o_nat[:, j, :], o_t[:, j * P:(j + 1) * P], fold[:, :], start=True, stop=True)
                mm.then_inc(s["o_turned"], 1)

            def head(hd, slot, first, last):
                for st in range(STEPS):
                    if st + 1 < STEPS:
                        score_mm(hd, slot, st + 1)
                    elif not last:
                        score_mm(hd + 1, 1 - slot, 0)
                    tiles = [] if last else max_tiles(st)
                    if st == 2 and not first:
                        turn_o(hd * 2 - 1)
                    before = (hd, slot, st - 1) if st else (hd - 1, 1 - slot, STEPS - 1)
                    for j in range(4):
                        if j < 3:
                            for i in tiles[j:j + 1]:
                                max_mm(hd + 1, 1 - slot, i)
                        if st or not first:
                            if j < 2:
                                pv_mm(*before, j)
                            else:
                                pv_rest(*before, 3 - j)
                    if st == TURN_MAX and not last:
                        turn_max(hd + 1)
                    if st == TURN_0:
                        turn_o(hd * 2)
                if last:
                    for c in range(2):
                        pv_mm(hd, slot, STEPS - 1, c)
                    for c in (1, 0):
                        pv_rest(hd, slot, STEPS - 1, c)
                    turn_o(hd * 2 + 1)

            for i in range(NMAX):
                max_mm(0, 0, i, True)
            turn_max(0)
            pe.wait_ge(s["fold_set"], 1)
            score_mm(0, 0, 0)
            each_head(pe, head)

        @block.scalar
        def _(act):
            def first_part(hd):
                act.wait_ge(s["m_turned"], hd + 1)
                act.wait_ge(s["m_stored"], hd * 16)
                nc.scalar.activation(m_parts[:, 0, :], ps_max[0][0:QT, 0:P], ACT.Copy, scale=-1.0).then_inc(s["m_first"], 1)

            def head(hd, slot, first, last):
                for st in range(STEPS):
                    act.wait_ge(s["s_mm"], hd * STEPS + st + 1)
                    if not (first and st < SLOTS):
                        act.wait_ge(s["b_done_pool"], slot_free(hd, st) * 2)
                        act.wait_ge(s["b_done_dve"], slot_free(hd, st))
                    nc.scalar.activation(prob[st % SLOTS][:, :], ps_s[st % 2][:, :], ACT.Exp).then_inc(s["e_done"], 1)
                    if not (first and st < 2):
                        act.wait_ge(s["o_mm"], hd * STEPS + st - 1)
                    nc.scalar.activation(prob_a[st % 2][:, :], ps_s[st % 2][:, :], ACT.Exp).then_inc(s["a_done"], 1)
                    if st == TURN_MAX and not last:
                        first_part(hd + 1)

            ident = keep["ident"]
            nc.scalar.activation(fold[0:DH1, 0:DH1], ident[0:DH1, 0:DH1], ACT.Copy)
            nc.scalar.activation(fold[DH1:2 * DH1, 0:DH1], ident[DH1:2 * DH1, DH1:2 * DH1], ACT.Copy)
            nc.scalar.activation(fold[0:2 * DH1, DH1:DH1 + 1], ident[0:2 * DH1, 2 * DH1:VW], ACT.Copy)
            nc.scalar.activation(fold[2 * DH1:VW, :], ident[2 * DH1:VW, DH1:2 * DH1 + 1], ACT.Copy).then_inc(s["fold_set"], 1)
            first_part(0)
            each_head(act, head)

        @block.vector
        def _(dve):
            def reduce(hd, i):
                qt, kc = divmod(i, S // CH)
                dve.wait_ge(s["max_mm"], hd * NMAX + i + 1)
                nc.vector.tensor_reduce(mx[:, qt, kc:kc + 1], ps_max[i % 2][:, :], AX.X, ALU.max).then_inc(s["max_red"], 1)

            def all_max(hd):
                dve.wait_ge(s["max_red"], (hd + 1) * NMAX)
                dve.wait_ge(s["m_turned"], hd)
                nc.vector.tensor_reduce(m_all[:, :], mx[:, :, :], AX.X, ALU.max).then_inc(s["m_done"], 1)

            def second_part(hd):
                dve.wait_ge(s["m_first"], hd + 1)
                nc.vector.scalar_tensor_tensor(out=m_parts[:, 1, :], in0=ps_max[0][0:QT, 0:P], scalar=-1.0,
                                               in1=m_parts[:, 0, :].bitcast(F32), op0=ALU.mult, op1=ALU.subtract
                                               ).then_inc(s["m_second"], 1)

            def copy_o(steps_done, done):
                dve.wait_ge(s["o_mm"], steps_done)
                if not (isinstance(done, int) and done == 0):
                    dve.wait_ge(s["o_turned"], done)
                for c in range(2):
                    nc.vector.tensor_copy(o_t[:, c * CH:(c + 1) * CH], ps_o[0:VW, c * CH:(c + 1) * CH]).then_inc(s["o_copied"], 1)

            def normalise(hd, half, done):
                dve.wait_ge(s["o_turned"], done + 1)
                dve.wait_ge(s["o_read"], done)
                nc.vector.reciprocal(rden[:, :, :], o_nat[:, :, DH1:DH1 + 1]).then_inc(s["own_dve"], 1)
                dve.wait_ge(s["own_dve"], done + 1)
                nc.vector.tensor_tensor(y[:, half * JT:(half + 1) * JT, bass.ds(hd * DH1, DH1)], o_nat[:, :, 0:DH1],
                                        rden[:, :, :].to_broadcast([P, JT, DH1]), ALU.mult).then_inc(s["o_read"], 1)

            def what_is_left(hd, st):
                dve.wait_ge(s["a_done"], hd * STEPS + st + 1)
                if not (isinstance(hd, int) and hd == 0 and st < 2):
                    dve.wait_ge(s["o_mm"], hd * STEPS + st - 1)
                nc.vector.tensor_tensor(prob_b[st % 2][:, 0:DVE_COLS], prob[st % SLOTS][:, 0:DVE_COLS],
                                        prob_a[st % 2][:, 0:DVE_COLS].bitcast(F32), ALU.subtract).then_inc(s["b_done_dve"], 1)

            def head(hd, slot, first, last):
                for st in range(STEPS):
                    if st:
                        what_is_left(hd, st - 1)
                    elif not first:
                        what_is_left(hd - 1, STEPS - 1)
                    if st == 1 and not first:
                        copy_o(hd * STEPS, hd * 2 - 1)
                    if st == 2 and not first:
                        normalise(hd - 1, 1, hd * 2 - 1)
                    if st == QT + 1:
                        copy_o(hd * STEPS + QT, hd * 2)
                    tiles = [] if last else max_tiles(st)
                    for i in tiles:
                        reduce(hd + 1, i)
                    if NMAX - 1 in tiles:
                        all_max(hd + 1)
                    if st == TURN_MAX and not last:
                        second_part(hd + 1)
                    if st == TURN_0 + 1:
                        normalise(hd, 0, hd * 2)
                if last:
                    what_is_left(hd, STEPS - 1)
                    copy_o(HEADS * STEPS, hd * 2 + 1)
                    normalise(hd, 1, hd * 2 + 1)

            for t in range(2):
                nc.vector.memset(q_st[t][3 * DH1:ROWS, :].bitcast(F32), 1.0)
                nc.vector.memset(k_st[t][3 * DH1:ROWS, :].bitcast(F32), 1.0).then_inc(s["stack_free"], 1)
            for i in range(NMAX):
                reduce(0, i)
            all_max(0)
            second_part(0)
            each_head(dve, head)


def stage_out(nc, a, keep, film, w_name, b_name, y, src, out):
    with ExitStack() as ctx:
        r = Room(nc, ctx, f"out{film}")
        m = Norm(r, keep)
        w = r.sb("w", [P, KD, D])
        bias = r.sb("bias", [P, D])
        x_res = r.sb("x_res", [P, 4, D])
        bank = [r.ps(f"bank{i}", [P, CH]) for i in range(4)]
        batch_film = r.sb("batch_film", [P, 2, KD])
        names = "weights_in residual_in film_set o_mm biased out_done stored own_dve"
        s = {n: r.sem(n) for n in names.split()}
        fa, fb = keep["film"][:, film, 0], keep["film"][:, film, 1]
        film_3 = Film(r, keep, 3, r.sb("film3_w", [P, KC, 2 * D])[:, :, :], bank[0])
        block = ctx.enter_context(nc.Block())

        @block.sync
        def _(sp):
            sp.dma_start(w[:, :, :], a[w_name].rearrange("(k p) n -> p k n", p=P)).then_inc(s["weights_in"], 16)
            sp.dma_start(bias[:, :], row_on_all(a[b_name])).then_inc(s["weights_in"], 16)
            film_load(sp, film_3, a)
            with sp.Fori(0, NCH) as it:
                sp.wait_ge(s["stored"], it * 16 * TT)
                sp.dma_start(x_res[:, :, :], src[bass.ds(it * CH, CH), :].rearrange("(t p) d -> p t d", p=P)).then_inc(s["residual_in"], 16)
                for t in range(TT):
                    sp.wait_ge(s["out_done"], it * TT + t + 1)
                    sp.dma_start(out[bass.ds(it * CH + t * P, P), :], x_res[:, t, :]).then_inc(s["stored"], 16)
            sp.wait_ge(s["stored"], NCH * TT * 16)

        @block.gpsimd
        def _(pool):
            with pool.Fori(0, NCH) as it:
                norm_pool(nc, pool, m, it)

        @block.tensor
        def _(pe):
            pe.wait_ge(s["weights_in"], 32)

            def chunk(it, c, more):
                pe.wait_ge(m.turned, (it + 1) * KD)
                for t in range(TT):
                    pe.wait_ge(s["out_done"], it * TT)
                    for k in range(KD):
                        mm = nc.tensor.matmul(bank[t][:, :], m.xn_t[:, k, t * P:(t + 1) * P], w[:, k, :],
                                              start=(k == 0), stop=(k == KD - 1))
                    mm.then_inc(s["o_mm"], 1)
                if more:
                    norm_pe(nc, pe, m, it + 1)

            with pe.Fori(0, NB) as b:
                each_chunk(pe, b, lambda it: norm_pe(nc, pe, m, it), chunk)
            pe.wait_ge(s["out_done"], NCH * TT)
            film_pe(nc, pe, film_3)

        @block.scalar
        def _(act):
            with act.Fori(0, NB) as b:
                take_film(nc, act, m, batch_film, (fa, fb), b, s["film_set"])

                def norm(it):
                    act.wait_ge(s["o_mm"], it * TT)
                    norm_act(nc, act, m, it, ACT.Silu, lambda k: batch_film[:, 0, k:k + 1], lambda k: batch_film[:, 1, k:k + 1])

                each_chunk(act, b, norm, lambda it, c, more: norm(it + 1) if more else None)

        @block.vector
        def _(dve):
            dve.wait_ge(s["weights_in"], 32)
            with dve.Fori(0, NB) as b:
                def norm(it, c):
                    own = Chain(dve, s["own_dve"], it, DVE_NORM)
                    norm_dve(nc, dve, m, own, it, lambda t: y[:, bass.ds(c * TT + t, 1), bass.ds(b * D, D)].rearrange("p a d -> p (a d)"))
                    own.end()

                def chunk(it, c, more):
                    for t in range(TT):
                        dve.wait_ge(s["o_mm"], it * TT + t + 1)
                        nc.vector.tensor_tensor(bank[t][:, :], bank[t][:, :], bias[:, :], ALU.add).then_inc(s["biased"], 1)
                        dve.wait_ge(s["biased"], it * TT + t + 1)
                        dve.wait_ge(s["residual_in"], (it + 1) * 16)
                        nc.vector.tensor_tensor(x_res[:, t, :], bank[t][:, :], x_res[:, t, :], ALU.add).then_inc(s["out_done"], 1)
                        if t == 0 and more:
                            norm(it + 1, c + 1)

                each_chunk(dve, b, lambda it: norm(it, 0), chunk)
            film_dve(nc, dve, film_3)



def stage_linear(nc, a, keep, layer, heads, names_of, int_mask, over_v, src, out):
    with ExitStack() as ctx:
        r = Room(nc, ctx, f"lin{layer}")
        dh = D // heads
        ident = keep["ident"]
        tb = [r.ps(f"turn_bank{i}", [P, CH]) for i in range(4)]
        mb = [r.ps(f"mm_bank{i}", [P, CH]) for i in range(4)]
        m1 = Norm(r, keep, tb)
        m2 = Norm(Room(nc, ctx, f"lin{layer}_out"), keep, tb)
        w = [r.sb(f"w_{n}", [P, KD, D]) for n in ("q", "k", "v", "out")]
        rows = r.sb("bias_rows", [P, 3, D])
        k_t = r.sb("k_t", [P, KD, S])
        q_t = r.sb("q_t", [P, KD, S])
        v_all = r.sb("v_all", [P, QT, D])
        q = r.sb("q", [P, TT, D])
        q_red = r.sb("q_red", [P, TT * heads])
        q_den = r.sb("q_den", [P, TT * heads])
        vb = r.sb("vb", [P, 2, D])
        mask_row = r.sb("mask_row", [P, CH], I32 if int_mask else F32)
        mask_add = r.sb("mask_add", [P, CH])
        mask_in = r.sb("mask_in", [P, NT], I32 if int_mask else F32)
        mask_col = r.sb("mask_col", [P, NT])
        k_max = r.sb("k_max", [P, KD])
        k_maxes = r.sb("k_maxes", [P, KD, NC_B])
        k_sum = r.sb("k_sum", [P, KD])
        k_rec = r.sb("k_rec", [P, KD])
        kn = r.sb("kn", [P, 4, D])
        blocks = r.sb("blocks", [P, P])
        kv = r.sb("kv", [P, KD, P])
        x_res = r.sb("x_res", [P, TT, D])
        batch_film = r.sb("batch_film", [P, 2, KD])
        w_in = [r.sem(f"w_in_{n}") for n in ("q", "k", "v", "out")]
        names = ("small_in blocks_set mask_set q_mm q_biased q_max q_exp q_done q_turned qt_done k_mm k_done k_reduced v_mm "
                 "v_biased v_done mask_loaded mask_made kmax_done kexp_done k_scaled k_turned kn_act kn_dve kv_mm kv_done y_mm "
                 "o_mm biased out_done residual_in stored film_set own_dve own_norm own2_dve")
        s = {n: r.sem(n) for n in names.split()}
        cols = keep["cols"]
        g, bvec, k_bias = (column(cols, names_of[n]) for n in ("norm_w", "norm_b", "bk"))
        fa, fb = keep["film"][:, layer, 0], keep["film"][:, layer, 1]
        mask_name = "mask_BxS_ik0" if int_mask else "mask_BxSx1_fk1"
        mask_flat = a[mask_name].rearrange("b s -> (b s)") if int_mask else a[mask_name].rearrange("b s o -> (b s o)")
        block = ctx.enter_context(nc.Block())

        def y_banks(c):
            return tb if c % 2 else mb

        @block.sync
        def _(sp):
            with sp.Fori(0, NB) as b:
                def start(it):
                    norm_load(sp, m1, src, it)
                    sp.wait_ge(w_in[0], 16)
                    sp.wait_ge(s["mask_made"], it)
                    sp.dma_start(mask_row[:, :], row_on_all(mask_flat[bass.ds(it * CH, CH)])).then_inc(s["mask_loaded"], 16)

                each_chunk(sp, b, start, lambda it, c, more: start(it + 1) if more else None)
                for c in range(NC_B):
                    it = b * NC_B + c
                    sp.wait_ge(s["stored"], it * 16)
                    sp.dma_start(x_res[:, :, :], src[bass.ds(it * CH, CH), :].rearrange("(t p) d -> p t d", p=P)).then_inc(s["residual_in"], 16)
                    sp.wait_ge(s["out_done"], (it + 1) * TT)
                    sp.dma_start(out[bass.ds(it * CH, CH), :].rearrange("(t p) d -> p t d", p=P), x_res[:, :, :]).then_inc(s["stored"], 16)
            sp.wait_ge(s["stored"], NCH * 16)

        @block.gpsimd
        def _(pool):
            nc.gpsimd.memset(blocks[:, :], 0.0).then_inc(s["blocks_set"], 1)
            pool.wait_ge(s["blocks_set"], 1)
            for i in range(P // dh):
                nc.gpsimd.memset(blocks[i * dh:(i + 1) * dh, i * dh:(i + 1) * dh], 1.0).then_inc(s["blocks_set"], 1)
            with pool.Fori(0, NB) as b:
                with pool.Fori(0, NC_B) as c:
                    norm_pool(nc, pool, m1, b * NC_B + c)
                with pool.Fori(0, NC_B) as c:
                    norm_pool(nc, pool, m2, b * NC_B + c)

        @block.tensor
        def _(pe):
            with pe.Fori(0, NB) as b:
                def start(it):
                    pe.wait_ge(s["out_done"], b * NC_B * TT)
                    norm_pe(nc, pe, m1, it)

                def chunk(it, c, more):
                    pe.wait_ge(m1.turned, (it + 1) * KD)
                    for which, used, made, read in ((0, (0, 1), "q_mm", "q_biased"), (2, (2, 3), "v_mm", "v_biased")):
                        pe.wait_ge(w_in[which], 16)
                        for t in range(TT):
                            pe.wait_ge(s[read], it * TT + max(t - 1, 0))
                            if which == 0 and t < 2:
                                pe.wait_ge(s["k_done"], it * KD)
                            for k in range(KD):
                                mm = nc.tensor.matmul(mb[used[t % 2]][:, :], m1.xn_t[:, k, t * P:(t + 1) * P], w[which][:, k, :],
                                                      start=(k == 0), stop=(k == KD - 1))
                            mm.then_inc(s[made], 1)
                    for mt in range(KD):
                        if mt == 0:
                            pe.wait_ge(w_in[1], 16)
                            pe.wait_ge(s["q_biased"], (it + 1) * TT)
                        pe.wait_ge(s["k_done"], it * KD + max(mt - 1, 0))
                        for k in range(KD):
                            mm = nc.tensor.matmul(mb[mt % 2][:, :], w[1][:, k, mt * P:(mt + 1) * P], m1.xn_t[:, k, :],
                                                  start=(k == 0), stop=(k == KD - 1))
                        mm.then_inc(s["k_mm"], 1)
                    if more:
                        pe.wait_ge(s["qt_done"], it * KD)
                        norm_pe(nc, pe, m1, it + 1)
                    pe.wait_ge(s["q_done"], it + 1)
                    for k in range(KD):
                        pe.wait_ge(m1.turned, (it + 1) * KD + (k + 1 if more else 0))
                        for t in range(TT):
                            mm = nc.tensor.transpose(tb[k][:, t * P:(t + 1) * P], q[:, t, k * P:(k + 1) * P], ident[:, :])
                        mm.then_inc(s["q_turned"], 1)

                each_chunk(pe, b, start, chunk)
                pe.wait_ge(s["qt_done"], (b + 1) * NC_B * KD)
                pe.wait_ge(s["k_done"], (b + 1) * NC_B * KD)
                pe.wait_ge(s["v_done"], (b + 1) * QT)
                pe.wait_ge(s["kexp_done"], (b + 1) * KD)
                if over_v:
                    pe.wait_ge(s["k_scaled"], (b + 1) * KD)

                def turn_k(tt):
                    if tt >= 4:
                        pe.wait_ge(s["kn_dve" if tt % 2 else "kn_act"], b * (QT // 2) + tt // 2 - 1)
                    for mt in range(KD):
                        mm = nc.tensor.transpose(tb[tt % 4][:, mt * P:(mt + 1) * P], k_t[:, mt, tt * P:(tt + 1) * P], ident[:, :])
                    mm.then_inc(s["k_turned"], 1)

                turn_k(0)
                turn_k(1)
                for tt in range(QT):
                    if tt + 2 < QT:
                        turn_k(tt + 2)
                    pe.wait_ge(s["kn_dve" if tt % 2 else "kn_act"], b * (QT // 2) + tt // 2 + 1)
                    for mt in range(KD):
                        k_part = kn[:, tt % 4, mt * P:(mt + 1) * P]
                        v_part = v_all[:, tt, mt * P:(mt + 1) * P]
                        mm = nc.tensor.matmul(mb[0][:, mt * P:(mt + 1) * P], v_part if over_v else k_part,
                                              k_part if over_v else v_part, start=(tt == 0 and mt == 0),
                                              stop=(tt == QT - 1), skip_group_check=True)
                    mm.then_inc(s["kv_mm"], 1)
                pe.wait_ge(s["kv_done"], (b + 1) * KD)

                def apply_q(c):
                    for t in range(TT):
                        for mt in range(KD):
                            mm = nc.tensor.matmul(y_banks(c)[t][:, mt * P:(mt + 1) * P],
                                                  q_t[:, mt, c * CH + t * P:c * CH + (t + 1) * P],
                                                  kv[:, mt, :], start=True, stop=True)
                        mm.then_inc(s["y_mm"], 1)

                apply_q(0)
                pe.wait_ge(w_in[3], 16)
                for c in range(NC_B):
                    it = b * NC_B + c
                    norm_pe(nc, pe, m2, it, y_banks(c + 1), (lambda k: (s["out_done"], it * TT - TT + k + 1)) if c else None)
                    pe.wait_ge(m2.turned, (it + 1) * KD)
                    if c + 1 < NC_B:
                        apply_q(c + 1)
                    for t in range(TT):
                        for k in range(KD):
                            mm = nc.tensor.matmul(y_banks(c)[t][:, :], m2.xn_t[:, k, t * P:(t + 1) * P], w[3][:, k, :],
                                                  start=(k == 0), stop=(k == KD - 1))
                        mm.then_inc(s["o_mm"], 1)

        @block.scalar
        def _(act):
            act.dma_start(mask_in[:, :], a["mask_ik0_columns" if int_mask else "mask_fk1_columns"]).then_inc(s["small_in"], 16)
            for i, n in enumerate(("bq", "bv", "bo")):
                act.dma_start(rows[:, i, :], row_on_all(a[names_of[n]])).then_inc(s["small_in"], 16)
            for i, n in ((0, "Wq"), (2, "Wv"), (1, "Wk"), (3, "Wo")):
                act.dma_start(w[i][:, :, :], a[names_of[n]].rearrange("(k p) n -> p k n", p=P)).then_inc(w_in[i], 16)
            act.wait_ge(s["mask_set"], 1)
            with act.Fori(0, NB) as b:
                def norm(it):
                    act.wait_ge(s["k_mm"], it * KD)
                    norm_act(nc, act, m1, it, ACT.Identity, lambda k: g[:, k:k + 1], lambda k: bvec[:, k:k + 1])

                def chunk(it, c, more):
                    act.wait_ge(s["q_max"], it + 1)
                    nc.scalar.activation(q[:, :, :], q[:, :, :], ACT.Exp).then_inc(s["q_exp"], 1)
                    act.wait_ge(s["kv_mm"], b * QT)
                    for t in range(TT):
                        act.wait_ge(s["v_biased"], it * TT + t + 1)
                        nc.scalar.activation(v_all[:, bass.ds(c * TT + t, 1), :].rearrange("p a d -> p (a d)"), vb[:, t % 2, :], ACT.Copy,
                                             scale=mask_col[:, bass.ds(it * TT + t, 1)]).then_inc(s["v_done"], 1)
                    if more:
                        norm(it + 1)
                    for k in range(KD):
                        act.wait_ge(s["q_turned"], it * KD + k + 1)
                        nc.scalar.activation(q_t[:, k, bass.ds(c * CH, CH)], tb[k][:, :], ACT.Copy).then_inc(s["qt_done"], 1)

                each_chunk(act, b, norm, chunk)
                for mt in range(KD):
                    act.wait_ge(s["kmax_done"], b + 1)
                    nc.scalar.activation(k_t[:, mt, :], k_t[:, mt, :], ACT.Exp, bias=k_max[:, mt:mt + 1],
                                         accum_out=k_sum[:, mt:mt + 1]).then_inc(s["kexp_done"], 1)
                for tt in range(0, QT, 2):
                    act.wait_ge(s["k_turned"], b * QT + tt + 1)
                    if tt >= 4:
                        act.wait_ge(s["kv_mm"], b * QT + tt - 3)
                    nc.scalar.activation(kn[:, tt % 4, :], tb[tt % 4][:, :], ACT.Copy).then_inc(s["kn_act"], 1)
                take_film(nc, act, m2, batch_film, (fa, fb), b, s["film_set"])
                for c in range(NC_B):
                    it = b * NC_B + c
                    act.wait_ge(s["o_mm"], it * TT)
                    norm_act(nc, act, m2, it, ACT.Silu, lambda k: batch_film[:, 0, k:k + 1], lambda k: batch_film[:, 1, k:k + 1],
                             y_banks(c + 1))

        @block.vector
        def _(dve):
            dve.wait_ge(s["small_in"], 64)
            if int_mask:
                nc.vector.tensor_scalar(mask_col[:, :], mask_in[:, :], 1.0, None, ALU.not_equal).then_inc(s["mask_set"], 1)
            else:
                nc.vector.tensor_copy(mask_col[:, :], mask_in[:, :]).then_inc(s["mask_set"], 1)
            dve.wait_ge(s["blocks_set"], 1 + P // dh)
            with dve.Fori(0, NB) as b:
                def norm(it):
                    own = Chain(dve, s["own_norm"], it, DVE_NORM)
                    dve.wait_ge(m1.x_loaded, (it + 1) * 16)
                    norm_dve(nc, dve, m1, own, it, lambda t: m1.x[:, t, :])
                    own.end()

                def chunk(it, c, more):
                    own = Chain(dve, s["own_dve"], it, 3)
                    dve.wait_ge(s["mask_loaded"], (it + 1) * 16)
                    dve.wait_ge(s["k_done"], it * KD)
                    if int_mask:
                        nc.vector.tensor_scalar(mask_add[:, :], mask_row[:, :], 1.0, -3.0e38, ALU.is_equal, ALU.mult).then_inc(s["mask_made"], 1)
                    else:
                        nc.vector.tensor_scalar(mask_add[:, :], mask_row[:, :], 1e6, -1e6, ALU.mult, ALU.add).then_inc(s["mask_made"], 1)
                    dve.wait_ge(s["q_turned"], it * KD)
                    for t in range(TT):
                        dve.wait_ge(s["q_mm"], it * TT + t + 1)
                        nc.vector.tensor_tensor(q[:, t, :], mb[t % 2][:, :], rows[:, 0, :], ALU.add).then_inc(s["q_biased"], 1)
                    heads_view = q[:, :, :].rearrange("p t (h e) -> p (t h) e", e=dh)
                    wide = lambda v: v[:, :].unsqueeze(2).to_broadcast([P, TT * heads, dh])
                    dve.wait_ge(s["q_biased"], (it + 1) * TT)
                    own.inc(nc.vector.tensor_reduce(q_red[:, :], heads_view, AX.X, ALU.max))
                    own.wait()
                    nc.vector.tensor_tensor(heads_view, heads_view, wide(q_red), ALU.subtract).then_inc(s["q_max"], 1)
                    for t in range(TT):
                        dve.wait_ge(s["v_mm"], it * TT + t + 1)
                        dve.wait_ge(s["v_done"], it * TT + max(t - 1, 0))
                        nc.vector.tensor_tensor(vb[:, t % 2, :], mb[2 + t % 2][:, :], rows[:, 1, :], ALU.add).then_inc(s["v_biased"], 1)
                        if t == 1:
                            dve.wait_ge(s["q_exp"], it + 1)
                            own.inc(nc.vector.tensor_reduce(q_den[:, :], heads_view, AX.X, ALU.add))
                            own.wait()
                            own.inc(nc.vector.reciprocal(q_den[:, :], q_den[:, :]))
                            own.wait()
                            nc.vector.tensor_tensor(heads_view, heads_view, wide(q_den), ALU.mult).then_inc(s["q_done"], 1)
                    dve.wait_ge(s["mask_made"], it + 1)
                    for mt in range(KD):
                        dve.wait_ge(s["k_mm"], it * KD + mt + 1)
                        nc.vector.scalar_tensor_tensor(out=k_t[:, mt, bass.ds(c * CH, CH)], in0=mb[mt % 2][:, :], scalar=k_bias[:, mt:mt + 1],
                                                       in1=mask_add[:, :], op0=ALU.add, op1=ALU.add).then_inc(s["k_done"], 1)
                        if mt == 1 and more:
                            norm(it + 1)
                    for mt in range(KD):
                        dve.wait_ge(s["k_done"], it * KD + mt + 1)
                        nc.vector.tensor_reduce(k_maxes[:, mt, bass.ds(c, 1)], k_t[:, mt, bass.ds(c * CH, CH)], AX.X, ALU.max).then_inc(s["k_reduced"], 1)
                    own.end()

                each_chunk(dve, b, norm, chunk)
                own = Chain(dve, s["own2_dve"], b, 2 + 2 * NC_B)
                dve.wait_ge(s["k_done"], (b + 1) * NC_B * KD)
                dve.wait_ge(s["k_reduced"], (b + 1) * NC_B * KD)
                own.inc(nc.vector.tensor_reduce(k_max[:, :], k_maxes[:, :, :], AX.X, ALU.max))
                own.wait()
                nc.vector.tensor_scalar(k_max[:, :], k_max[:, :], -1.0, None, ALU.mult).then_inc(s["kmax_done"], 1)
                dve.wait_ge(s["kexp_done"], (b + 1) * KD)
                own.inc(nc.vector.reciprocal(k_rec[:, :], k_sum[:, :]))
                own.wait()
                for mt in range(KD if over_v else 0):
                    nc.vector.tensor_scalar(k_t[:, mt, :], k_t[:, mt, :], k_rec[:, mt:mt + 1], None, ALU.mult).then_inc(s["k_scaled"], 1)
                for tt in range(1, QT, 2):
                    dve.wait_ge(s["k_turned"], b * QT + tt + 1)
                    if tt >= 4:
                        dve.wait_ge(s["kv_mm"], b * QT + tt - 3)
                    nc.vector.tensor_copy(kn[:, tt % 4, :], tb[tt % 4][:, :]).then_inc(s["kn_dve"], 1)
                dve.wait_ge(s["kv_mm"], (b + 1) * QT)
                own.wait()
                for mt in range(KD):
                    nc.vector.scalar_tensor_tensor(out=kv[:, mt, :], in0=mb[0][:, mt * P:(mt + 1) * P],
                                                   scalar=1.0 if over_v else k_rec[:, mt:mt + 1],
                                                   in1=blocks[:, :], op0=ALU.mult, op1=ALU.mult).then_inc(s["kv_done"], 1)

                def norm_y(c):
                    it = b * NC_B + c
                    dve.wait_ge(s["y_mm"], (it + 1) * TT)
                    norm_dve(nc, dve, m2, own, it, lambda t: y_banks(c)[t][:, :])

                norm_y(0)
                for c in range(NC_B):
                    it = b * NC_B + c
                    if c + 1 < NC_B:
                        norm_y(c + 1)
                    for t in range(TT):
                        dve.wait_ge(s["o_mm"], it * TT + t + 1)
                        sums = y_banks(c)[t]
                        nc.vector.tensor_tensor(sums[:, :], sums[:, :], rows[:, 2, :], ALU.add).then_inc(s["biased"], 1)
                        dve.wait_ge(s["biased"], it * TT + t + 1)
                        dve.wait_ge(s["residual_in"], (it + 1) * 16)
                        nc.vector.tensor_tensor(x_res[:, t, :], sums[:, :], x_res[:, t, :], ALU.add).then_inc(s["out_done"], 1)
                own.end()


NAMES2 = {"norm_w": "L2_cond_norm_scale", "norm_b": "L2_cond_norm_bias", "Wq": "L2_cond_Wq", "Wk": "L2_cond_Wk", "Wv": "L2_cond_Wv",
          "Wo": "L2_cond_film_out_W", "bq": "L2_cond_bq", "bk": "L2_cond_bk", "bv": "L2_cond_bv", "bo": "L2_cond_film_out_b"}
NAMES3 = {"norm_w": "L3_cond_ln_w", "norm_b": "L3_cond_ln_b", "Wq": "L3_cond_Wq", "Wk": "L3_cond_Wk", "Wv": "L3_cond_Wv",
          "Wo": "L3_cond_W_out", "bq": "L3_cond_bq", "bk": "L3_cond_bk", "bv": "L3_cond_bv", "bo": "L3_cond_b_out"}


def build(nc, a, out):
    with ExitStack() as ctx:
        def sb(name, shape):
            return ctx.enter_context(nc.sbuf_tensor(name, shape, F32))

        def dram(name, shape):
            return nc.dram_tensor(name, shape, F32, kind="Internal").ap()

        keep = {"cols": sb("cols", [P, NCOLS]),
                "film": sb("film", [P, NB * 2, 2, KD, NB]),
                "silu": sb("silu", [P, KC, NB]),
                "gate": sb("gate", [P, NB, D]),
                "ident": sb("ident", [P, P]),
                "neg_half": sb("neg_half", [P, TT])}
        x1, x2, x3 = (dram(f"x_after_L{i}", [NB * S, D]) for i in range(3))
        qk_parts = dram("qk_parts", [2, 2, D, NB * S])
        mask_parts = dram("mask_parts", [2, NB * S])
        max_rows = dram("max_rows", [2, 2, S])
        stage_condition(nc, a, keep)
        stage_mamba(nc, a, keep, x1)
        with ExitStack() as for_y:
            y = for_y.enter_context(nc.sbuf_tensor("y", [P, QT, NB * D], F32))
            with ExitStack() as for_v:
                v = for_v.enter_context(nc.sbuf_tensor("v", [P, QT, NB * D], F32))
                stage_qkv(nc, a, keep, x1, qk_parts, mask_parts, v, y)
                stage_attention(nc, a, keep, qk_parts, mask_parts, max_rows, v, y)
            stage_out(nc, a, keep, 1, "L1_cond_out_w", "L1_cond_out_b", y, x1, x2)
        stage_linear(nc, a, keep, 2, 16, NAMES2, True, True, x2, x3)
        stage_linear(nc, a, keep, 3, 8, NAMES3, False, False, x3, out.rearrange("b s d -> (b s) d"))


def kernel(**inputs):
    import numpy as np
    import concourse.bacc as bacc
    from concourse.bass_utils import run_bass_kernel_spmd

    def as_columns(v):
        v = np.asarray(v)
        return np.ascontiguousarray(v.reshape(-1, P, *v.shape[1:]).swapaxes(0, 1).reshape(P, -1))

    sent = {name: np.asarray(v) for name, v in inputs.items()}
    sent["cond_T"] = sent.pop("cond_2048").T
    sent["ada_w_T"] = sent.pop("L0_cond_ada_w").T
    for name in ("in_proj_w", "x_proj_w", "dt_proj_w", "out_proj_w"):
        sent[f"{name}_T"] = sent.pop(f"L0_cond_{name}").T
    sent["columns"] = np.concatenate([as_columns(sent[name]) for name, _ in COLUMNS], axis=1)
    for name, _ in COLUMNS:
        if name != "L0_cond_ada_b":
            del sent[name]
    sent["mask_ff1_columns"] = as_columns(sent["mask_BxS_ff1"].reshape(-1))
    sent["mask_ik0_columns"] = as_columns(sent["mask_BxS_ik0"].reshape(-1))
    sent["mask_fk1_columns"] = as_columns(sent["mask_BxSx1_fk1"].reshape(-1))

    nc = bacc.Bacc("TRN2", target_bir_lowering=False, num_devices=1)
    arrays, a = {}, {}
    for name, v in sent.items():
        v = np.ascontiguousarray(v)
        arrays[f"in_{name}"] = v
        a[name] = nc.dram_tensor(f"in_{name}", v.shape, mybir.dt.from_np(v.dtype), kind="ExternalInput").ap()
    out = nc.dram_tensor("out", (NB, S, D), F32, kind="ExternalOutput").ap()
    build(nc, a, out)
    r = run_bass_kernel_spmd(nc, [arrays], core_ids=[0])
    return r.results[0]["out"]
```
